# Optimizing a Trainium2 kernel written in Bass

```python
import numpy as np
import jax
import jax.numpy as jnp

def _softmax(x, axis=-1):
    return jax.nn.softmax(x, axis=axis)

def _gelu(x):
    return jax.nn.gelu(x, approximate=True)

def _silu(x):
    return jax.nn.silu(x)

def _sigmoid(x):
    return jax.nn.sigmoid(x)

def _layernorm(x, axis=-1, eps=1e-05):
    m = jnp.mean(x, axis=axis, keepdims=True)
    v = jnp.var(x, axis=axis, keepdims=True)
    return (x - m) / jnp.sqrt(v + eps)

def _scatter_add(tgt, idx, src, axis=0):
    return tgt.at[idx].add(src)

def _segment_sum(src, seg, n):
    return jax.ops.segment_sum(src, seg, n)
kernel_name = 'mk_hybrid_d1_jaxref_r8_f57250'

def setup_inputs(seed: int=0):
    np.random.seed(seed)
    _w = jnp.asarray

    def _L0_attn_a_setup():
        import jax, jax.numpy as jnp
        import numpy as np
        B, L, D_MODEL, D_STATE, D_MAMBA, DT_RANK = (2, 128, 128, 16, 256, 64)
        K_CONV = 4

        def _silu(v):
            return v * jax.nn.sigmoid(v)
        key = jax.random.key(seed)
        ks = jax.random.split(key, 10)
        x = jax.random.normal(ks[0], (B, L, D_MODEL), dtype=jnp.float32)
        s_in = 1.0 / np.sqrt(D_MODEL)
        s_xm = 1.0 / np.sqrt(D_MAMBA)
        s_dt = 1.0 / np.sqrt(DT_RANK)
        W_in = jax.random.normal(ks[1], (D_MODEL, 2 * D_MAMBA), dtype=jnp.float32) * s_in
        conv_w = jax.random.normal(ks[2], (K_CONV, 1, D_MAMBA), dtype=jnp.float32) * 0.5
        conv_b = jnp.zeros((D_MAMBA,), dtype=jnp.float32)
        A_log = jax.random.uniform(ks[3], (D_MAMBA, D_STATE), dtype=jnp.float32, minval=-3.0, maxval=1.0)
        D = jnp.ones((D_MAMBA,), dtype=jnp.float32)
        W_x = jax.random.normal(ks[4], (D_MAMBA, DT_RANK + 2 * D_STATE), dtype=jnp.float32) * s_xm
        W_dt = jax.random.normal(ks[5], (DT_RANK, D_MAMBA), dtype=jnp.float32) * s_dt
        b_dt = jnp.zeros((D_MAMBA,), dtype=jnp.float32)
        W_out = jax.random.normal(ks[6], (D_MAMBA, D_MODEL), dtype=jnp.float32) * s_xm
        return {'x': x, 'W_in': W_in, 'conv_w': conv_w, 'conv_b': conv_b, 'A_log': A_log, 'D': D, 'W_x': W_x, 'W_dt': W_dt, 'b_dt': b_dt, 'W_out': W_out}
    _L0_attn_a_in = _L0_attn_a_setup()

    def _L0_attn_b_setup():
        import jax, jax.numpy as jnp
        import numpy as np
        import math
        B, N, E, D = (4, 1024, 128, 64)
        key = jax.random.key(seed)
        kx, kq, kk, kv, ko = jax.random.split(key, 5)
        x = jax.random.normal(kx, (B, N, E), dtype=jnp.float32)
        wq = jnp.sign(jax.random.normal(kq, (D, E), dtype=jnp.float32)) / math.sqrt(E)
        wk = jnp.sign(jax.random.normal(kk, (D, E), dtype=jnp.float32)) / math.sqrt(E)
        wv = jnp.sign(jax.random.normal(kv, (D, E), dtype=jnp.float32)) / math.sqrt(E)
        wo = jnp.sign(jax.random.normal(ko, (E, D), dtype=jnp.float32)) / math.sqrt(D)
        return {'x': x, 'wq': wq, 'wk': wk, 'wv': wv, 'wo': wo}
    _L0_attn_b_in = _L0_attn_b_setup()

    def _L0_ffn_setup():
        import jax, jax.numpy as jnp
        import numpy as np
        EMBED_DIM = 128
        MLP_RATIO = 4
        NUM_EXPERTS = 8
        CAPACITY = 1.0
        LN_EPS = 1e-05

        def _layernorm(y, gamma, beta):
            mu = jnp.mean(y, axis=-1, keepdims=True)
            var = jnp.mean(jnp.square(y - mu), axis=-1, keepdims=True)
            return (y - mu) * jax.lax.rsqrt(var + LN_EPS) * gamma + beta
        key = jax.random.key(seed)
        k0, k1, k2, k3, k4, k5 = jax.random.split(key, 6)
        d = EMBED_DIM
        dd = EMBED_DIM * MLP_RATIO
        n = NUM_EXPERTS
        x = jax.random.normal(k0, (4, 256, d), dtype=jnp.float32)
        gate_w = jax.random.normal(k1, (n, d), dtype=jnp.float32) * 0.02
        ln_gamma = jnp.ones((d,), dtype=jnp.float32)
        ln_beta = jnp.zeros((d,), dtype=jnp.float32)
        fc1s = jax.random.normal(k2, (n, dd, d), dtype=jnp.float32) * (1.0 / np.sqrt(d))
        b1s = jax.random.normal(k3, (n, dd), dtype=jnp.float32) * 0.02
        fc2s = jax.random.normal(k4, (n, d, dd), dtype=jnp.float32) * (1.0 / np.sqrt(dd))
        b2s = jax.random.normal(k5, (n, d), dtype=jnp.float32) * 0.02
        return {'x': x, 'gate_w': gate_w, 'ln_gamma': ln_gamma, 'ln_beta': ln_beta, 'fc1s': fc1s, 'b1s': b1s, 'fc2s': fc2s, 'b2s': b2s}
    _L0_ffn_in = _L0_ffn_setup()
    _d = {'L0_attn_a_x': _L0_attn_a_in['x'], 'L0_attn_a_W_in': _L0_attn_a_in['W_in'], 'L0_attn_a_conv_w': _L0_attn_a_in['conv_w'], 'L0_attn_a_conv_b': _L0_attn_a_in['conv_b'], 'L0_attn_a_A_log': _L0_attn_a_in['A_log'], 'L0_attn_a_D': _L0_attn_a_in['D'], 'L0_attn_a_W_x': _L0_attn_a_in['W_x'], 'L0_attn_a_W_dt': _L0_attn_a_in['W_dt'], 'L0_attn_a_b_dt': _L0_attn_a_in['b_dt'], 'L0_attn_a_W_out': _L0_attn_a_in['W_out'], 'L0_attn_b_wq': _L0_attn_b_in['wq'], 'L0_attn_b_wk': _L0_attn_b_in['wk'], 'L0_attn_b_wv': _L0_attn_b_in['wv'], 'L0_attn_b_wo': _L0_attn_b_in['wo'], 'L0_ffn_gate_w': _L0_ffn_in['gate_w'], 'L0_ffn_ln_gamma': _L0_ffn_in['ln_gamma'], 'L0_ffn_ln_beta': _L0_ffn_in['ln_beta'], 'L0_ffn_fc1s': _L0_ffn_in['fc1s'], 'L0_ffn_b1s': _L0_ffn_in['b1s'], 'L0_ffn_fc2s': _L0_ffn_in['fc2s'], 'L0_ffn_b2s': _L0_ffn_in['b2s']}
    _x0 = _d['L0_attn_a_x']
    _d['L0_attn_a_x'] = jax.random.normal(jax.random.fold_in(jax.random.key(seed), 1), (2, 2048, 128), dtype=_x0.dtype)
    del _x0
    return _d

def reference(L0_attn_a_x, L0_attn_a_W_in, L0_attn_a_conv_w, L0_attn_a_conv_b, L0_attn_a_A_log, L0_attn_a_D, L0_attn_a_W_x, L0_attn_a_W_dt, L0_attn_a_b_dt, L0_attn_a_W_out, L0_attn_b_wq, L0_attn_b_wk, L0_attn_b_wv, L0_attn_b_wo, L0_ffn_gate_w, L0_ffn_ln_gamma, L0_ffn_ln_beta, L0_ffn_fc1s, L0_ffn_b1s, L0_ffn_fc2s, L0_ffn_b2s):

    def _L0_attn_a_ref(x, W_in, conv_w, conv_b, A_log, D, W_x, W_dt, b_dt, W_out):
        import jax, jax.numpy as jnp
        import numpy as np
        B, L, D_MODEL, D_STATE, D_MAMBA, DT_RANK = (2, 128, 128, 16, 256, 64)
        K_CONV = 4

        def _silu(v):
            return v * jax.nn.sigmoid(v)
        xz = x @ W_in
        x_m, z = jnp.split(xz, 2, axis=-1)
        x_m = jax.lax.conv_general_dilated(x_m, conv_w, window_strides=(1,), padding=[(1, 2)], dimension_numbers=('NWC', 'WIO', 'NWC'), feature_group_count=D_MAMBA) + conv_b
        x_m = _silu(x_m)
        x_dbl = x_m @ W_x
        dt_low, Bc, Cc = jnp.split(x_dbl, [DT_RANK, DT_RANK + D_STATE], axis=-1)
        dt = jax.nn.softplus(dt_low @ W_dt + b_dt)
        A = -jnp.exp(A_log)
        dA = jnp.exp(dt[..., None] * A[None, None])
        dB = dt[..., None] * Bc[:, :, None, :]
        u = x_m[..., None]
        dA_T = jnp.transpose(dA, (1, 0, 2, 3))
        dB_T = jnp.transpose(dB, (1, 0, 2, 3))
        u_T = jnp.transpose(u, (1, 0, 2, 3))

        def step(state, inp):
            da_t, db_t, u_t = inp
            s = da_t * state + db_t * u_t
            return (s, s)
        init = jnp.zeros((x.shape[0], D_MAMBA, D_STATE), dtype=x.dtype)
        _, states = jax.lax.scan(step, init, (dA_T, dB_T, u_T))
        states = jnp.transpose(states, (1, 0, 2, 3))
        y = jnp.einsum('blms,bls->blm', states, Cc)
        y = y + x_m * D
        y = y * _silu(z)
        return y @ W_out

    def _L0_attn_b_ref(x, wq, wk, wv, wo):
        import jax, jax.numpy as jnp
        import numpy as np
        import math
        B, N, E, D = (4, 1024, 128, 64)
        Q = jnp.einsum('bne,de->bnd', x, wq)
        K = jnp.einsum('bne,de->bnd', x, wk)
        V = jnp.einsum('bne,de->bnd', x, wv)
        energy = jnp.einsum('bnd,bne->bde', K, V)
        context = jnp.einsum('bnd,bde->bne', Q, energy)
        context = context * jnp.asarray(math.sqrt(3.0 / D), dtype=context.dtype)
        out = jnp.einsum('bnd,ed->bne', context, wo)
        return out

    def _L0_ffn_ref(x, gate_w, ln_gamma, ln_beta, fc1s, b1s, fc2s, b2s):
        import jax, jax.numpy as jnp
        import numpy as np
        EMBED_DIM = 128
        MLP_RATIO = 4
        NUM_EXPERTS = 8
        CAPACITY = 1.0
        LN_EPS = 1e-05

        def _layernorm(y, gamma, beta):
            mu = jnp.mean(y, axis=-1, keepdims=True)
            var = jnp.mean(jnp.square(y - mu), axis=-1, keepdims=True)
            return (y - mu) * jax.lax.rsqrt(var + LN_EPS) * gamma + beta
        og_shape = x.shape
        d = og_shape[-1]
        xf = x.reshape(-1, d)
        bs = xf.shape[0]
        n = gate_w.shape[0]
        k = int(bs * CAPACITY) // n
        scores = xf @ gate_w.T
        scores = (jnp.tanh(scores) + 1.0) * 0.5
        vals, idx = jax.lax.top_k(scores.T, k)
        kept_w = vals.T
        flat_idx = idx.T.reshape(-1)
        y = xf[flat_idx].reshape(k, n, d)
        y = _layernorm(y, ln_gamma, ln_beta)
        h = jnp.einsum('knd,nfd->knf', y, fc1s) + b1s
        h = jax.nn.gelu(h, approximate=True)
        o = jnp.einsum('knf,ndf->knd', h, fc2s) + b2s
        o = o * kept_w[:, :, None]
        out = xf.at[flat_idx].add(o.reshape(k * n, d))
        return out.reshape(og_shape)
    x = L0_attn_a_x
    x = x + _L0_attn_a_ref(_layernorm(x, axis=-1), L0_attn_a_W_in, L0_attn_a_conv_w, L0_attn_a_conv_b, L0_attn_a_A_log, L0_attn_a_D, L0_attn_a_W_x, L0_attn_a_W_dt, L0_attn_a_b_dt, L0_attn_a_W_out)
    x = x + _L0_ffn_ref(_layernorm(x, axis=-1), L0_ffn_gate_w, L0_ffn_ln_gamma, L0_ffn_ln_beta, L0_ffn_fc1s, L0_ffn_b1s, L0_ffn_fc2s, L0_ffn_b2s)
    x = x + _L0_attn_b_ref(_layernorm(x, axis=-1), L0_attn_b_wq, L0_attn_b_wk, L0_attn_b_wv, L0_attn_b_wo)
    x = x + _L0_ffn_ref(_layernorm(x, axis=-1), L0_ffn_gate_w, L0_ffn_ln_gamma, L0_ffn_ln_beta, L0_ffn_fc1s, L0_ffn_b1s, L0_ffn_fc2s, L0_ffn_b2s)
    return x

_drawn_inputs = setup_inputs


def setup_inputs(seed=0):
    import zlib

    import numpy as np

    out = dict(_drawn_inputs(seed))
    spreads = {'L0_attn_a_conv_b': (0.0, 0.1),
     'L0_attn_a_D': (1.0, 0.2),
     'L0_attn_a_b_dt': (0.0, 0.1),
     'L0_ffn_ln_gamma': (1.0, 0.2),
     'L0_ffn_ln_beta': (0.0, 0.346)}
    factors = {'L0_ffn_b1s': 8.0, 'L0_ffn_b2s': 7.73}
    for name, (base, spread) in spreads.items():
        noise = np.random.default_rng([zlib.crc32(name.encode()), seed]).standard_normal(out[name].shape)
        drawn = base * np.exp(spread * noise) if base else spread * noise
        out[name] = jnp.asarray(drawn.astype(out[name].dtype))
    for name, factor in factors.items():
        out[name] = (out[name] * factor).astype(out[name].dtype)
    return out
```

```python
from contextlib import ExitStack

import concourse.bass as bass
from concourse import mybir

F32 = mybir.dt.float32
F32R = mybir.dt.float32r
BF16 = mybir.dt.bfloat16
I32 = mybir.dt.int32
ACT = mybir.ActivationFunctionType
ALU = mybir.AluOpType

P = 128
BANK = 512
LN_EPS = 1e-5


def layer_norm_constants(dve, chain, at, stats, moments, source, tiles):
    for i in range(tiles):
        dve.bn_stats(stats[:, i, :], source(i)).then_inc(chain, 1)
    dve.wait_ge(chain, at + tiles)
    for i in range(tiles):
        dve.bn_aggr(moments[:, i, :], stats[:, i, :]).then_inc(chain, 1)
    dve.wait_ge(chain, at + 2 * tiles)
    return at + 2 * tiles


def mamba(nc, X, ident, x, W_in, conv_w, conv_b, A_log, D, W_x, W_dt, b_dt, W_out):
    BATCH, L, DM = x.shape
    KC, _, CH = conv_w.shape
    NS = A_log.shape[1]
    R = W_dt.shape[0]
    KB = CH // P
    TILES = L // P
    TB = L // BANK
    CHUNK = 1024
    NCHUNK = L // CHUNK
    CT = CHUNK // P
    CBANKS = CHUNK // BANK
    RING = 4
    STEPS = NCHUNK * NS * KB
    LPAD = L + KC - 1

    with nc.cleanup_on_exit(), ExitStack() as ctx:
        def sb(name, shape, dt=F32):
            return ctx.enter_context(nc.sbuf_tensor(name, shape, dt))

        def sem(name):
            return nc.alloc_semaphore(name)

        psum = ctx.enter_context(nc.psum_tensor("m_psum", [P, 8, BANK], F32))

        w_in = sb("w_in", [P, 2 * CH])
        w_x = sb("w_x", [P, KB, R + 2 * NS])
        w_bc = sb("w_bc", [P, KB, P])
        w_dt = sb("w_dt", [R, CH])
        w_out = sb("w_out", [P, KB, DM])
        taps = sb("taps", [P, KB, KC])
        chan = sb("chan", [P, 3, KB])
        decay_rate = sb("decay_rate", [P, KB, NS])
        pick = sb("pick", [64, NS, P])
        pick_r = sb("pick_r", [64, NS, P], F32R)
        stats = sb("m_stats", [P, BATCH * TILES, 6])
        moments = sb("m_moments", [P, BATCH * TILES, 2])
        rstd = sb("m_rstd", [P, BATCH * TILES])
        shift = sb("m_shift", [P, BATCH * TILES])
        u = sb("u", [P, KB, L])
        z = sb("z", [P, KB, L])
        dt = sb("dt", [P, KB, L])
        dtu = sb("dtu", [P, KB, L])
        b_split = sb("b_split", [64, L], F32R)
        c_rows = sb("c_rows", [P, L])
        low = sb("low", [R, L])
        yz = sb("yz", [P, KB, CHUNK])
        carry = sb("carry", [P, NS, KB])
        decay = sb("decay", [P, RING, CHUNK])
        xn = decay[:, 0:RING // 2, :].rearrange("p a (t d) -> p (a t) d", d=DM)
        xn_T = decay[:, RING // 2:RING, :].rearrange("p a t -> p (a t)")
        state_raw = sb("state_raw", [P, max(RING * CHUNK, KB * LPAD)])
        state = state_raw[:, 0:RING * CHUNK].rearrange("p (r t) -> p r t", r=RING)
        conv_in = state_raw[:, 0:KB * LPAD].rearrange("p (k t) -> p k t", k=KB)
        drive = sb("drive", [P, 2, CHUNK])
        product = sb("product", [P, 2, CHUNK])
        c_all = sb("c_all", [P, RING, CHUNK])
        c_dram = nc.dram_tensor("c_dram", [NS, L], F32, kind="Internal").ap()

        x_loaded = sem("x_loaded")
        w_loaded = sem("w_loaded")
        bc_loaded = sem("bc_loaded")
        constants = sem("m_constants")
        dve_chain = sem("m_dve_chain")
        rate_exp = sem("rate_exp")
        variance = sem("variance")
        std_done = sem("std_done")
        ln_ready = sem("ln_ready")
        normed = sem("normed")
        turned = sem("turned")
        xnT_ready = sem("xnT_ready")
        xz_ready = sem("xz_ready")
        xz_taken = sem("xz_taken")
        pads = sem("pads")
        conv_done = sem("conv_done")
        u_ready = sem("u_ready")
        bc_ready = sem("bc_ready")
        b_high = sem("b_high")
        b_ready = sem("b_ready")
        c_taken = sem("c_taken")
        c_stored = sem("c_stored")
        low_ready = sem("low_ready")
        low_taken = sem("low_taken")
        dtp_ready = sem("dtp_ready")
        dt_clamped = sem("dt_clamped")
        dt_exp = sem("dt_exp")
        dt_log = sem("dt_log")
        dt_ready = sem("dt_ready")
        dtu_ready = sem("dtu_ready")
        b_bcast = sem("b_bcast")
        c_loaded = [sem(f"c_loaded{r}") for r in range(RING)]
        decay_ready = sem("decay_ready")
        drive_ready = sem("drive_ready")
        scanned = sem("scanned")
        carried = sem("carried")
        product_ready = sem("product_ready")
        summed = sem("summed")
        y_gated = sem("y_gated")
        projected = sem("projected")
        added = sem("added")

        block = ctx.enter_context(nc.Block())

        LATE = 4
        turns = []
        for c in range(NCHUNK):
            for s in range(NS):
                if c and s == LATE:
                    turns.append(("out", c - 1))
                turns.append(("b", c * NS + s))
        turns.append(("out", NCHUNK - 1))
        assert len(turns) % 2 == 0
        slot_of = {t: n % 2 for n, t in enumerate(turns)}

        def slot(turn):
            first = 4 + 2 * slot_of[turn]
            return psum[:, first:first + CBANKS, :]

        def step(c, s, k):
            return (c * NS + s) * KB + k

        steps = [(c, s, k) for c in range(NCHUNK) for s in range(NS) for k in range(KB)]

        @block.sync
        def _(sp):
            for b in range(BATCH):
                sp.dma_start(X[:, b * TILES:(b + 1) * TILES, :],
                             x[b].rearrange("(i p) d -> p i d", p=P)).then_inc(x_loaded, 16)
            for out, source in ((w_in[:], W_in),
                                (w_x[:], W_x.rearrange("(k p) n -> p k n", p=P)),
                                (w_dt[:], W_dt),
                                (w_out[:], W_out.rearrange("(k p) n -> p k n", p=P)),
                                (decay_rate[:], A_log.rearrange("(k p) s -> p k s", p=P))):
                sp.dma_start(out, source).then_inc(w_loaded, 16)
            with nc.allow_non_contiguous_dma(reason="a few scalars of each channel"):
                for out, source in ((taps[:, 0, :], conv_w[:, 0, 0:P].rearrange("t p -> p t")),
                                    (taps[:, 1, :], conv_w[:, 0, P:2 * P].rearrange("t p -> p t")),
                                    (chan[:, 0, :], conv_b.rearrange("(k p) -> p k", p=P)),
                                    (chan[:, 1, :], D.rearrange("(k p) -> p k", p=P)),
                                    (chan[:, 2, :], b_dt.rearrange("(k p) -> p k", p=P))):
                    sp.dma_start(out, source).then_inc(w_loaded, 16)
            with sp.Fori(0, BATCH) as b:
                sp.wait_ge(c_taken, TB * (b + 1))
                sp.dma_start(c_dram, c_rows[64:64 + NS, :]).then_inc(c_stored, 16)
                sp.wait_ge(c_stored, 16 * (b + 1))
                for q in range(NCHUNK * NS):
                    c, s = divmod(q, NS)
                    if q >= RING:
                        sp.wait_ge(product_ready, STEPS * b + KB * (q - RING + 1))
                    sp.dma_start(c_all[:, q % RING, :],
                                 c_dram[s:s + 1, c * CHUNK:(c + 1) * CHUNK].broadcast_to([P, CHUNK])
                                 ).then_inc(c_loaded[q % RING], 16)

        @block.gpsimd
        def _(pool):
            pool.memset(pick[:], 0.0).then_inc(constants, 1)
            pool.memset(w_bc[:], 0.0).then_inc(constants, 1)
            for n, base in enumerate((0, -32)):
                pool.wait_ge(constants, 2 + n)
                pool.affine_select(out=pick[:], in_=pick[:], compare_op=ALU.not_equal, fill=1.0,
                                   base=base, pattern=[[-1, NS], [0, P]],
                                   channel_multiplier=1).then_inc(constants, 1)
            pool.wait_ge(constants, 4)
            pool.tensor_copy(pick_r[:], pick[:]).then_inc(constants, 1)
            with pool.Fori(0, BATCH) as b:
                for k in range(KB):
                    pool.wait_ge(dt_ready, KB * TB * b + TB * (k + 1))
                    pool.wait_ge(u_ready, KB * b + k + 1)
                    pool.tensor_tensor(dtu[:, k, :], dt[:, k, :], u[:, k, :],
                                       ALU.mult).then_inc(dtu_ready, 1)
                for n, (c, s, k) in enumerate(steps):
                    q = c * NS + s
                    if k == 0:
                        pool.wait_ge(c_loaded[q % RING],
                                     16 * (NCHUNK * NS // RING * b + q // RING + 1))
                    pool.wait_ge(scanned, STEPS * b + n + 1)
                    if n >= 2:
                        pool.wait_ge(summed, STEPS * b + n - 1)
                    pool.tensor_tensor(product[:, n % 2, :], state[:, n % RING, :],
                                       c_all[:, q % RING, :], ALU.mult).then_inc(product_ready, 1)

        @block.scalar
        def _(act):
            act.wait_ge(w_loaded, 16 * 10)
            act.activation(decay_rate[:], decay_rate[:], ACT.Exp).then_inc(rate_exp, 1)
            act.wait_ge(variance, 1)
            act.activation(rstd[:], rstd[:], ACT.Sqrt).then_inc(std_done, 1)
            act.wait_ge(ln_ready, 1)
            with act.Fori(0, BATCH) as b:
                act.wait_ge(added, NCHUNK * b + 1)
                for i in range(TILES):
                    tile = bass.ds(TILES * b + i, 1)
                    act.activation(xn[:, i, :], X[:, TILES * b + i, :], ACT.Identity,
                                   bias=shift[:, tile], scale=rstd[:, tile]).then_inc(normed, 1)
                act.wait_ge(pads, b + 1)
                for n in range(2 * KB * TB):
                    j, t = divmod(n, TB)
                    act.wait_ge(xz_ready, 2 * KB * TB * b + n + 1)
                    span = slice(t * BANK, (t + 1) * BANK)
                    if j < KB:
                        act.copy(conv_in[:, j, 1 + t * BANK:1 + (t + 1) * BANK],
                                 psum[:, 4 + n % 4, :]).then_inc(xz_taken, 1)
                    else:
                        act.activation(z[:, j - KB, span], psum[:, 4 + n % 4, :],
                                       ACT.Silu).then_inc(xz_taken, 1)
                for k in range(KB):
                    act.wait_ge(conv_done, KB * b + k + 1)
                    act.activation(u[:, k, :], u[:, k, :], ACT.Silu,
                                   bias=chan[:, 0, k:k + 1]).then_inc(u_ready, 1)
                for t in range(TB):
                    act.wait_ge(bc_ready, TB * b + t + 1)
                    act.copy(c_rows[64:64 + NS, t * BANK:(t + 1) * BANK],
                             psum[64:64 + NS, t, :]).then_inc(c_taken, 1)
                    act.wait_ge(low_ready, TB * b + t + 1)
                    act.copy(low[:, t * BANK:(t + 1) * BANK], psum[0:R, 4 + t, :]).then_inc(low_taken, 1)
                for n in range(KB * TB):
                    k, t = divmod(n, TB)
                    part = dt[:, k, t * BANK:(t + 1) * BANK]
                    act.wait_ge(dt_clamped, KB * TB * b + n + 1)
                    act.activation(part, part, ACT.Exp).then_inc(dt_exp, 1)
                    act.wait_ge(dt_exp, KB * TB * b + n + 1)
                    act.activation(part, part, ACT.Ln, bias=1.0).then_inc(dt_log, 1)

                def carry_over(n):
                    c, s, k = steps[n]
                    act.wait_ge(scanned, STEPS * b + n + 1)
                    act.copy(carry[:, s, k:k + 1],
                             state[:, n % RING, CHUNK - 1:CHUNK]).then_inc(carried, 1)

                act.wait_ge(dt_ready, KB * TB * (b + 1))
                for n, (c, s, k) in enumerate(steps):
                    if n >= RING:
                        act.wait_ge(scanned, STEPS * b + n - RING + 1)
                    act.activation(decay[:, n % RING, :], dt[:, k, c * CHUNK:(c + 1) * CHUNK], ACT.Exp,
                                   scale=decay_rate[:, k, s:s + 1]).then_inc(decay_ready, 1)
                    if 2 <= n < NS * KB + 2:
                        carry_over(n - 2)

        @block.vector
        def _(dve):
            dve.wait_ge(w_loaded, 16 * 10)
            dve.wait_ge(constants, 2)
            for k in range(KB):
                for first, of in ((0, R), (32, R), (64, R + NS)):
                    dve.tensor_copy(w_bc[:, k, first:first + NS],
                                    w_x[:, k, of:of + NS]).then_inc(bc_loaded, 1)
            dve.wait_ge(rate_exp, 1)
            dve.tensor_scalar(decay_rate[:], decay_rate[:], -1.0, None, ALU.mult).then_inc(bc_loaded, 1)
            dve.wait_ge(x_loaded, 16 * BATCH)
            dve.sem_inc(added, 1)
            begin = layer_norm_constants(dve, dve_chain, 0, stats, moments, lambda i: X[:, i, :],
                                         BATCH * TILES)
            dve.tensor_scalar(rstd[:], moments[:, :, 1], LN_EPS, None, ALU.add).then_inc(variance, 1)
            dve.wait_ge(std_done, 1)
            dve.reciprocal(rstd[:], rstd[:]).then_inc(dve_chain, 1)
            begin = begin + 1
            dve.wait_ge(dve_chain, begin)
            dve.scalar_tensor_tensor(out=shift[:], in0=moments[:, :, 0], scalar=-1.0, in1=rstd[:],
                                     op0=ALU.mult, op1=ALU.mult).then_inc(ln_ready, 1)
            LINKS = 1 + (KC - 1) * KB
            with dve.Fori(0, BATCH) as b:
                at = begin + LINKS * b
                dve.memset(conv_in[:, :, 0:1], 0.0).then_inc(dve_chain, 1)
                dve.memset(conv_in[:, :, 1 + L:LPAD], 0.0).then_inc(pads, 1)
                at = at + 1
                for g in range(TB):
                    dve.wait_ge(turned, TB * b + g + 1)
                    dve.tensor_copy(xn_T[:, g * BANK:(g + 1) * BANK], psum[:, g, :]).then_inc(xnT_ready, 1)
                for k in range(KB):
                    dve.wait_ge(xz_taken, 2 * KB * TB * b + TB * (k + 1))
                    if k == 0:
                        dve.wait_ge(dve_chain, at)
                        dve.wait_ge(pads, b + 1)
                    dve.tensor_scalar(u[:, k, :], conv_in[:, k, 0:L], taps[:, k, 0:1], None,
                                      ALU.mult).then_inc(dve_chain, 1)
                    at = at + 1
                    for j in range(1, KC):
                        dve.wait_ge(dve_chain, at)
                        ins = dve.scalar_tensor_tensor(out=u[:, k, :], in0=conv_in[:, k, j:j + L],
                                                       scalar=taps[:, k, j:j + 1], in1=u[:, k, :],
                                                       op0=ALU.mult, op1=ALU.add)
                        if j < KC - 1:
                            ins.then_inc(dve_chain, 1)
                            at = at + 1
                        else:
                            ins.then_inc(conv_done, 1)
                for t in range(TB):
                    dve.wait_ge(bc_ready, TB * b + t + 1)
                    part = slice(t * BANK, (t + 1) * BANK)
                    dve.tensor_copy(b_split[:, part], psum[0:64, t, :]).then_inc(b_high, 1)
                    dve.wait_ge(b_high, TB * b + t + 1)
                    dve.tensor_tensor(b_split[32:64, part], psum[32:64, t, :],
                                      b_split[32:64, part].bitcast(F32), ALU.subtract).then_inc(b_ready, 1)
                for n in range(KB * TB + 2):
                    if n < KB * TB:
                        k, t = divmod(n, TB)
                        dve.wait_ge(dtp_ready, KB * TB * b + n + 1)
                        dve.tensor_scalar(dt[:, k, t * BANK:(t + 1) * BANK], psum[:, n % 4, :],
                                          chan[:, 2, k:k + 1], 40.0, ALU.add,
                                          ALU.min).then_inc(dt_clamped, 1)
                    if n >= 2:
                        k, t = divmod(n - 2, TB)
                        part = dt[:, k, t * BANK:(t + 1) * BANK]
                        dve.wait_ge(dt_log, KB * TB * b + n - 1)
                        dve.scalar_tensor_tensor(out=part, in0=psum[:, (n - 2) % 4, :],
                                                 scalar=chan[:, 2, k:k + 1], in1=part, op0=ALU.add,
                                                 op1=ALU.max).then_inc(dt_ready, 1)

                def force(n):
                    c, s, k = steps[n]
                    dve.wait_ge(b_bcast, NCHUNK * NS * b + c * NS + s + 1)
                    if n < KB:
                        dve.wait_ge(dtu_ready, KB * b + k + 1)
                    if n >= 2:
                        dve.wait_ge(scanned, STEPS * b + n - 1)
                    dve.tensor_tensor(
                        drive[:, n % 2, :].rearrange("p (a t) -> p a t", t=BANK),
                        slot(("b", c * NS + s)),
                        dtu[:, k, c * CHUNK:(c + 1) * CHUNK].rearrange("p (a t) -> p a t", t=BANK),
                        ALU.mult).then_inc(drive_ready, 1)

                def gate(c):
                    dve.wait_ge(summed, STEPS * b + KB * NS * (c + 1))
                    if c:
                        dve.wait_ge(projected, NCHUNK * b + c)
                    for k in range(KB):
                        dve.scalar_tensor_tensor(
                            out=yz[:, k, :].rearrange("p (a t) -> p a t", t=BANK),
                            in0=u[:, k, c * CHUNK:(c + 1) * CHUNK].rearrange("p (a t) -> p a t", t=BANK),
                            scalar=chan[:, 1, k:k + 1], in1=psum[:, 2 * k:2 * k + CBANKS, :],
                            op0=ALU.mult, op1=ALU.add).then_inc(y_gated, 1)
                    for k in range(KB):
                        dve.wait_ge(y_gated, 2 * KB * (NCHUNK * b + c) + KB + k)
                        dve.tensor_tensor(yz[:, k, :], yz[:, k, :], z[:, k, c * CHUNK:(c + 1) * CHUNK],
                                          ALU.mult).then_inc(y_gated, 1)

                def add(c):
                    dve.wait_ge(projected, NCHUNK * b + c + 1)
                    rows = X[:, bass.ds(TILES * b + CT * c, CT), :]
                    dve.tensor_tensor(rows, rows,
                                      slot(("out", c)).rearrange("p a (t d) -> p (a t) d", d=DM),
                                      ALU.add).then_inc(added, 1)

                force(0)
                for n, (c, s, k) in enumerate(steps):
                    if n + 1 < STEPS:
                        force(n + 1)
                    dve.wait_ge(decay_ready, STEPS * b + n + 1)
                    dve.wait_ge(drive_ready, STEPS * b + n + 1)
                    if n >= RING:
                        dve.wait_ge(product_ready, STEPS * b + n - RING + 1)
                    if c == 0 and n >= RING:
                        dve.wait_ge(carried, NS * KB * b + n - RING + 1)
                    if c:
                        dve.wait_ge(carried, NS * KB * b + (n - NS * KB) + 1)
                        if n - RING < NS * KB:
                            dve.wait_ge(carried, NS * KB * b + n - RING + 1)
                    dve.tensor_tensor_scan(state[:, n % RING, :], decay[:, n % RING, :],
                                           drive[:, n % 2, :], carry[:, s, k:k + 1] if c else 0.0,
                                           ALU.mult, ALU.add).then_inc(scanned, 1)
                    if c and s == 1 and k == 1:
                        gate(c - 1)
                    if c and s == LATE and k == 0:
                        add(c - 1)
                gate(NCHUNK - 1)
                add(NCHUNK - 1)

        @block.tensor
        def _(pe):
            pe.wait_ge(w_loaded, 16 * 10)
            pe.wait_ge(constants, 5)
            pe.wait_ge(bc_loaded, 3 * KB)
            with pe.Fori(0, BATCH) as b:
                for g in range(TB):
                    for i in range(4):
                        tile = 4 * g + i
                        pe.wait_ge(normed, TILES * b + tile + 1)
                        last = pe.transpose(psum[:, g, i * P:(i + 1) * P], xn[:, tile, :], ident[:])
                    last.then_inc(turned, 1)
                for n in range(2 * KB * TB):
                    j, t = divmod(n, TB)
                    if j == 0:
                        pe.wait_ge(xnT_ready, TB * b + t + 1)
                    if n >= 4:
                        pe.wait_ge(xz_taken, 2 * KB * TB * b + n - 3)
                    pe.matmul(psum[:, 4 + n % 4, :], w_in[:, j * P:(j + 1) * P],
                              xn_T[:, t * BANK:(t + 1) * BANK], start=True, stop=True).then_inc(xz_ready, 1)
                pe.wait_ge(xz_taken, 2 * KB * TB * (b + 1))
                pe.wait_ge(u_ready, KB * (b + 1))
                for t in range(TB):
                    for k in range(KB):
                        last = pe.matmul(psum[:, t, :], w_bc[:, k, :], u[:, k, t * BANK:(t + 1) * BANK],
                                         start=(k == 0), stop=(k == KB - 1))
                    last.then_inc(bc_ready, 1)
                    for k in range(KB):
                        last = pe.matmul(psum[0:R, 4 + t, :], w_x[:, k, 0:R],
                                         u[:, k, t * BANK:(t + 1) * BANK],
                                         start=(k == 0), stop=(k == KB - 1))
                    last.then_inc(low_ready, 1)
                for n in range(KB * TB):
                    k, t = divmod(n, TB)
                    if k == 0:
                        pe.wait_ge(low_taken, TB * b + t + 1)
                        pe.wait_ge(b_ready, TB * b + t + 1)
                        pe.wait_ge(c_taken, TB * b + t + 1)
                    else:
                        pe.wait_ge(dt_ready, KB * TB * b + n - 3)
                    pe.matmul(psum[:, n % 4, :], w_dt[:, k * P:(k + 1) * P],
                              low[:, t * BANK:(t + 1) * BANK], start=True, stop=True).then_inc(dtp_ready, 1)
                pe.wait_ge(dt_ready, KB * TB * (b + 1))

                def free(position):
                    if position < 2:
                        return
                    kind, which = turns[position - 2]
                    if kind == "b":
                        pe.wait_ge(drive_ready, STEPS * b + KB * (which + 1))
                    else:
                        pe.wait_ge(added, NCHUNK * b + which + 2)

                def sum_state(q):
                    c, s = divmod(q, NS)
                    for k in range(KB):
                        n = step(c, s, k)
                        if s == 0 and c:
                            pe.wait_ge(y_gated, 2 * KB * (NCHUNK * b + c - 1) + k + 1)
                        pe.wait_ge(product_ready, STEPS * b + n + 1)
                        for h in range(CBANKS):
                            last = pe.matmul(psum[:, 2 * k + h, :], ident[:],
                                             product[:, n % 2, h * BANK:(h + 1) * BANK],
                                             start=(s == 0), stop=(s == NS - 1))
                        last.then_inc(summed, 1)

                LAG = 2
                waiting = []
                for position, (kind, which) in enumerate(turns):
                    out = slot((kind, which))
                    if kind == "b":
                        free(position)
                        c, s = divmod(which, NS)
                        for h in range(CBANKS):
                            first = c * CHUNK + h * BANK
                            last = pe.matmul(out[:, h, :], pick_r[:, s, :],
                                             b_split[:, first:first + BANK], start=True, stop=True)
                        last.then_inc(b_bcast, 1)
                        waiting.append(which)
                        if len(waiting) > LAG:
                            sum_state(waiting.pop(0))
                    else:
                        if which == NCHUNK - 1:
                            for q in waiting:
                                sum_state(q)
                        free(position)
                        pe.wait_ge(y_gated, 2 * KB * (NCHUNK * b + which + 1))
                        for i in range(CT):
                            h, at = divmod(i * DM, BANK)
                            for k in range(KB):
                                last = pe.matmul(out[:, h, at:at + DM], yz[:, k, i * P:(i + 1) * P],
                                                 w_out[:, k, :], start=(k == 0), stop=(k == KB - 1))
                        last.then_inc(projected, 1)


def identity(nc, ident):
    with nc.semaphore("ident_zero") as zeroed, nc.Block() as block:
        @block.gpsimd
        def _(pool):
            pool.memset(ident[:], 0.0).then_inc(zeroed, 1)
            pool.wait_ge(zeroed, 1)
            pool.affine_select(out=ident[:], in_=ident[:], compare_op=ALU.not_equal, fill=1.0, base=0,
                               pattern=[[-1, P]], channel_multiplier=1).then_inc(zeroed, 1)
            pool.wait_ge(zeroed, 2)


def moe(nc, X, ident, name, dst, gate_w, ln_gamma, ln_beta, fc1s, b1s, fc2s, b2s):
    E, FF, DM = fc1s.shape
    TILES = X.shape[1]
    T = TILES * P
    K = T // E
    KT = K // P
    FB = FF // P
    J = P // E
    SPAN = T // J
    HALVES = SPAN // P
    PAIRS = HALVES * P
    ROW = DM + E
    STEPS = 25
    LO = 32
    HI = K // LO
    FAR = float(4 * K)

    dram = lambda what, shape: nc.dram_tensor(f"{name}_{what}", shape, F32, kind="Internal").ap()
    table = dram("table", [T, ROW])
    score_dram = dram("score_dram", [E, T])

    with ExitStack() as keep:
        def kept(what, shape, dt=F32):
            return keep.enter_context(nc.sbuf_tensor(f"{name}_{what}", shape, dt))

        tokens = kept("tokens", [P, E, KT], I32)
        gamma = kept("gamma", [P, 2])
        b1_T = kept("b1_T", [P, E * FB])
        b2_all = kept("b2_all", [P, E, DM])
        search = kept("search", [P, SPAN])

        with nc.cleanup_on_exit(), ExitStack() as ctx:
            def sb(what, shape, dt=F32):
                return ctx.enter_context(nc.sbuf_tensor(f"{name}_{what}", shape, dt))

            def sem(what):
                return nc.alloc_semaphore(f"{name}_{what}")

            psum = ctx.enter_context(nc.psum_tensor(f"{name}_psum1", [P, 8, BANK], F32))
            stats = sb("stats", [P, TILES, 6])
            moments = sb("moments", [P, TILES, 2])
            rstd = sb("rstd", [P, TILES])
            shift = sb("shift", [P, TILES])
            again = sb("again", [P, TILES])
            rstd2 = sb("rstd2", [P, TILES])
            shift2 = sb("shift2", [P, TILES])
            f = sb("f", [P, TILES, DM])
            base = sb("base", [P, TILES, DM])
            f_T = sb("f_T", [P, T])
            rows = sb("rows", [P, TILES, ROW])
            gate_raw = sb("gate_raw", [E, DM])
            gate_T = sb("gate_T", [P, E])
            b1_raw = sb("b1_raw", [E * FB, P])
            score = sb("score", [E, T])

            loaded = sem("loaded")
            chain = sem("chain")
            variance = sem("variance")
            std_done = sem("std_done")
            ln_ready = sem("ln_ready")
            variance2 = sem("variance2")
            std2_done = sem("std2_done")
            ln2_ready = sem("ln2_ready")
            f_ready = sem("f_ready")
            base_ready = sem("base_ready")
            rows_ready = sem("rows_ready")
            f_turned = sem("f_turned")
            fT_even = sem("fT_even")
            fT_odd = sem("fT_odd")
            small_turned = sem("small_turned")
            small_ready = sem("small_ready")
            gated = sem("gated")
            tanh_done = sem("tanh_done")
            score_ready = sem("score_ready")
            score_turned = sem("score_turned")
            weights_ready = sem("weights_ready")
            score_stored = sem("score_stored")
            search_loaded = sem("search_loaded")
            stored = sem("stored")
            NB = T // BANK
            block = ctx.enter_context(nc.Block())

            @block.sync
            def _(sp):
                with nc.allow_non_contiguous_dma(reason="one scalar of each channel"):
                    sp.dma_start(gamma[:, 0:1], ln_gamma.rearrange("(p o) -> p o", o=1)).then_inc(loaded, 16)
                    sp.dma_start(gamma[:, 1:2], ln_beta.rearrange("(p o) -> p o", o=1)).then_inc(loaded, 16)
                sp.dma_start(gate_raw[:], gate_w).then_inc(loaded, 16)
                sp.dma_start(b1_raw[:], b1s.rearrange("e (q f) -> (e q) f", f=P)).then_inc(loaded, 16)
                sp.dma_start(b2_all[:].rearrange("p e d -> p (e d)"),
                             b2s.rearrange("(o e) d -> o (e d)", o=1).broadcast_to([P, E * DM])
                             ).then_inc(loaded, 16)
                sp.wait_ge(score_ready, NB)
                sp.dma_start(score_dram, score[:]).then_inc(score_stored, 16)
                sp.wait_ge(score_stored, 16)
                sp.dma_start(search[:], score_dram.rearrange("e (j t) -> (e j) t", j=J)
                             ).then_inc(search_loaded, 16)
                sp.wait_ge(base_ready, 4)
                sp.dma_start(dst.rearrange("(i p) d -> p i d", p=P), base[:]).then_inc(stored, 16)
                sp.wait_ge(rows_ready, TILES)
                sp.wait_ge(weights_ready, 1)
                sp.dma_start(table.rearrange("(i p) d -> p i d", p=P), rows[:]).then_inc(stored, 16)
                sp.wait_ge(search_loaded, 16)
                sp.wait_ge(stored, 32)
                sp.wait_ge(loaded, 16 * 5)

            @block.vector
            def _(dve):
                at = layer_norm_constants(dve, chain, 0, stats, moments, lambda i: X[:, i, :], TILES)
                dve.tensor_scalar(rstd[:], moments[:, :, 1], LN_EPS, None, ALU.add).then_inc(variance, 1)
                dve.wait_ge(std_done, 1)
                dve.reciprocal(rstd[:], rstd[:]).then_inc(ln_ready, 1)
                dve.wait_ge(ln_ready, 1)
                dve.scalar_tensor_tensor(out=shift[:], in0=moments[:, :, 0], scalar=-1.0, in1=rstd[:],
                                         op0=ALU.mult, op1=ALU.mult).then_inc(ln_ready, 1)
                dve.tensor_tensor(again[:], rstd[:], rstd[:], ALU.mult).then_inc(chain, 1)
                dve.wait_ge(chain, at + 1)
                dve.tensor_tensor(again[:], again[:], moments[:, :, 1], ALU.mult).then_inc(chain, 1)
                dve.wait_ge(chain, at + 2)
                dve.tensor_scalar(again[:], again[:], LN_EPS, None, ALU.add).then_inc(variance2, 1)
                dve.wait_ge(ln_ready, 2)
                for i in range(TILES):
                    dve.tensor_scalar(f[:, i, :], X[:, i, :], rstd[:, i:i + 1], shift[:, i:i + 1],
                                      ALU.mult, ALU.add).then_inc(f_ready, 1)
                    if i == 3:
                        dve.wait_ge(std2_done, 1)
                        dve.reciprocal(again[:], again[:]).then_inc(chain, 1)
                        dve.wait_ge(chain, at + 3)
                        dve.tensor_tensor(rstd2[:], rstd[:], again[:], ALU.mult).then_inc(ln2_ready, 1)
                        dve.tensor_tensor(shift2[:], shift[:], again[:], ALU.mult).then_inc(ln2_ready, 1)
                dve.wait_ge(small_turned, 2)
                dve.tensor_copy(gate_T[:], psum[:, 7, 0:E]).then_inc(small_ready, 1)
                dve.tensor_copy(b1_T[:], psum[:, 7, P:P + E * FB]).then_inc(small_ready, 1)
                for g in range(0, NB, 2):
                    dve.wait_ge(f_turned, g + 1)
                    dve.tensor_copy(f_T[:, g * BANK:(g + 1) * BANK], psum[:, g % 4, :]).then_inc(fT_even, 1)
                for g in range(NB):
                    dve.wait_ge(tanh_done, g + 1)
                    part = score[:, g * BANK:(g + 1) * BANK]
                    dve.tensor_scalar(part, part, 1.0, -1.0, ALU.add, ALU.add).then_inc(score_ready, 1)
                dve.wait_ge(score_turned, TILES)
                dve.tensor_scalar(rows[:, :, DM:ROW],
                                  psum[:, 7, 0:TILES * E].rearrange("p (i e) -> p i e", e=E), 1.0, 0.5,
                                  ALU.add, ALU.mult).then_inc(weights_ready, 1)

            @block.scalar
            def _(act):
                act.wait_ge(variance, 1)
                act.activation(rstd[:], rstd[:], ACT.Sqrt).then_inc(std_done, 1)
                act.wait_ge(variance2, 1)
                act.activation(again[:], again[:], ACT.Sqrt).then_inc(std2_done, 1)
                for g in range(1, NB, 2):
                    act.wait_ge(f_turned, g + 1)
                    act.copy(f_T[:, g * BANK:(g + 1) * BANK], psum[:, g % 4, :]).then_inc(fT_odd, 1)
                for g in range(NB):
                    act.wait_ge(gated, g + 1)
                    act.activation(score[:, g * BANK:(g + 1) * BANK], psum[0:E, 4 + g % 2, :],
                                   ACT.Tanh).then_inc(tanh_done, 1)
                act.wait_ge(ln2_ready, 2)
                for i in range(TILES):
                    act.activation(rows[:, i, 0:DM], X[:, i, :], ACT.Identity, bias=shift2[:, i:i + 1],
                                   scale=rstd2[:, i:i + 1]).then_inc(rows_ready, 1)

            @block.gpsimd
            def _(pool):
                quarter = TILES // 4
                for n in range(4):
                    part = slice(n * quarter, (n + 1) * quarter)
                    pool.wait_ge(f_ready, (n + 1) * quarter)
                    pool.tensor_tensor(base[:, part, :], X[:, part, :], f[:, part, :],
                                       ALU.add).then_inc(base_ready, 1)

            @block.tensor
            def _(pe):
                pe.wait_ge(loaded, 16 * 5)
                pe.transpose(psum[:, 7, 0:E], gate_raw[:], ident[0:E, 0:E]).then_inc(small_turned, 1)
                pe.transpose(psum[:, 7, P:P + E * FB], b1_raw[:],
                             ident[0:E * FB, 0:E * FB]).then_inc(small_turned, 1)
                for g in range(NB):
                    if g >= 4:
                        pe.wait_ge(fT_even if g % 2 == 0 else fT_odd, (g - 4) // 2 + 1)
                    for i in range(4):
                        pe.wait_ge(f_ready, 4 * g + i + 1)
                        last = pe.transpose(psum[:, g % 4, i * P:(i + 1) * P], f[:, 4 * g + i, :], ident[:])
                    last.then_inc(f_turned, 1)
                pe.wait_ge(small_ready, 2)
                for g in range(NB):
                    pe.wait_ge(fT_even if g % 2 == 0 else fT_odd, g // 2 + 1)
                    if g >= 2:
                        pe.wait_ge(tanh_done, g - 1)
                    pe.matmul(psum[0:E, 4 + g % 2, :], gate_T[:], f_T[:, g * BANK:(g + 1) * BANK],
                              start=True, stop=True).then_inc(gated, 1)
                for i in range(TILES):
                    pe.wait_ge(score_ready, i // 4 + 1)
                    pe.transpose(psum[:, 7, i * E:(i + 1) * E], score[:, i * P:(i + 1) * P],
                                 ident[0:E, 0:E]).then_inc(score_turned, 1)

        with nc.cleanup_on_exit(), ExitStack() as ctx:
            def sb(what, shape, dt=F32):
                return ctx.enter_context(nc.sbuf_tensor(f"{name}_{what}", shape, dt))

            def sem(what):
                return nc.alloc_semaphore(f"{name}_{what}")

            psum = ctx.enter_context(nc.psum_tensor(f"{name}_psum2", [P, 8, BANK], F32))
            same = sb("same", [P, P])
            before = sb("before", [P, P])
            same_b = sb("same_b", [P, P], BF16)
            before_b = sb("before_b", [P, P], BF16)
            steps = sb("steps", [P, 2, STEPS])
            candidate = sb("candidate", [P, 1])
            move = sb("move", [P, 1])
            hits = sb("hits", [P, SPAN], BF16)
            count = sb("count", [P, 1], BF16)
            ones = sb("ones", [P, SPAN])
            above = sb("above", [P, 2, SPAN])
            rank = sb("rank", [P, 2, SPAN])
            row_count = sb("row_count", [P, 2], BF16)
            offset = sb("offset", [P, 2])
            place = sb("place", [P, SPAN])
            place_T = sb("place_T", [P, PAIRS], I32)
            low_T = sb("low_T", [P, PAIRS], I32)
            high_T = sb("high_T", [P, PAIRS], I32)
            iota_i = sb("iota_i", [P, LO], I32)
            iota = sb("iota", [P, LO])
            lane_i = sb("lane_i", [P, 1], I32)
            lane = sb("lane", [P, 1])
            first_i = sb("first_i", [P, PAIRS], I32)
            first = sb("first", [P, PAIRS], BF16)
            one_low = sb("one_low", [P, PAIRS, LO], BF16)
            one_high = sb("one_high", [P, PAIRS, 3, HI], BF16)
            found = sb("found", [LO, E, HI])

            made = sem("made")
            cast = sem("cast")
            counted = sem("counted")
            totalled = sem("totalled")
            moved = sem("moved")
            chain = sem("chain2")
            rowed = sem("rowed")
            offsets = sem("offsets")
            placed = sem("placed")
            place_turned = sem("place_turned")
            high_ready = sem("high_ready")
            low_ready = sem("low_ready2")
            listed = sem("listed")
            GROUP = 32
            block = ctx.enter_context(nc.Block())

            @block.gpsimd
            def _(pool):
                pool.memset(same[:], 1.0).then_inc(made, 1)
                view = same[:].rearrange("p (e j) -> p e j", j=J)
                pool.wait_ge(made, 1)
                pool.affine_select(out=view, in_=view, compare_op=ALU.is_ge, fill=0.0, base=0,
                                   pattern=[[-J, E], [0, J]], channel_multiplier=1).then_inc(made, 1)
                pool.wait_ge(made, 2)
                pool.affine_select(out=view, in_=view, compare_op=ALU.is_ge, fill=0.0, base=J - 1,
                                   pattern=[[J, E], [0, J]], channel_multiplier=-1).then_inc(made, 1)
                pool.wait_ge(made, 3)
                pool.affine_select(out=before[:], in_=same[:], compare_op=ALU.is_ge, fill=0.0, base=-1,
                                   pattern=[[1, P]], channel_multiplier=-1).then_inc(made, 1)
                pool.memset(ones[:], 1.0).then_inc(made, 1)
                pool.iota(iota_i[:], pattern=[[1, LO]], base=0, channel_multiplier=0).then_inc(made, 1)
                pool.iota(lane_i[:], pattern=[[0, 1]], base=0, channel_multiplier=1).then_inc(made, 1)
                pool.iota(first_i[:], pattern=[[1, HALVES], [0, E], [HALVES, J]], base=0,
                          channel_multiplier=0).then_inc(made, 1)
                pool.wait_ge(made, 8)
                pool.tensor_copy(before_b[:], before[:]).then_inc(cast, 1)
                pool.tensor_copy(iota[:], iota_i[:]).then_inc(cast, 1)
                pool.tensor_copy(lane[:], lane_i[:]).then_inc(cast, 1)
                pool.tensor_copy(first[:], first_i[:]).then_inc(cast, 1)
                pool.tensor_copy(same_b[:], same[:]).then_inc(cast, 1)

            @block.vector
            def _(dve):
                for i in range(STEPS):
                    size = 2.0 ** -i
                    dve.memset(steps[:, 0, i:i + 1], size).then_inc(chain, 1)
                    dve.memset(steps[:, 1, i:i + 1],
                               -size / 2 if i < STEPS - 1 else -size).then_inc(chain, 1)
                dve.memset(candidate[:], 0.0).then_inc(moved, 1)
                at = 2 * STEPS
                dve.wait_ge(chain, at)
                with dve.Fori(0, STEPS) as i:
                    dve.wait_ge(moved, i + 1)
                    dve.tensor_scalar(hits[:], search[:], candidate[:, 0:1], None, ALU.is_ge, ALU.add,
                                      accum_out=count[:]).then_inc(counted, 1)
                    dve.wait_ge(totalled, i + 1)
                    dve.tensor_scalar(move[:], psum[:, 0, 0:1], K - 0.5, steps[:, 0, bass.ds(i, 1)],
                                      ALU.is_ge, ALU.mult).then_inc(chain, 1)
                    dve.wait_ge(chain, at + i + 1)
                    dve.scalar_tensor_tensor(out=candidate[:], in0=move[:],
                                             scalar=steps[:, 1, bass.ds(i, 1)], in1=candidate[:],
                                             op0=ALU.add, op1=ALU.add).then_inc(moved, 1)
                dve.wait_ge(moved, STEPS + 1)
                at = at + STEPS
                dve.tensor_scalar(above[:, 0, :], search[:], candidate[:, 0:1], None,
                                  ALU.is_gt).then_inc(chain, 1)
                dve.tensor_scalar(above[:, 1, :], search[:], candidate[:, 0:1], None,
                                  ALU.is_equal).then_inc(chain, 1)
                dve.wait_ge(cast, 5)
                for n in range(2):
                    dve.wait_ge(chain, at + n + 1)
                    dve.tensor_tensor_scan(rank[:, n, :], ones[:], above[:, n, :], 0.0, ALU.mult,
                                           ALU.add).then_inc(chain, 1)
                dve.wait_ge(chain, at + 4)
                dve.tensor_copy(row_count[:], rank[:, :, SPAN - 1]).then_inc(rowed, 1)
                dve.wait_ge(offsets, 1)
                dve.tensor_scalar(offset[:, 0:1], psum[:, 0, 8:9], -1.0 - FAR, None,
                                  ALU.add).then_inc(chain, 1)
                dve.tensor_scalar(offset[:, 1:2], psum[:, 0, 9:10], -1.0 - FAR, None,
                                  ALU.add).then_inc(chain, 1)
                dve.wait_ge(chain, at + 6)
                dve.tensor_tensor(offset[:, 1:2], offset[:, 1:2], psum[:, 0, 16:17],
                                  ALU.add).then_inc(chain, 1)
                dve.wait_ge(chain, at + 7)
                for n in range(2):
                    dve.scalar_tensor_tensor(out=rank[:, n, :], in0=rank[:, n, :],
                                             scalar=offset[:, n:n + 1], in1=above[:, n, :],
                                             op0=ALU.add, op1=ALU.mult).then_inc(chain, 1)
                dve.wait_ge(chain, at + 9)
                dve.scalar_tensor_tensor(out=place[:], in0=rank[:, 0, :], scalar=FAR, in1=rank[:, 1, :],
                                         op0=ALU.add, op1=ALU.add).then_inc(placed, 1)
                dve.wait_ge(place_turned, 1)
                dve.tensor_copy(place_T[:], psum[:, 1, 0:PAIRS]).then_inc(chain, 1)
                dve.wait_ge(chain, at + 10)
                dve.tensor_scalar(high_T[:], place_T[:], LO.bit_length() - 1, None,
                                  ALU.logical_shift_right).then_inc(chain, 1)
                dve.tensor_scalar(low_T[:], place_T[:], LO - 1, None, ALU.bitwise_and).then_inc(chain, 1)
                dve.wait_ge(chain, at + 12)
                dve.tensor_tensor(one_high[:, :, 0, :],
                                  high_T[:].unsqueeze(2).broadcast_to([P, PAIRS, HI]),
                                  iota[:, 0:HI].unsqueeze(1).broadcast_to([P, PAIRS, HI]),
                                  ALU.is_equal).then_inc(chain, 1)
                dve.wait_ge(chain, at + 13)
                dve.tensor_scalar(one_high[:, :, 1, :], one_high[:, :, 0, :], lane[:, 0:1], None,
                                  ALU.mult).then_inc(high_ready, 1)
                dve.tensor_tensor(one_high[:, :, 2, :], one_high[:, :, 0, :],
                                  first[:].unsqueeze(2).broadcast_to([P, PAIRS, HI]),
                                  ALU.mult).then_inc(high_ready, 1)
                for n in range(PAIRS // GROUP):
                    part = one_low[:].rearrange("p (h e j) l -> p h e j l", h=HALVES, j=J)[:, :, n]
                    dve.tensor_tensor(
                        part,
                        low_T[:].rearrange("p (h e j) -> p h e j", h=HALVES, j=J)[:, :, n]
                        .unsqueeze(3).broadcast_to([P, HALVES, J, LO]),
                        iota[:].unsqueeze(1).unsqueeze(1).broadcast_to([P, HALVES, J, LO]),
                        ALU.is_equal).then_inc(low_ready, 1)
                for e in range(E):
                    dve.wait_ge(listed, e + 1)
                    dve.tensor_copy(found[:, e, :], psum[0:LO, 2 + e % 2, HI:2 * HI]).then_inc(chain, 1)
                    dve.wait_ge(chain, at + 13 + e + 1)
                    for q in range(P // LO):
                        dve.scalar_tensor_tensor(
                            out=tokens[q * LO:(q + 1) * LO, e, :],
                            in0=found[:, e, q:HI:P // LO], scalar=float(P),
                            in1=psum[0:LO, 2 + e % 2, q:HI:P // LO],
                            op0=ALU.mult, op1=ALU.add).then_inc(rowed, 1)

            @block.tensor
            def _(pe):
                pe.wait_ge(cast, 5)
                with pe.Fori(0, STEPS) as i:
                    pe.wait_ge(counted, i + 1)
                    pe.matmul(psum[:, 0, 0:1], same_b[:], count[:], start=True,
                              stop=True).then_inc(totalled, 1)
                pe.wait_ge(rowed, 1)
                pe.matmul(psum[:, 0, 8:10], before_b[:], row_count[:], start=True, stop=True)
                pe.matmul(psum[:, 0, 16:17], same_b[:], row_count[:, 0:1], start=True,
                          stop=True).then_inc(offsets, 1)
                pe.wait_ge(placed, 1)
                for h in range(HALVES):
                    last = pe.transpose(psum[:, 1, h * P:(h + 1) * P], place[:, h * P:(h + 1) * P],
                                        ident[:])
                last.then_inc(place_turned, 1)
                pe.wait_ge(high_ready, 2)
                for e in range(E):
                    pe.wait_ge(low_ready, e + 1)
                    if e >= 2:
                        pe.wait_ge(rowed, 1 + P // LO * (e - 1))
                    pairs = [h * P + e * J + j for h in range(HALVES) for j in range(J)]
                    for pair in pairs:
                        last = pe.matmul(psum[0:LO, 2 + e % 2, 0:2 * HI], one_low[:, pair, :],
                                         one_high[:, pair, 1:3, :].rearrange("p a h -> p (a h)"),
                                         start=(pair == pairs[0]), stop=(pair == pairs[-1]))
                    last.then_inc(listed, 1)

        with nc.cleanup_on_exit(), ExitStack() as ctx:
            def sb(what, shape, dt=F32):
                return ctx.enter_context(nc.sbuf_tensor(f"{name}_{what}", shape, dt))

            def sem(what):
                return nc.alloc_semaphore(f"{name}_{what}")

            psum = ctx.enter_context(nc.psum_tensor(f"{name}_psum3", [P, 8, BANK], F32))
            TURN, YT, HID, OUT = 0, 2, 3, 5
            HBANKS = 2
            w1 = sb("w1", [P, 2, FB, DM])
            w2 = sb("w2", [P, 2, FF])
            w1_T = sb("w1_T", [P, 2, FF])
            w2_T = sb("w2_T", [P, 2, FB, DM])
            got = sb("got", [P, 2, KT, ROW])
            y_T = sb("y_T", [P, 2, K])
            hidden = sb("hidden", [P, 2, FB, K])
            o = sb("o", [P, 2, KT, DM])
            w1_loaded = [sem(f"w1_loaded{r}") for r in range(2)]
            w2_loaded = [sem(f"w2_loaded{r}") for r in range(2)]
            w1_turned = sem("w1_turned")
            w2_turned = sem("w2_turned")
            w1_ready = sem("w1_ready")
            w2_ready = sem("w2_ready")
            gathered = [sem(f"gathered{r}") for r in range(2)]
            y_turned = sem("y_turned")
            y_ready = sem("y_ready")
            hidden_summed = sem("hidden_summed")
            hidden_ready = sem("hidden_ready")
            o_summed = sem("o_summed")
            o_biased = sem("o_biased")
            o_ready = sem("o_ready")
            o_free = sem("o_free")
            scattered = [sem(f"scattered{r}") for r in range(2)]
            block = ctx.enter_context(nc.Block())
            TWO = E // 2

            @block.sync
            def _(sp):
                with sp.Fori(0, TWO) as m:
                    for r in range(2):
                        sp.wait_ge(w2_turned, 2 * m + 1)
                        sp.dma_start(w1[:, r], fc1s[bass.ds(2 * m + r, 1)]
                                     .rearrange("o (q p) d -> p (o q) d", p=P)).then_inc(w1_loaded[r], 16)
                        sp.dma_start(w2[:, r], fc2s[bass.ds(2 * m + r, 1)]
                                     .rearrange("o d f -> d (o f)")).then_inc(w2_loaded[r], 16)

            @block.gpsimd
            def _(pool):
                def gather(e):
                    for t in range(KT):
                        pool.indirect_dma_start(got[:, e % 2, t, :], None, table,
                                                bass.IndirectOffsetOnAxis(ap=tokens[:, e, t:t + 1], axis=0)
                                                ).then_inc(gathered[e % 2], 16)

                gather(0)
                gather(1)
                pool.sem_inc(o_free, 2)
                for e in range(E):
                    pool.wait_ge(o_ready, e + 1)
                    if e:
                        pool.wait_ge(scattered[(e - 1) % 2], 16 * KT * ((e - 1) // 2 + 1))
                        pool.sem_inc(o_free, 1)
                    for t in range(KT):
                        pool.indirect_dma_start(dst,
                                                bass.IndirectOffsetOnAxis(ap=tokens[:, e, t:t + 1], axis=0),
                                                o[:, e % 2, t, :], None, compute_op=ALU.add
                                                ).then_inc(scattered[e % 2], 16)
                    if e + 2 < E:
                        gather(e + 2)
                pool.wait_ge(scattered[(E - 1) % 2], 16 * KT * TWO)
                pool.wait_ge(scattered[(E - 2) % 2], 16 * KT * TWO)

            @block.vector
            def _(dve):
                dve.sem_inc(w1_ready, 1)
                dve.sem_inc(w2_ready, 1)
                with dve.Fori(0, TWO) as m:
                    for r in range(2):
                        dve.wait_ge(w1_turned, 2 * m + r + 1)
                        dve.tensor_copy(w1_T[:, r, :], psum[:, TURN, :]).then_inc(w1_ready, 1)
                        dve.wait_ge(w2_turned, 2 * m + r + 2)
                        dve.tensor_copy(w2_T[:, r].rearrange("p q d -> p (q d)"),
                                        psum[:, TURN + 1, :]).then_inc(w2_ready, 1)
                        dve.wait_ge(o_summed, 2 * m + r + 1)
                        dve.wait_ge(o_free, 2 * m + r + 1)
                        dve.wait_ge(gathered[r], 16 * KT * (m + 1))
                        dve.tensor_tensor(
                            o[:, r],
                            psum[:, OUT + r, :].rearrange("p (t d) -> p t d", d=DM),
                            b2_all[:, bass.ds(2 * m + r, 1), :].broadcast_to([P, KT, DM]),
                            ALU.add).then_inc(o_biased, 1)
                        dve.wait_ge(o_biased, 2 * m + r + 1)
                        for t in range(KT):
                            last = dve.tensor_scalar(o[:, r, t, :], o[:, r, t, :],
                                                     got[:, r, t, bass.ds(DM + 2 * m + r, 1)], None,
                                                     ALU.mult)
                        last.then_inc(o_ready, 1)

            @block.scalar
            def _(act):
                act.sem_inc(y_ready, 1)
                with act.Fori(0, TWO) as m:
                    for r in range(2):
                        act.wait_ge(y_turned, 2 * m + r + 1)
                        act.activation(y_T[:, r, :], psum[:, YT, :], ACT.Identity, bias=gamma[:, 1:2],
                                       scale=gamma[:, 0:1]).then_inc(y_ready, 1)
                        for q in range(FB):
                            act.wait_ge(hidden_summed, FB * (2 * m + r) + q + 1)
                            act.activation(hidden[:, r, q, :], psum[:, HID + q % HBANKS, :],
                                           ACT.Gelu_apprx_tanh,
                                           bias=b1_T[:, bass.ds(FB * (2 * m + r) + q, 1)]
                                           ).then_inc(hidden_ready, 1)

            @block.tensor
            def _(pe):
                pe.sem_inc(w2_turned, 1)
                with pe.Fori(0, TWO) as m:
                    for r in range(2):
                        e = 2 * m + r
                        pe.wait_ge(w1_loaded[r], 16 * (m + 1))
                        pe.wait_ge(w1_ready, e + 1)
                        for q in range(FB):
                            last = pe.transpose(psum[:, TURN, q * P:(q + 1) * P], w1[:, r, q, :], ident[:])
                        last.then_inc(w1_turned, 1)
                        pe.wait_ge(w2_loaded[r], 16 * (m + 1))
                        pe.wait_ge(w2_ready, e + 1)
                        for q in range(FB):
                            last = pe.transpose(psum[:, TURN + 1, q * P:(q + 1) * P],
                                                w2[:, r, q * P:(q + 1) * P], ident[:])
                        last.then_inc(w2_turned, 1)
                        pe.wait_ge(gathered[r], 16 * KT * (m + 1))
                        pe.wait_ge(y_ready, e + 1)
                        for t in range(KT):
                            last = pe.transpose(psum[:, YT, t * P:(t + 1) * P], got[:, r, t, 0:DM], ident[:])
                        last.then_inc(y_turned, 1)
                        pe.wait_ge(y_ready, e + 2)
                        pe.wait_ge(w1_ready, e + 2)
                        for q in range(FB):
                            if q >= HBANKS:
                                pe.wait_ge(hidden_ready, FB * e + q - HBANKS + 1)
                            pe.matmul(psum[:, HID + q % HBANKS, :], w1_T[:, r, q * P:(q + 1) * P],
                                      y_T[:, r, :], start=True, stop=True).then_inc(hidden_summed, 1)
                        pe.wait_ge(w2_ready, e + 2)
                        pe.wait_ge(hidden_ready, FB * (e + 1))
                        for t in range(KT):
                            for q in range(FB):
                                last = pe.matmul(psum[:, OUT + r, t * DM:(t + 1) * DM],
                                                 hidden[:, r, q, t * P:(t + 1) * P], w2_T[:, r, q, :],
                                                 start=(q == 0), stop=(q == FB - 1))
                        last.then_inc(o_summed, 1)


def attention(nc, X, ident, source, wq, wk, wv, wo):
    HD, DM = wq.shape
    BATCH = 2
    TILES = X.shape[1]
    TB = TILES // BATCH
    T = TILES * P
    NB = T // BANK
    SCALE = (3.0 / HD) ** 0.5
    with nc.cleanup_on_exit(), ExitStack() as ctx:
        def sb(what, shape, dt=F32):
            return ctx.enter_context(nc.sbuf_tensor(f"a_{what}", shape, dt))

        def sem(what):
            return nc.alloc_semaphore(f"a_{what}")

        psum = ctx.enter_context(nc.psum_tensor("a_psum", [P, 8, BANK], F32))
        stats = sb("stats", [P, TILES, 6])
        moments = sb("moments", [P, TILES, 2])
        rstd = sb("rstd", [P, TILES])
        shift = sb("shift", [P, TILES])
        f = sb("f", [P, TILES, DM])
        f_T = sb("f_T", [P, T])
        q_w = sb("q_w", [HD, DM])
        kv_w = sb("kv_w", [HD, 2, DM])
        o_w = sb("o_w", [DM, HD])
        kv_T = sb("kv_T", [P, 2, HD])
        o_T = sb("o_T", [HD, DM])
        gram = sb("gram", [P, BATCH, DM])
        gv = sb("gv", [P, BATCH, HD])
        energy_T = sb("energy_T", [HD, BATCH, HD])
        eo = sb("eo", [HD, BATCH, DM])
        mix = sb("mix", [P, BATCH, DM])

        x_loaded = [sem(f"x_loaded{n}") for n in range(4)]
        loaded = sem("loaded")
        chain = sem("chain")
        variance = sem("variance")
        std_done = sem("std_done")
        ln_ready = sem("ln_ready")
        f_ready = sem("f_ready")
        turned = sem("turned")
        fT_ready = sem("fT_ready")
        small_turned = sem("small_turned")
        small_ready = sem("small_ready")
        gram_summed = sem("gram_summed")
        link = sem("link")
        linked = sem("linked")
        out_ready = sem("out_ready")
        added = sem("added")
        block = ctx.enter_context(nc.Block())
        QT = TILES // 4

        @block.sync
        def _(sp):
            for n in range(4):
                sp.dma_start(X[:, n * QT:(n + 1) * QT, :],
                             source[n * QT * P:(n + 1) * QT * P, :].rearrange("(i p) d -> p i d", p=P)
                             ).then_inc(x_loaded[n], 16)
            for out, what in ((q_w[:], wq), (kv_w[:, 0, :], wk), (kv_w[:, 1, :], wv), (o_w[:], wo)):
                sp.dma_start(out, what).then_inc(loaded, 16)

        @block.vector
        def _(dve):
            for i in range(TILES):
                if i % QT == 0:
                    dve.wait_ge(x_loaded[i // QT], 16)
                dve.bn_stats(stats[:, i, :], X[:, i, :]).then_inc(chain, 1)
            dve.wait_ge(chain, TILES)
            for i in range(TILES):
                dve.bn_aggr(moments[:, i, :], stats[:, i, :]).then_inc(chain, 1)
            dve.wait_ge(chain, 2 * TILES)
            dve.tensor_scalar(rstd[:], moments[:, :, 1], LN_EPS, None, ALU.add).then_inc(variance, 1)
            dve.wait_ge(std_done, 1)
            dve.reciprocal(rstd[:], rstd[:]).then_inc(ln_ready, 1)
            dve.wait_ge(ln_ready, 1)
            dve.scalar_tensor_tensor(out=shift[:], in0=moments[:, :, 0], scalar=-1.0, in1=rstd[:],
                                     op0=ALU.mult, op1=ALU.mult).then_inc(ln_ready, 1)
            dve.wait_ge(ln_ready, 2)
            for i in range(TILES):
                dve.tensor_scalar(f[:, i, :], X[:, i, :], rstd[:, i:i + 1], shift[:, i:i + 1],
                                  ALU.mult, ALU.add).then_inc(f_ready, 1)
            dve.wait_ge(small_turned, 3)
            dve.tensor_copy(kv_T[:], psum[:, 7, 0:2 * HD].rearrange("p (a h) -> p a h", a=2)
                            ).then_inc(small_ready, 1)
            dve.tensor_copy(o_T[:], psum[0:HD, 7, 2 * HD:2 * HD + DM]).then_inc(small_ready, 1)
            n = 0
            for b in range(BATCH):
                dve.wait_ge(gram_summed, b + 1)
                dve.tensor_copy(gram[:, b, :], psum[:, 4 + b, 0:DM]).then_inc(linked, 1)
                for where in (gv[:, b, :], energy_T[:, b, :], eo[:, b, :], mix[:, b, :]):
                    rows, width = where.shape
                    dve.wait_ge(link, n + 1)
                    if n % 4 == 2:
                        dve.tensor_scalar(where, psum[0:rows, 6, 0:width], SCALE, None,
                                          ALU.mult).then_inc(linked, 1)
                    else:
                        dve.tensor_copy(where, psum[0:rows, 6, 0:width]).then_inc(linked, 1)
                    n += 1
            for g in range(NB):
                dve.wait_ge(out_ready, g + 1)
                rows = X[:, 4 * g:4 * g + 4, :].rearrange("p i d -> p (i d)")
                dve.tensor_tensor(rows, rows, psum[:, g % 4, :], ALU.add).then_inc(added, 1)

        @block.scalar
        def _(act):
            act.wait_ge(variance, 1)
            act.activation(rstd[:], rstd[:], ACT.Sqrt).then_inc(std_done, 1)
            for g in range(NB):
                act.wait_ge(turned, g + 1)
                act.copy(f_T[:, g * BANK:(g + 1) * BANK], psum[:, g % 4, :]).then_inc(fT_ready, 1)

        @block.tensor
        def _(pe):
            pe.wait_ge(loaded, 16 * 4)
            for n in range(2):
                pe.transpose(psum[:, 7, n * HD:(n + 1) * HD], kv_w[:, n, :],
                             ident[0:HD, 0:HD]).then_inc(small_turned, 1)
            pe.transpose(psum[0:HD, 7, 2 * HD:2 * HD + DM], o_w[:], ident[:]).then_inc(small_turned, 1)
            for g in range(NB):
                if g >= 4:
                    pe.wait_ge(fT_ready, g - 3)
                for i in range(4):
                    tile = 4 * g + i
                    pe.wait_ge(f_ready, tile + 1)
                    last = pe.transpose(psum[:, g % 4, i * P:(i + 1) * P], f[:, tile, :], ident[:])
                    b, first = divmod(tile, TB)
                    gram_last = pe.matmul(psum[:, 4 + b, 0:DM], f[:, tile, :], f[:, tile, :],
                                          start=(first == 0), stop=(first == TB - 1))
                    if first == TB - 1:
                        gram_last.then_inc(gram_summed, 1)
                last.then_inc(turned, 1)
            pe.wait_ge(small_ready, 2)
            n = 0
            for b in range(BATCH):
                for out, left, right in (
                    (psum[:, 6, 0:HD], gram[:, b, :], kv_T[:, 1, :]),
                    (psum[0:HD, 6, 0:HD], gv[:, b, :], kv_T[:, 0, :]),
                    (psum[0:HD, 6, 0:DM], energy_T[:, b, :], o_T[:]),
                    (psum[:, 6, 0:DM], q_w[:], eo[:, b, :]),
                ):
                    pe.wait_ge(linked, n + b + 1)
                    pe.matmul(out, left, right, start=True, stop=True).then_inc(link, 1)
                    n += 1
            pe.wait_ge(linked, 5 * BATCH)
            pe.wait_ge(fT_ready, NB)
            for g in range(NB):
                if g >= 4:
                    pe.wait_ge(added, g - 3)
                for i in range(4):
                    tile = 4 * g + i
                    last = pe.matmul(psum[:, g % 4, i * P:(i + 1) * P], f_T[:, tile * P:(tile + 1) * P],
                                     mix[:, tile // TB, :], start=True, stop=True)
                last.then_inc(out_ready, 1)


def build(nc, inputs, out):
    mixer = {k[len("L0_attn_a_"):]: v for k, v in inputs.items() if k.startswith("L0_attn_a_")}
    linear = {k[len("L0_attn_b_"):]: v for k, v in inputs.items() if k.startswith("L0_attn_b_")}
    experts = {k[len("L0_ffn_"):]: v for k, v in inputs.items() if k.startswith("L0_ffn_")}
    BATCH, L, DM = mixer["x"].shape
    T = BATCH * L
    between = nc.dram_tensor("between", [T, DM], F32, kind="Internal").ap()
    with ExitStack() as ctx:
        X = ctx.enter_context(nc.sbuf_tensor("X", [P, T // P, DM], F32))
        ident = ctx.enter_context(nc.sbuf_tensor("ident", [P, P], F32))
        identity(nc, ident)
        mamba(nc, X, ident, **mixer)
        moe(nc, X, ident, "f1", between, **experts)
        attention(nc, X, ident, between, **linear)
        moe(nc, X, ident, "f2", out.rearrange("b l d -> (b l) d"), **experts)


_INS = ["L0_attn_a_x", "L0_attn_a_W_in", "L0_attn_a_conv_w", "L0_attn_a_conv_b", "L0_attn_a_A_log",
        "L0_attn_a_D", "L0_attn_a_W_x", "L0_attn_a_W_dt", "L0_attn_a_b_dt", "L0_attn_a_W_out",
        "L0_attn_b_wq", "L0_attn_b_wk", "L0_attn_b_wv", "L0_attn_b_wo",
        "L0_ffn_gate_w", "L0_ffn_ln_gamma", "L0_ffn_ln_beta", "L0_ffn_fc1s", "L0_ffn_b1s",
        "L0_ffn_fc2s", "L0_ffn_b2s"]


def kernel(**inputs):
    import numpy as _np
    import concourse.bacc as _bacc
    from concourse.bass_utils import run_bass_kernel_spmd as _run

    nc = _bacc.Bacc("TRN2", target_bir_lowering=False, num_devices=1)
    arrays, args = {}, {}
    for name in _INS:
        a = _np.ascontiguousarray(inputs[name])
        arrays[f"in_{name}"] = a
        args[name] = nc.dram_tensor(f"in_{name}", a.shape, mybir.dt.from_np(a.dtype),
                                    kind="ExternalInput").ap()
    out = nc.dram_tensor("out_0", arrays["in_L0_attn_a_x"].shape, F32, kind="ExternalOutput").ap()
    build(nc, args, out)
    r = _run(nc, [arrays], core_ids=[0])
    return r.results[0]["out_0"]
```

```python
from contextlib import ExitStack

import concourse.bass as bass
from concourse import mybir

F32 = mybir.dt.float32
F32R = mybir.dt.float32r
BF16 = mybir.dt.bfloat16
F16 = mybir.dt.float16
I32 = mybir.dt.int32
ACT = mybir.ActivationFunctionType
ALU = mybir.AluOpType

P = 128
BANK = 512
LN_EPS = 1e-5


def layer_norm_constants(dve, chain, at, stats, moments, source, tiles):
    for i in range(tiles):
        dve.bn_stats(stats[:, i, :], source(i)).then_inc(chain, 1)
    dve.wait_ge(chain, at + tiles)
    for i in range(tiles):
        dve.bn_aggr(moments[:, i, :], stats[:, i, :]).then_inc(chain, 1)
    dve.wait_ge(chain, at + 2 * tiles)
    return at + 2 * tiles


def mamba(nc, X, ident, x, W_in, conv_w, conv_b, A_log, D, W_x, W_dt, b_dt, W_out):
    BATCH, L, DM = x.shape
    KC, _, CH = conv_w.shape
    NS = A_log.shape[1]
    R = W_dt.shape[0]
    KB = CH // P
    TILES = L // P
    CHUNK = 1024
    NCHUNK = L // CHUNK
    CT = CHUNK // P
    TB = CHUNK // BANK
    RING = 4
    STEPS = NCHUNK * NS * KB
    LEFT = 1
    B_AT, LOW_AT, C_AT = 64, 96, 96
    assert NCHUNK == 2 and BATCH == 2 and R <= B_AT and KB == TB == 2

    with nc.cleanup_on_exit(), ExitStack() as ctx:
        def sb(name, shape, dt=F32):
            return ctx.enter_context(nc.sbuf_tensor(name, shape, dt))

        def sem(name):
            return nc.alloc_semaphore(name)

        psum = ctx.enter_context(nc.psum_tensor("m_psum", [P, 8, BANK], F32))
        Y, BCAST, PIECE = 0, 4, 6

        w_z = sb("w_z", [P, CH])
        w_tap = sb("w_tap", [P, KC, CH])
        w_x = sb("w_x", [P, KB, R + 2 * NS])
        w_all = sb("w_all", [P, KB, P])
        w_dt = sb("w_dt", [R, CH])
        w_out = sb("w_out", [P, KB, DM])
        chan = sb("chan", [P, 3, KB])
        decay_rate = sb("decay_rate", [P, KB, NS])
        pick_r = sb("pick_r", [P, NS, P], F32R)
        stats = sb("m_stats", [P, BATCH * TILES, 6])
        moments = sb("m_moments", [P, BATCH * TILES, 2])
        rstd = sb("m_rstd", [P, BATCH * TILES])
        shift = sb("m_shift", [P, BATCH * TILES])
        xn_T = sb("xn_T", [P, BATCH * L])
        u = sb("u", [P, NCHUNK, KB, CHUNK])
        z = sb("z", [P, NCHUNK, KB, CHUNK])
        dt = sb("dt", [P, NCHUNK, KB, CHUNK])
        dtu = sb("dtu", [P, NCHUNK, KB, CHUNK])
        b_split = sb("b_split", [P, NCHUNK, CHUNK], F32R)
        low_c = sb("low_c", [P, CHUNK])
        low = low_c[0:R]
        c_rows = low_c[C_AT:C_AT + NS]
        carry = sb("carry", [P, NS, KB])
        decay = sb("decay", [P, RING, CHUNK])
        state = sb("state", [P, RING, CHUNK])
        drive = sb("drive", [P, RING, CHUNK])
        product = sb("product", [P, RING, CHUNK])
        c_all = sb("c_all", [P, RING, CHUNK])
        xn = decay[:].rearrange("p r (t d) -> p (r t) d", d=DM)
        pick = state[:, 0:2, :].rearrange("p a (s q) -> p (a s) q", q=P)
        w_u = drive[:, 0, 0:CH]
        taps = drive[:, 1, 0:KC * CH].rearrange("p (j c) -> p j c", j=KC)
        c_dram = nc.dram_tensor("c_dram", [NCHUNK, NS, CHUNK], F32, kind="Internal").ap()

        x_loaded = [sem(f"x_loaded{g}") for g in range(BATCH * NCHUNK)]
        u_weights = sem("u_weights")
        w_loaded = sem("w_loaded")
        constants = sem("m_constants")
        taps_ready = sem("taps_ready")
        w_all_ready = sem("w_all_ready")
        rate_exp = sem("rate_exp")
        rate_ready = sem("rate_ready")
        dve_chain = sem("m_dve_chain")
        variance = sem("variance")
        std_done = sem("std_done")
        normed = sem("normed")
        turned = sem("turned")
        xnT_ready = sem("xnT_ready")
        u_summed = sem("u_summed")
        u_ready = sem("u_ready")
        z_summed = sem("z_summed")
        z_ready = sem("z_ready")
        mixed_summed = sem("mixed_summed")
        low_ready = sem("low_ready")
        c_taken = sem("c_taken")
        c_stored = sem("c_stored")
        b_high = sem("b_high")
        b_ready = sem("b_ready")
        v_summed = sem("v_summed")
        v_ready = sem("v_ready")
        clamped = sem("clamped")
        dt_exp = sem("dt_exp")
        dt_log = sem("dt_log")
        dt_ready = sem("dt_ready")
        dtu_ready = sem("dtu_ready")
        b_bcast = sem("b_bcast")
        c_loaded = [sem(f"c_loaded{r}") for r in range(RING)]
        decay_ready = sem("decay_ready")
        drive_ready = sem("drive_ready")
        scanned = sem("scanned")
        carried = sem("carried")
        product_ready = sem("product_ready")
        summed = sem("summed")
        y_read = sem("y_read")
        gated = sem("gated")
        projected = sem("projected")
        added = sem("added")

        block = ctx.enter_context(nc.Block())

        def pieces(with_out):
            blocks = [(k, t) for k in range(KB) for t in range(TB)]
            order = [(("u", k, t), KC) for k, t in blocks]
            order += [(("mixed", t), KB) for t in range(TB)]
            if with_out:
                order += [(("out", t), 2) for t in range(TB)]
            order += [(("v", k, t), 1) for k, t in blocks]
            order += [(("z", k, t), 1) for k, t in blocks]
            return order

        FIRST = sorted(pieces(False), key=lambda p: ("u", "z", "mixed", "v").index(p[0][0]))
        assert FIRST[0][0] == ("u", 0, 0) and len(FIRST) % 2 == 0

        UNITS = [2, 3, 3, 3, 3, 2, 2, 2, 2, 2, 2, 2, 1, 1, 1, 1]
        due, unit_due = {}, {}
        at_state = [s for s, count in enumerate(UNITS) for _ in range(count)]
        for piece, cost in pieces(True):
            for i in range(cost):
                due[piece] = unit_due[piece, i] = at_state[len(unit_due)]
        V_DUE = due["v", KB - 1, TB - 1]
        SOFTEN, RAISE = 2, 2
        EARLY = CHUNK // BANK + 1
        LAG = 3

        def next_chunk(b, c):
            if c == 0:
                return NCHUNK * b + 1, 1, L * b + CHUNK
            return NCHUNK * b + NCHUNK, 0, b * -L + (BATCH - 1) * L

        def after_scan(b, n):
            return STEPS * b + (n + 1 + RING)

        @block.sync
        def _(sp):
            for g in range(BATCH * NCHUNK):
                b, c = divmod(g, NCHUNK)
                sp.dma_start(X[:, g * CT:(g + 1) * CT, :],
                             x[b, c * CHUNK:(c + 1) * CHUNK].rearrange("(i p) d -> p i d", p=P)
                             ).then_inc(x_loaded[g], 16)
            for out, source in ((w_x[:], W_x.rearrange("(k p) n -> p k n", p=P)),
                                (w_dt[:], W_dt),
                                (w_out[:], W_out.rearrange("(k p) n -> p k n", p=P)),
                                (decay_rate[:], A_log.rearrange("(k p) s -> p k s", p=P))):
                sp.dma_start(out, source).then_inc(w_loaded, 16)
            with nc.allow_non_contiguous_dma(reason="a few scalars of each channel"):
                for n, source in enumerate((conv_b, D, b_dt)):
                    sp.dma_start(chan[:, n, :], source.rearrange("(k p) -> p k", p=P)
                                 ).then_inc(w_loaded, 16)

            def load_c(q):
                c, s = divmod(q % (NCHUNK * NS), NS)
                sp.dma_start(c_all[:, q % RING, :], c_dram[c, s:s + 1, :].broadcast_to([P, CHUNK])
                             ).then_inc(c_loaded[q % RING], 16)

            sp.wait_ge(c_stored, 16)
            for q in range(RING):
                load_c(q)
            with sp.Fori(0, BATCH) as b:
                for q in range(NCHUNK * NS):
                    sp.wait_ge(product_ready, STEPS * b + KB * (q + 1))
                    load_c(q + RING)
            for r in range(RING):
                sp.wait_ge(c_loaded[r], 16 * (NCHUNK * NS // RING * BATCH + 1))
            sp.wait_ge(c_stored, 16 * (NCHUNK * BATCH + 1))

        @block.gpsimd
        def _(pool):
            pool.memset(w_all[:], 0.0).then_inc(constants, 1)
            pool.memset(pick, 0.0).then_inc(constants, 1)
            for n, base in enumerate((-B_AT, -LOW_AT)):
                pool.wait_ge(constants, 2 + n)
                pool.affine_select(out=pick, in_=pick, compare_op=ALU.not_equal, fill=1.0,
                                   base=base, pattern=[[-1, NS], [0, P]],
                                   channel_multiplier=1).then_inc(constants, 1)
            pool.wait_ge(u_weights, 16 * 3)
            for j in range(KC):
                pool.tensor_tensor(w_tap[:, j, :], w_u, taps[:, j, :], ALU.mult).then_inc(taps_ready, 1)
            pool.wait_ge(constants, 4)
            pool.wait_ge(taps_ready, KC)
            pool.tensor_copy(pick_r[B_AT:P], pick[B_AT:P]).then_inc(constants, 1)

            pool.wait_ge(constants, 5)

            def dt_times_u(pre, buf, k):
                pool.wait_ge(dt_ready, KB * pre + k + 1)
                pool.wait_ge(u_ready, KB * TB * pre + TB * (k + 1))
                pool.tensor_tensor(dtu[:, buf, k, :], dt[:, buf, k, :], u[:, buf, k, :],
                                   ALU.mult).then_inc(dtu_ready, 1)

            for k in range(KB):
                dt_times_u(0, 0, k)
            with pool.Fori(0, BATCH) as b:
                for n in range(STEPS):
                    q, k = divmod(n, KB)
                    c, s = divmod(q, NS)
                    if s == V_DUE + RAISE + 1:
                        pre, buf, _ = next_chunk(b, c)
                        dt_times_u(pre, buf, k)
                    if k == 1 and (q + RING) % NS == 0:
                        pool.wait_ge(c_stored, 16 * (NCHUNK * b + (q + RING) // NS + 1))
                    if k == 0:
                        pool.wait_ge(c_loaded[q % RING],
                                     16 * (NCHUNK * NS // RING * b + q // RING + 1))
                    pool.wait_ge(scanned, after_scan(b, n))
                    if n >= RING:
                        pool.wait_ge(summed, STEPS * b + n - RING + 1)
                    pool.tensor_tensor(product[:, n % RING, :], state[:, n % RING, :],
                                       c_all[:, q % RING, :], ALU.mult).then_inc(product_ready, 1)

        @block.scalar
        def _(act):
            act.dma_start(w_u, W_in[:, 0:CH]).then_inc(u_weights, 16)
            act.dma_start(w_z[:], W_in[:, CH:2 * CH]).then_inc(u_weights, 16)
            act.dma_start(taps, conv_w.rearrange("j o c -> o j c").broadcast_to([P, KC, CH])
                          ).then_inc(u_weights, 16)

            def std(g):
                act.wait_ge(variance, g + 1)
                part = rstd[:, g * CT:(g + 1) * CT]
                act.activation(part, part, ACT.Sqrt).then_inc(std_done, 1)

            def take_turned(g):
                act.wait_ge(turned, g + 1)
                act.copy(xn_T[:, g * BANK:(g + 1) * BANK], psum[:, g % 4, :]).then_inc(xnT_ready, 1)

            def take(piece, number, pre, buf):
                bank = psum[:, PIECE + number % 2, :]
                kind, index = piece[0], piece[1:]
                span = slice(index[-1] * BANK, (index[-1] + 1) * BANK)
                i = index[0] * TB + index[1] if len(index) == 2 else index[0]
                if kind == "u":
                    act.wait_ge(u_summed, KB * TB * pre + i + 1)
                    act.activation(u[:, buf, index[0], span], bank, ACT.Silu,
                                   bias=chan[:, 0, index[0]:index[0] + 1]).then_inc(u_ready, 1)
                elif kind == "z":
                    act.wait_ge(z_summed, KB * TB * pre + i + 1)
                    act.activation(z[:, buf, index[0], span], bank, ACT.Silu).then_inc(z_ready, 1)
                elif kind == "v":
                    act.wait_ge(v_summed, KB * TB * pre + i + 1)
                    act.activation(dtu[:, buf, index[0], span], bank, ACT.Identity,
                                   bias=chan[:, 2, index[0]:index[0] + 1]).then_inc(v_ready, 1)
                elif kind == "mixed":
                    act.wait_ge(mixed_summed, TB * pre + i + 1)
                    act.copy(low[:, span], bank[0:R]).then_inc(low_ready, 1)
                    act.copy(b_split[B_AT:B_AT + 32, buf, span], bank[B_AT:B_AT + 32]).then_inc(b_high, 1)
                    act.copy(c_rows[:, span], bank[C_AT:C_AT + NS]).then_inc(c_taken, 1)

            def store_c(pre, buf):
                act.wait_ge(c_taken, TB * (pre + 1))
                act.dma_start(c_dram[buf], c_rows).then_inc(c_stored, 16)

            def soften(pre, buf):
                for k in range(KB):
                    act.wait_ge(clamped, KB * pre + k + 1)
                    act.activation(dt[:, buf, k, :], dt[:, buf, k, :], ACT.Exp).then_inc(dt_exp, 1)
                for k in range(KB):
                    act.wait_ge(dt_exp, KB * pre + k + 1)
                    act.activation(dt[:, buf, k, :], dt[:, buf, k, :], ACT.Ln,
                                   bias=1.0).then_inc(dt_log, 1)

            act.wait_ge(w_loaded, 16 * 7)
            act.activation(decay_rate[:], decay_rate[:], ACT.Exp).then_inc(rate_exp, 1)
            std(0)
            take_turned(0)
            take_turned(1)
            std(1)
            take_turned(2)
            std(2)
            std(3)
            for number, (piece, _) in enumerate(FIRST):
                take(piece, number, 0, 0)
                if piece == ("mixed", TB - 1):
                    store_c(0, 0)
            soften(0, 0)

            with act.Fori(0, BATCH) as b:
                act.wait_ge(rate_ready, 1)
                for n in range(STEPS):
                    q, k = divmod(n, KB)
                    c, s = divmod(q, NS)
                    pre, buf, _ = next_chunk(b, c)
                    if s == 0 and k == 0:
                        act.wait_ge(dt_ready, KB * (NCHUNK * b + c + 1))
                    act.wait_ge(scanned, after_scan(b, n - RING))
                    if RING <= n < NS * KB + RING:
                        last_q, last_k = divmod(n - RING, KB)
                        act.copy(carry[:, last_q, last_k:last_k + 1],
                                 state[:, n % RING, CHUNK - 1:CHUNK]).then_inc(carried, 1)
                    act.activation(decay[:, n % RING, :], dt[:, c, k, :], ACT.Exp,
                                   scale=decay_rate[:, k, s:s + 1]).then_inc(decay_ready, 1)
                    if k == 1:
                        for number, (piece, _) in enumerate(pieces(c > 0)):
                            at = due[piece]
                            if piece[0] == "z":
                                at = due[piece[0], piece[1], TB - 1]
                            if at != s:
                                continue
                            if piece[0] == "u" and c and piece[1] == 0:
                                act.wait_ge(gated, KB * (NCHUNK * b + c))
                            if piece == ("mixed", 0):
                                act.wait_ge(c_stored, 16 * pre)
                            if piece[0] == "z" and c and piece[1:] == (0, 0):
                                act.wait_ge(projected, TB * (NCHUNK * b + c))
                            take(piece, number, pre, buf)
                            if piece == ("mixed", TB - 1):
                                store_c(pre, buf)
                        if s == V_DUE + SOFTEN:
                            soften(pre, buf)

        @block.vector
        def _(dve):
            at = 0

            def token_stats(g, at):
                dve.wait_ge(x_loaded[g], 16)
                tiles = slice(g * CT, (g + 1) * CT)
                at = layer_norm_constants(dve, dve_chain, at, stats[:, tiles, :], moments[:, tiles, :],
                                          lambda i: X[:, g * CT + i, :], CT)
                dve.tensor_scalar(rstd[:, tiles], moments[:, tiles, 1], LN_EPS, None,
                                  ALU.add).then_inc(variance, 1)
                return at

            def normalise(g, at):
                tiles = slice(g * CT, (g + 1) * CT)
                dve.wait_ge(std_done, g + 1)
                dve.reciprocal(rstd[:, tiles], rstd[:, tiles]).then_inc(dve_chain, 1)
                dve.wait_ge(dve_chain, at + 1)
                dve.scalar_tensor_tensor(out=shift[:, tiles], in0=moments[:, tiles, 0], scalar=-1.0,
                                         in1=rstd[:, tiles], op0=ALU.mult,
                                         op1=ALU.mult).then_inc(dve_chain, 1)
                dve.wait_ge(dve_chain, at + 2)
                for i in range(g * CT, (g + 1) * CT):
                    dve.tensor_scalar(xn[:, i, :], X[:, i, :], rstd[:, i:i + 1], shift[:, i:i + 1],
                                      ALU.mult, ALU.add).then_inc(normed, 1)
                return at + 2

            def normalise_all(groups, at):
                for g in groups:
                    at = normalise(g, token_stats(g, at))
                return at

            at = normalise_all(range(2), at)
            dve.wait_ge(w_loaded, 16 * 7)
            dve.wait_ge(constants, 1)
            for k in range(KB):
                for first, of, width in ((0, 0, R), (B_AT, R, NS), (C_AT, R + NS, NS)):
                    last = dve.tensor_copy(w_all[:, k, first:first + width], w_x[:, k, of:of + width])
            last.then_inc(w_all_ready, 1)
            normalise_all(range(2, BATCH * NCHUNK), at)
            dve.sem_inc(scanned, RING)
            dve.sem_inc(added, 1)

            def split_b(pre, buf, t):
                span = slice(t * BANK, (t + 1) * BANK)
                number = KB * TB + t
                dve.wait_ge(b_high, TB * pre + t + 1)
                dve.tensor_tensor(b_split[LOW_AT:LOW_AT + 32, buf, span],
                                  psum[B_AT:B_AT + 32, PIECE + number % 2, :],
                                  b_split[B_AT:B_AT + 32, buf, span].bitcast(F32),
                                  ALU.subtract).then_inc(b_ready, 1)

            def clamp(pre, buf, k):
                dve.wait_ge(v_ready, KB * TB * pre + TB * (k + 1))
                dve.tensor_scalar(dt[:, buf, k, :], dtu[:, buf, k, :], 40.0, None,
                                  ALU.min).then_inc(clamped, 1)

            def raise_dt(pre, buf, k):
                dve.wait_ge(dt_log, KB * pre + k + 1)
                dve.tensor_tensor(dt[:, buf, k, :], dt[:, buf, k, :], dtu[:, buf, k, :],
                                  ALU.max).then_inc(dt_ready, 1)

            for t in range(TB):
                split_b(0, 0, t)
            for k in range(KB):
                clamp(0, 0, k)
            dve.wait_ge(rate_exp, 1)
            dve.tensor_scalar(decay_rate[:], decay_rate[:], -1.0, None, ALU.mult).then_inc(rate_ready, 1)
            for g in range(EARLY, BATCH * L // BANK):
                dve.wait_ge(turned, g + 1)
                dve.tensor_copy(xn_T[:, g * BANK:(g + 1) * BANK], psum[:, g % 4, :]).then_inc(xnT_ready, 1)
            for k in range(KB):
                raise_dt(0, 0, k)

            with dve.Fori(0, BATCH) as b:
                def force(n):
                    q, k = divmod(n, KB)
                    c = q // NS
                    dve.wait_ge(b_bcast, NCHUNK * NS * b + q + 1)
                    if q % NS == 0:
                        dve.wait_ge(dtu_ready, KB * (NCHUNK * b + c) + k + 1)
                    dve.wait_ge(scanned, after_scan(b, n - RING))
                    dve.tensor_tensor(
                        drive[:, n % RING, :].rearrange("p (a t) -> p a t", t=BANK),
                        psum[:, BCAST:BCAST + TB, :],
                        dtu[:, c, k, :].rearrange("p (a t) -> p a t", t=BANK),
                        ALU.mult).then_inc(drive_ready, 1)

                def scan(n):
                    q, k = divmod(n, KB)
                    c, s = divmod(q, NS)
                    dve.wait_ge(decay_ready, STEPS * b + n + 1)
                    dve.wait_ge(drive_ready, STEPS * b + n + 1)
                    if n >= RING:
                        dve.wait_ge(product_ready, STEPS * b + n - RING + 1)
                    if c == 0 and n >= RING:
                        dve.wait_ge(carried, NS * KB * b + n - RING + 1)
                    if c:
                        dve.wait_ge(carried, NS * KB * b + min(NS * KB, max(n - NS * KB, n - RING) + 1))
                    dve.tensor_tensor_scan(state[:, n % RING, :], decay[:, n % RING, :],
                                           drive[:, n % RING, :], carry[:, s, k:k + 1] if c else 0.0,
                                           ALU.mult, ALU.add).then_inc(scanned, 1)

                def gate(c):
                    for k in range(KB):
                        dve.wait_ge(summed, STEPS * b + KB * NS * (c + 1) - KB + k + 1)
                        dve.scalar_tensor_tensor(
                            out=u[:, c, k, :].rearrange("p (a t) -> p a t", t=BANK),
                            in0=u[:, c, k, :].rearrange("p (a t) -> p a t", t=BANK),
                            scalar=chan[:, 1, k:k + 1], in1=psum[:, Y + TB * k:Y + TB * (k + 1), :],
                            op0=ALU.mult, op1=ALU.add).then_inc(y_read, 1)
                    for k in range(KB):
                        dve.wait_ge(y_read, KB * (NCHUNK * b + c) + k + 1)
                        if k == 0:
                            dve.wait_ge(z_ready, KB * TB * (NCHUNK * b + c + 1))
                        dve.tensor_tensor(z[:, c, k, :], u[:, c, k, :], z[:, c, k, :],
                                          ALU.mult).then_inc(gated, 1)

                def add(c, t, number):
                    dve.wait_ge(projected, TB * (NCHUNK * b + c) + t + 1)
                    rows = X[:, bass.ds(TILES * b + CT * c + CT // TB * t, CT // TB), :]
                    dve.tensor_tensor(rows, rows, psum[:, PIECE + number % 2, :].rearrange(
                        "p (t d) -> p t d", d=DM), ALU.add).then_inc(added, 1)

                for k in range(KB):
                    force(k)
                for q in range(NCHUNK * NS):
                    if q + 1 < NCHUNK * NS:
                        for k in range(KB):
                            force(KB * (q + 1) + k)
                    for k in range(KB):
                        scan(KB * q + k)
                    c, s = divmod(q, NS)
                    pre, buf, _ = next_chunk(b, c)
                    if c and s == 1:
                        gate(c - 1)
                    for t in range(TB):
                        if s == due["mixed", t]:
                            split_b(pre, buf, t)
                        if c and s == due["out", t]:
                            add(c - 1, t, KB * TB + TB + t)
                    for k in range(KB):
                        if s == V_DUE - 1 + k:
                            clamp(pre, buf, k)
                    if s == V_DUE + RAISE:
                        for k in range(KB):
                            raise_dt(pre, buf, k)
                gate(NCHUNK - 1)
                for t in range(TB):
                    add(NCHUNK - 1, t, t)

        @block.tensor
        def _(pe):
            def turn(g):
                if g >= 4:
                    pe.wait_ge(xnT_ready, g - 3)
                for i in range(4):
                    pe.wait_ge(normed, 4 * g + i + 1)
                    last = pe.transpose(psum[:, g % 4, i * P:(i + 1) * P], xn[:, 4 * g + i, :], ident[:])
                last.then_inc(turned, 1)

            def wait_read(piece, pre):
                kind, index = piece[0], piece[1:]
                i = index[0] * TB + index[1] if len(index) == 2 else index[0]
                if kind == "u":
                    pe.wait_ge(u_ready, KB * TB * pre + i + 1)
                elif kind == "z":
                    pe.wait_ge(z_ready, KB * TB * pre + i + 1)
                elif kind == "v":
                    pe.wait_ge(v_ready, KB * TB * pre + i + 1)
                elif kind == "mixed":
                    pe.wait_ge(low_ready, TB * pre + i + 1)
                    pe.wait_ge(c_taken, TB * pre + i + 1)
                    pe.wait_ge(b_ready, TB * pre + i + 1)

            def project(bank, chunks, c, t, half):
                out = psum[:, PIECE + bank, :]
                pe.wait_ge(gated, KB * (chunks + c + 1))
                for i in range(2 * half, 2 * half + 2):
                    tile = CT // TB * t + i
                    for k in range(KB):
                        last = pe.matmul(out[:, i * DM:(i + 1) * DM],
                                         z[:, c, k, tile * P:(tile + 1) * P], w_out[:, k, :],
                                         start=(k == 0), stop=(k == KB - 1))
                if half:
                    last.then_inc(projected, 1)

            def unit(piece, number, i, pre, buf, first_token):
                out = psum[:, PIECE + number % 2, :]
                kind, index = piece[0], piece[1:]
                t = index[-1]
                if kind == "u":
                    k = index[0]
                    at_start = buf == 0 and t == 0
                    at_end = buf == NCHUNK - 1 and t == TB - 1
                    j = ((1, 0, 2, 3) if at_start else (1, 2, 3, 0))[i]
                    lo = LEFT - j if at_start and j < LEFT else 0
                    hi = BANK - (j - LEFT) if at_end and j > LEFT else BANK
                    ins = pe.matmul(out[:, lo:hi], w_tap[:, j, k * P:(k + 1) * P],
                                    xn_T[:, bass.ds(first_token + (t * BANK + lo + j - LEFT), hi - lo)],
                                    start=(i == 0), stop=(i == KC - 1))
                    if i == KC - 1:
                        ins.then_inc(u_summed, 1)
                elif kind == "z":
                    pe.matmul(out, w_z[:, index[0] * P:(index[0] + 1) * P],
                              xn_T[:, bass.ds(first_token + t * BANK, BANK)], start=True,
                              stop=True).then_inc(z_summed, 1)
                elif kind == "mixed":
                    pe.wait_ge(u_ready, KB * TB * pre + TB * i + t + 1)
                    ins = pe.matmul(out, w_all[:, i, :], u[:, buf, i, t * BANK:(t + 1) * BANK],
                                    start=(i == 0), stop=(i == KB - 1))
                    if i == KB - 1:
                        ins.then_inc(mixed_summed, 1)
                elif kind == "v":
                    pe.wait_ge(low_ready, TB * pre + t + 1)
                    pe.matmul(out, w_dt[:, index[0] * P:(index[0] + 1) * P],
                              low[:, t * BANK:(t + 1) * BANK], start=True,
                              stop=True).then_inc(v_summed, 1)

            for g in range(EARLY):
                turn(g)
            pe.wait_ge(taps_ready, KC)
            pe.wait_ge(w_loaded, 16 * 7)
            for number, (piece, cost) in enumerate(FIRST):
                if number >= 2:
                    wait_read(FIRST[number - 2][0], 0)
                if piece[0] == "u":
                    pe.wait_ge(xnT_ready, piece[2] + 2)
                if piece[0] == "mixed":
                    pe.wait_ge(w_all_ready, 1)
                    pe.wait_ge(constants, 5)
                for i in range(cost):
                    unit(piece, number, i, 0, 0, 0)
            for g in range(EARLY, BATCH * L // BANK):
                turn(g)

            with pe.Fori(0, BATCH) as b:
                def sum_state(q, k):
                    c, s = divmod(q, NS)
                    n = KB * q + k
                    if s == 0 and c:
                        pe.wait_ge(y_read, KB * (NCHUNK * b + c - 1) + k + 1)
                    pe.wait_ge(product_ready, STEPS * b + n + 1)
                    for h in range(TB):
                        last = pe.matmul(psum[:, Y + TB * k + h, :], ident[:],
                                         product[:, n % RING, h * BANK:(h + 1) * BANK],
                                         start=(s == 0), stop=(s == NS - 1))
                    last.then_inc(summed, 1)

                def prepare(c, s, half):
                    pre, buf, first_token = next_chunk(b, c)
                    mine = [(number, piece, i) for number, (piece, cost) in enumerate(pieces(c > 0))
                            for i in range(cost) if unit_due[piece, i] == s]
                    cut = (len(mine) + 1) // 2
                    for number, piece, i in mine[cut:] if half else mine[:cut]:
                        if i == 0 and number >= 2:
                            before = pieces(c > 0)[number - 2][0]
                            if before[0] == "out":
                                pe.wait_ge(added, TB * (NCHUNK * b + c - 1) + before[1] + 2)
                            else:
                                wait_read(before, pre)
                        elif i == 0:
                            wait_read(("z", KB - 1, number), pre - 1)
                            if c == 0:
                                pe.wait_ge(added, TB * NCHUNK * b + 1)
                        if piece[0] == "out":
                            project(number % 2, NCHUNK * b, c - 1, piece[1], i)
                        else:
                            unit(piece, number, i, pre, buf, first_token)

                pe.wait_ge(xnT_ready, BATCH * L // BANK)
                for q in range(NCHUNK * NS + LAG):
                    if q < NCHUNK * NS:
                        c, s = divmod(q, NS)
                        if q:
                            pe.wait_ge(drive_ready, STEPS * b + KB * q)
                        if s == 0:
                            pe.wait_ge(b_ready, TB * (NCHUNK * b + c + 1))
                        for h in range(TB):
                            last = pe.matmul(psum[:, BCAST + h, :], pick_r[B_AT:P, s, :],
                                             b_split[B_AT:P, c, h * BANK:(h + 1) * BANK],
                                             start=True, stop=True)
                        last.then_inc(b_bcast, 1)
                    for k in range(KB):
                        if q >= LAG:
                            sum_state(q - LAG, k)
                        if q < NCHUNK * NS:
                            prepare(c, s, k)
                for t in range(TB):
                    wait_read(("z", KB - 1, t), NCHUNK * b + NCHUNK)
                    for half in range(2):
                        project(t, NCHUNK * b, NCHUNK - 1, t, half)


def identity(nc, ident):
    with nc.semaphore("ident_zero") as zeroed, nc.Block() as block:
        @block.gpsimd
        def _(pool):
            pool.memset(ident[:], 0.0).then_inc(zeroed, 1)
            pool.wait_ge(zeroed, 1)
            pool.affine_select(out=ident[:], in_=ident[:], compare_op=ALU.not_equal, fill=1.0, base=0,
                               pattern=[[-1, P]], channel_multiplier=1).then_inc(zeroed, 1)
            pool.wait_ge(zeroed, 2)


def moe(nc, X, ident, shared, name, dst, first_use, gate_w, ln_gamma, ln_beta, fc1s, b1s, fc2s, b2s):
    E, FF, DM = fc1s.shape
    TILES = X.shape[1]
    T = TILES * P
    K = T // E
    KT = K // P
    FB = FF // P
    J = P // E
    SPAN = T // J
    HALVES = SPAN // P
    PAIRS = HALVES * P
    ROW = DM + E
    NB = T // BANK
    STEPS = 13
    WAYS = 4
    LO = 32
    HI = K // LO
    FAR = float(4 * K)
    MIDDLE = T // 2
    GROUPS = 2
    assert MIDDLE <= 2048 and HALVES == 2

    dram = lambda what, shape: nc.dram_tensor(f"{name}_{what}", shape, F32, kind="Internal").ap()
    table = dram("table", [T, ROW])
    score_dram = dram("score_dram", [E, T])
    gamma, b1_T, b2_all, gate_T, w1_T, w2_T = (
        shared[key] for key in ("gamma", "b1_T", "b2_all", "gate_T", "w1_T", "w2_T"))

    with ExitStack() as keep:
        tokens = keep.enter_context(nc.sbuf_tensor(f"{name}_tokens", [P, E, KT], I32))

        with nc.cleanup_on_exit(), ExitStack() as ctx:
            def sb(what, shape, dt=F32):
                return ctx.enter_context(nc.sbuf_tensor(f"{name}_{what}", shape, dt))

            def sem(what):
                return nc.alloc_semaphore(f"{name}_{what}")

            psum = ctx.enter_context(nc.psum_tensor(f"{name}_psum1", [P, 8, BANK], F32))
            COUNTS, PLACES, LISTS, SCORES, W_TURN, SMALL = 0, 1, 2, 4, 5, 7
            stats = sb("stats", [P, TILES, 6])
            moments = sb("moments", [P, TILES, 2])
            rstd = sb("rstd", [P, TILES])
            shift = sb("shift", [P, TILES])
            again = sb("again", [P, TILES])
            rstd2 = sb("rstd2", [P, TILES])
            shift2 = sb("shift2", [P, TILES])
            f = sb("f", [P, TILES, DM])
            f_T = sb("f_T", [P, T])
            rows = sb("rows", [P, TILES, ROW])
            score = sb("score", [E, T])
            if first_use:
                gate_raw = sb("gate_raw", [E, DM])
                b1_raw = sb("b1_raw", [E * FB, P])
                w1_raw = sb("w1_raw", [P, E, FB, DM])
                w2_raw = sb("w2_raw", [P, E, FF])
            search = sb("search", [P, SPAN])
            same = sb("same", [P, P])
            before = sb("before", [P, P])
            same_b = sb("same_b", [P, P], BF16)
            before_b = sb("before_b", [P, P], BF16)
            steps = sb("steps", [P, (STEPS + 1) * WAYS])
            bounds = sb("bounds", [P, WAYS])
            following = sb("following", [P, WAYS])
            hits = sb("hits", [P, WAYS - 1, SPAN], BF16)
            count = sb("count", [P, WAYS - 1], BF16)
            passed = sb("passed", [P, WAYS - 1])
            passes = sb("passes", [P, 1])
            ones = sb("ones", [P, SPAN])
            above = sb("above", [P, 2, SPAN])
            rank = sb("rank", [P, 2, SPAN])
            row_count = sb("row_count", [P, 2], BF16)
            offset = sb("offset", [P, 2])
            place = sb("place", [P, SPAN])
            place_T = sb("place_T", [P, PAIRS], I32)
            low_i = sb("low_i", [P, PAIRS], I32)
            high_i = sb("high_i", [P, PAIRS], I32)
            low = sb("low_h", [P, PAIRS], F16)
            high = sb("high_h", [P, PAIRS], F16)
            token_i = sb("token_i", [P, PAIRS], I32)
            token = sb("token", [P, PAIRS], F16)
            one_low = sb("one_low", [P, LO, PAIRS], F16)
            token_high = sb("token_high", [P, HI, PAIRS], F16)

            loaded = sem("loaded")
            w_loaded = sem("w_loaded")
            chain = sem("chain")
            variance = sem("variance")
            std_done = sem("std_done")
            ln_ready = sem("ln_ready")
            variance2 = sem("variance2")
            std2_done = sem("std2_done")
            ln2_ready = sem("ln2_ready")
            f_ready = sem("f_ready")
            base_ready = sem("base_ready")
            rows_ready = sem("rows_ready")
            f_turned = sem("f_turned")
            fT_even = sem("fT_even")
            fT_odd = sem("fT_odd")
            small_turned = sem("small_turned")
            small_ready = sem("small_ready")
            w_turned = sem("w_turned")
            w_taken = sem("w_taken")
            gated = sem("gated")
            tanh_done = sem("tanh_done")
            score_ready = sem("score_ready")
            score_turned = sem("score_turned")
            weights_ready = sem("weights_ready")
            score_stored = sem("score_stored")
            search_loaded = sem("search_loaded")
            stored = sem("stored")
            made = sem("made")
            cast = sem("cast")
            steps_made = sem("steps_made")
            counted = sem("counted")
            totalled = sem("totalled")
            passes_ready = sem("passes_ready")
            following_ready = sem("following_ready")
            moved = sem("moved")
            link = sem("link")
            rowed = sem("rowed")
            offsets = sem("offsets")
            placed = sem("placed")
            place_turned = sem("place_turned")
            split_ready = sem("split_ready")
            one_hot = sem("one_hot")
            listed = sem("listed")
            tokens_ready = sem("tokens_ready")
            block = ctx.enter_context(nc.Block())

            @block.sync
            def _(sp):
                if first_use:
                    sp.dma_start(gate_raw[:], gate_w).then_inc(loaded, 16)
                    sp.dma_start(b1_raw[:], b1s.rearrange("e (q f) -> (e q) f", f=P)).then_inc(loaded, 16)
                    with nc.allow_non_contiguous_dma(reason="one scalar of each channel"):
                        for n, source in enumerate((ln_gamma, ln_beta)):
                            sp.dma_start(gamma[:, n:n + 1],
                                         source.rearrange("(p o) -> p o", o=1)).then_inc(loaded, 16)
                    sp.dma_start(b2_all[:].rearrange("p e d -> p (e d)"),
                                 b2s.rearrange("(o e) d -> o (e d)", o=1).broadcast_to([P, E * DM])
                                 ).then_inc(loaded, 16)
                    sp.dma_start(w1_raw[:].rearrange("p e q d -> p (e q) d"),
                                 fc1s.rearrange("e (q p) d -> p (e q) d", p=P)).then_inc(w_loaded, 16)
                    sp.dma_start(w2_raw[:], fc2s.rearrange("e d f -> d e f")).then_inc(w_loaded, 16)
                sp.wait_ge(score_ready, NB)
                sp.dma_start(score_dram, score[:]).then_inc(score_stored, 16)
                sp.wait_ge(score_stored, 16)
                sp.dma_start(search[:], score_dram.rearrange("e (j t) -> (e j) t", j=J)
                             ).then_inc(search_loaded, 16)
                sp.wait_ge(base_ready, 4)
                sp.dma_start(dst.rearrange("(i p) d -> p i d", p=P), f[:]).then_inc(stored, 16)
                sp.wait_ge(rows_ready, TILES)
                sp.wait_ge(weights_ready, 1)
                sp.dma_start(table.rearrange("(i p) d -> p i d", p=P), rows[:]).then_inc(stored, 16)
                sp.wait_ge(stored, 32)
                if first_use:
                    sp.wait_ge(loaded, 16 * 5)

            @block.gpsimd
            def _(pool):
                for i in range(STEPS):
                    for way in range(WAYS):
                        pool.memset(steps[:, i * WAYS + way:i * WAYS + way + 1], way * 2.0 ** (-1 - 2 * i))
                pool.memset(steps[:, STEPS * WAYS:], 0.0).then_inc(steps_made, 1)
                pool.memset(same[:], 1.0).then_inc(made, 1)
                view = same[:].rearrange("p (e j) -> p e j", j=J)
                pool.wait_ge(made, 1)
                pool.affine_select(out=view, in_=view, compare_op=ALU.is_ge, fill=0.0, base=0,
                                   pattern=[[-J, E], [0, J]], channel_multiplier=1).then_inc(made, 1)
                pool.wait_ge(made, 2)
                pool.affine_select(out=view, in_=view, compare_op=ALU.is_ge, fill=0.0, base=J - 1,
                                   pattern=[[J, E], [0, J]], channel_multiplier=-1).then_inc(made, 1)
                pool.wait_ge(made, 3)
                pool.affine_select(out=before[:], in_=same[:], compare_op=ALU.is_ge, fill=0.0, base=-1,
                                   pattern=[[1, P]], channel_multiplier=-1).then_inc(made, 1)
                pool.memset(ones[:], 1.0).then_inc(made, 1)
                pool.iota(token_i[:], pattern=[[P, HALVES], [0, E], [SPAN, J]], base=-MIDDLE,
                          channel_multiplier=1).then_inc(made, 1)
                pool.wait_ge(made, 6)
                pool.tensor_copy(same_b[:], same[:]).then_inc(cast, 1)
                pool.tensor_copy(before_b[:], before[:]).then_inc(cast, 1)
                pool.tensor_copy(token[:], token_i[:]).then_inc(cast, 1)
                quarter = TILES // 4
                for n in range(4):
                    part = slice(n * quarter, (n + 1) * quarter)
                    pool.wait_ge(f_turned, (n + 1) * quarter // 4)
                    pool.tensor_tensor(f[:, part, :], X[:, part, :], f[:, part, :],
                                       ALU.add).then_inc(base_ready, 1)

            @block.scalar
            def _(act):
                act.wait_ge(variance, 1)
                act.activation(rstd[:], rstd[:], ACT.Sqrt).then_inc(std_done, 1)
                act.wait_ge(variance2, 1)
                act.activation(again[:], again[:], ACT.Sqrt).then_inc(std2_done, 1)
                for g in range(1, NB, 2):
                    act.wait_ge(f_turned, g + 1)
                    act.copy(f_T[:, g * BANK:(g + 1) * BANK], psum[:, g % 4, :]).then_inc(fT_odd, 1)
                for g in range(NB):
                    act.wait_ge(gated, g + 1)
                    act.activation(score[:, g * BANK:(g + 1) * BANK], psum[0:E, SCORES + g % 2, :],
                                   ACT.Tanh).then_inc(tanh_done, 1)
                act.wait_ge(ln2_ready, 2)
                for i in range(TILES):
                    act.activation(rows[:, i, 0:DM], X[:, i, :], ACT.Identity, bias=shift2[:, i:i + 1],
                                   scale=rstd2[:, i:i + 1]).then_inc(rows_ready, 1)
                    if first_use and i % 2:
                        n = i // 2
                        e, layer = divmod(n, 2)
                        act.wait_ge(w_turned, n + 1)
                        where = w2_T[:, e].rearrange("p q d -> p (q d)") if layer else w1_T[:, e, :]
                        act.copy(where, psum[:, W_TURN + n % 2, :]).then_inc(w_taken, 1)

            @block.vector
            def _(dve):
                at = layer_norm_constants(dve, chain, 0, stats, moments, lambda i: X[:, i, :], TILES)
                dve.tensor_scalar(rstd[:], moments[:, :, 1], LN_EPS, None, ALU.add).then_inc(variance, 1)
                dve.wait_ge(std_done, 1)
                dve.reciprocal(rstd[:], rstd[:]).then_inc(ln_ready, 1)
                dve.wait_ge(ln_ready, 1)
                dve.scalar_tensor_tensor(out=shift[:], in0=moments[:, :, 0], scalar=-1.0, in1=rstd[:],
                                         op0=ALU.mult, op1=ALU.mult).then_inc(ln_ready, 1)
                dve.tensor_tensor(again[:], rstd[:], rstd[:], ALU.mult).then_inc(chain, 1)
                dve.wait_ge(chain, at + 1)
                dve.tensor_tensor(again[:], again[:], moments[:, :, 1], ALU.mult).then_inc(chain, 1)
                dve.wait_ge(chain, at + 2)
                dve.tensor_scalar(again[:], again[:], LN_EPS, None, ALU.add).then_inc(variance2, 1)
                dve.wait_ge(ln_ready, 2)
                for i in range(TILES):
                    dve.tensor_scalar(f[:, i, :], X[:, i, :], rstd[:, i:i + 1], shift[:, i:i + 1],
                                      ALU.mult, ALU.add).then_inc(f_ready, 1)
                    if i == 3:
                        dve.wait_ge(std2_done, 1)
                        dve.reciprocal(again[:], again[:]).then_inc(chain, 1)
                        dve.wait_ge(chain, at + 3)
                        dve.tensor_tensor(rstd2[:], rstd[:], again[:], ALU.mult).then_inc(ln2_ready, 1)
                        dve.tensor_tensor(shift2[:], shift[:], again[:], ALU.mult).then_inc(ln2_ready, 1)
                if first_use:
                    dve.wait_ge(small_turned, 2)
                    dve.tensor_copy(gate_T[:], psum[:, SMALL, 0:E]).then_inc(small_ready, 1)
                    dve.tensor_copy(b1_T[:], psum[:, SMALL, P:P + E * FB]).then_inc(small_ready, 1)
                for g in range(0, NB, 2):
                    dve.wait_ge(f_turned, g + 1)
                    dve.tensor_copy(f_T[:, g * BANK:(g + 1) * BANK], psum[:, g % 4, :]).then_inc(fT_even, 1)
                for g in range(NB):
                    dve.wait_ge(tanh_done, g + 1)
                    part = score[:, g * BANK:(g + 1) * BANK]
                    dve.tensor_scalar(part, part, 1.0, -1.0, ALU.add, ALU.add).then_inc(score_ready, 1)
                dve.wait_ge(score_turned, TILES)
                dve.tensor_scalar(rows[:, :, DM:ROW],
                                  psum[:, SMALL, 0:TILES * E].rearrange("p (i e) -> p i e", e=E), 1.0, 0.5,
                                  ALU.add, ALU.mult).then_inc(weights_ready, 1)

                dve.wait_ge(steps_made, 1)
                dve.tensor_scalar(bounds[:], steps[:, 0:WAYS], -1.0, None, ALU.add).then_inc(moved, 1)
                dve.wait_ge(search_loaded, 16)
                with dve.Fori(0, STEPS) as i:
                    dve.wait_ge(moved, i + 1)
                    for way in range(1, WAYS):
                        last = dve.tensor_scalar(hits[:, way - 1, :], search[:], bounds[:, way:way + 1],
                                                 None, ALU.is_ge, ALU.add,
                                                 accum_out=count[:, way - 1:way])
                    last.then_inc(counted, 1)
                    dve.tensor_scalar(following[:], steps[:, bass.ds(WAYS * i + WAYS, WAYS)],
                                      bounds[:, 0:1], None, ALU.add).then_inc(following_ready, 1)
                    dve.wait_ge(totalled, i + 1)
                    dve.tensor_scalar(passed[:], psum[:, COUNTS, 0:WAYS - 1], K - 0.5, None, ALU.is_ge,
                                      ALU.add, accum_out=passes[:]).then_inc(passes_ready, 1)
                    dve.wait_ge(passes_ready, i + 1)
                    dve.wait_ge(following_ready, i + 1)
                    dve.scalar_tensor_tensor(out=bounds[:], in0=passes[:].broadcast_to([P, WAYS]),
                                             scalar=steps[:, bass.ds(WAYS * i + 1, 1)],
                                             in1=following[:], op0=ALU.mult,
                                             op1=ALU.add).then_inc(moved, 1)
                dve.wait_ge(moved, STEPS + 1)

                dve.tensor_scalar(above[:, 0, :], search[:], bounds[:, 0:1], None,
                                  ALU.is_gt).then_inc(link, 1)
                dve.tensor_scalar(above[:, 1, :], search[:], bounds[:, 0:1], None,
                                  ALU.is_equal).then_inc(link, 1)
                dve.wait_ge(cast, 3)
                for n in range(2):
                    dve.wait_ge(link, n + 1)
                    dve.tensor_tensor_scan(rank[:, n, :], ones[:], above[:, n, :], 0.0, ALU.mult,
                                           ALU.add).then_inc(link, 1)
                dve.wait_ge(link, 4)
                dve.tensor_copy(row_count[:], rank[:, :, SPAN - 1]).then_inc(rowed, 1)
                dve.wait_ge(offsets, 1)
                dve.tensor_scalar(offset[:], psum[:, COUNTS, 8:10], -1.0 - FAR, None,
                                  ALU.add).then_inc(link, 1)
                dve.wait_ge(link, 5)
                dve.tensor_tensor(offset[:, 1:2], offset[:, 1:2], psum[:, COUNTS, 16:17],
                                  ALU.add).then_inc(link, 1)
                dve.wait_ge(link, 6)
                for n in range(2):
                    dve.scalar_tensor_tensor(out=rank[:, n, :], in0=rank[:, n, :],
                                             scalar=offset[:, n:n + 1], in1=above[:, n, :],
                                             op0=ALU.add, op1=ALU.mult).then_inc(link, 1)
                dve.wait_ge(link, 8)
                dve.scalar_tensor_tensor(out=place[:], in0=rank[:, 0, :], scalar=FAR, in1=rank[:, 1, :],
                                         op0=ALU.add, op1=ALU.add).then_inc(placed, 1)
                dve.wait_ge(place_turned, 1)
                dve.tensor_copy(place_T[:], psum[:, PLACES, 0:PAIRS]).then_inc(link, 1)
                dve.wait_ge(link, 9)
                dve.tensor_scalar(high_i[:], place_T[:], LO.bit_length() - 1, None,
                                  ALU.logical_shift_right).then_inc(link, 1)
                dve.tensor_scalar(low_i[:], place_T[:], LO - 1, None, ALU.bitwise_and).then_inc(link, 1)
                dve.wait_ge(link, 10)
                dve.tensor_copy(high[:], high_i[:]).then_inc(split_ready, 1)
                dve.wait_ge(link, 11)
                dve.tensor_copy(low[:], low_i[:]).then_inc(split_ready, 1)
                dve.wait_ge(split_ready, 2)
                for group in range(GROUPS):
                    def pairs_of(tile, *index):
                        view = tile[(slice(None), *index, slice(None))]
                        return view.rearrange("p (h m) -> p h m", h=HALVES)[
                            :, :, group * P // GROUPS:(group + 1) * P // GROUPS]

                    for h in range(HI):
                        dve.scalar_tensor_tensor(out=pairs_of(token_high, h), in0=pairs_of(high),
                                                 scalar=float(h), in1=pairs_of(token),
                                                 op0=ALU.is_equal, op1=ALU.mult)
                    for n in range(LO):
                        last = dve.tensor_scalar(pairs_of(one_low, n), pairs_of(low), float(n), None,
                                                 ALU.is_equal)
                    last.then_inc(one_hot, 1)
                for group in range(GROUPS):
                    dve.wait_ge(listed, group + 1)
                    experts = slice(group * E // GROUPS, (group + 1) * E // GROUPS)
                    lists = psum[0:LO, LISTS + group, 0:E // GROUPS * HI].rearrange(
                        "p (e h) -> p e h", h=HI)
                    for q in range(P // LO):
                        dve.tensor_scalar(tokens[q * LO:(q + 1) * LO, experts, :],
                                          lists[:, :, q:HI:P // LO], float(MIDDLE), None,
                                          ALU.add).then_inc(tokens_ready, 1)
                dve.wait_ge(tokens_ready, GROUPS * P // LO)

            @block.tensor
            def _(pe):
                def turn_weights(n):
                    e, layer = divmod(n, 2)
                    if n >= 2:
                        pe.wait_ge(w_taken, n - 1)
                    for q in range(FB):
                        raw = w2_raw[:, e, q * P:(q + 1) * P] if layer else w1_raw[:, e, q, :]
                        last = pe.transpose(psum[:, W_TURN + n % 2, q * P:(q + 1) * P], raw, ident[:])
                    last.then_inc(w_turned, 1)

                if first_use:
                    pe.wait_ge(loaded, 16 * 5)
                    pe.transpose(psum[:, SMALL, 0:E], gate_raw[:], ident[0:E, 0:E]
                                 ).then_inc(small_turned, 1)
                    pe.transpose(psum[:, SMALL, P:P + E * FB], b1_raw[:],
                                 ident[0:E * FB, 0:E * FB]).then_inc(small_turned, 1)
                for g in range(NB):
                    if g >= 4:
                        pe.wait_ge(fT_even if g % 2 == 0 else fT_odd, (g - 4) // 2 + 1)
                    for i in range(4):
                        pe.wait_ge(f_ready, 4 * g + i + 1)
                        last = pe.transpose(psum[:, g % 4, i * P:(i + 1) * P], f[:, 4 * g + i, :], ident[:])
                    last.then_inc(f_turned, 1)
                if first_use:
                    pe.wait_ge(small_ready, 2)
                for g in range(NB):
                    pe.wait_ge(fT_even if g % 2 == 0 else fT_odd, g // 2 + 1)
                    if g >= 2:
                        pe.wait_ge(tanh_done, g - 1)
                    pe.matmul(psum[0:E, SCORES + g % 2, :], gate_T[:], f_T[:, g * BANK:(g + 1) * BANK],
                              start=True, stop=True).then_inc(gated, 1)
                for i in range(TILES):
                    pe.wait_ge(score_ready, i // 4 + 1)
                    last = pe.transpose(psum[:, SMALL, i * E:(i + 1) * E], score[:, i * P:(i + 1) * P],
                                        ident[0:E, 0:E])
                    last.then_inc(score_turned, 1)
                pe.wait_ge(cast, 3)

                def total(i):
                    pe.wait_ge(counted, i + 1)
                    pe.matmul(psum[:, COUNTS, 0:WAYS - 1], same_b[:], count[:], start=True,
                              stop=True).then_inc(totalled, 1)

                if first_use:
                    pe.wait_ge(w_loaded, 32)
                    for n in range(2 * E - STEPS):
                        turn_weights(n)
                    for i in range(STEPS):
                        total(i)
                        turn_weights(2 * E - STEPS + i)
                else:
                    with pe.Fori(0, STEPS) as i:
                        total(i)
                pe.wait_ge(rowed, 1)
                pe.matmul(psum[:, COUNTS, 8:10], before_b[:], row_count[:], start=True, stop=True)
                pe.matmul(psum[:, COUNTS, 16:17], same_b[:], row_count[:, 0:1], start=True,
                          stop=True).then_inc(offsets, 1)
                pe.wait_ge(placed, 1)
                for h in range(HALVES):
                    last = pe.transpose(psum[:, PLACES, h * P:(h + 1) * P], place[:, h * P:(h + 1) * P],
                                        ident[:])
                last.then_inc(place_turned, 1)
                for group in range(GROUPS):
                    pe.wait_ge(one_hot, group + 1)
                    for n in range(E // GROUPS):
                        e = group * E // GROUPS + n
                        pairs = [h * P + e * J + j for h in range(HALVES) for j in range(J)]
                        for pair in pairs:
                            last = pe.matmul(psum[0:LO, LISTS + group, n * HI:(n + 1) * HI],
                                             one_low[:, :, pair], token_high[:, :, pair],
                                             start=(pair == pairs[0]), stop=(pair == pairs[-1]))
                    last.then_inc(listed, 1)

        with nc.cleanup_on_exit(), ExitStack() as ctx:
            def sb(what, shape, dt=F32):
                return ctx.enter_context(nc.sbuf_tensor(f"{name}_{what}", shape, dt))

            def sem(what):
                return nc.alloc_semaphore(f"{name}_{what}")

            psum = ctx.enter_context(nc.psum_tensor(f"{name}_psum3", [P, 8, BANK], F32))
            YT, HID, OUT = 0, 2, 6
            AHEAD = 4
            got = sb("got", [P, AHEAD, KT, ROW])
            y_T = sb("y_T", [P, 2, K])
            hidden = sb("hidden", [P, 2, FB, K])
            o = sb("o", [P, 2, KT, DM])
            gathered = [sem(f"gathered{r}") for r in range(AHEAD)]
            y_turned = sem("y_turned")
            y_ready = sem("y_ready")
            hidden_summed = sem("hidden_summed")
            hidden_ready = sem("hidden_ready")
            o_summed = sem("o_summed")
            o_biased = sem("o_biased")
            o_ready = sem("o_ready")
            o_free = sem("o_free")
            scattered = [sem(f"scattered{r}") for r in range(2)]
            block = ctx.enter_context(nc.Block())
            TWO = E // 2

            @block.gpsimd
            def _(pool):
                def gather(e):
                    for t in range(KT):
                        pool.indirect_dma_start(got[:, e % AHEAD, t, :], None, table,
                                                bass.IndirectOffsetOnAxis(ap=tokens[:, e, t:t + 1], axis=0)
                                                ).then_inc(gathered[e % AHEAD], 16)

                for e in range(AHEAD - 1):
                    gather(e)
                pool.sem_inc(o_free, 2)
                for e in range(E):
                    if e + AHEAD - 1 < E:
                        gather(e + AHEAD - 1)
                    pool.wait_ge(o_ready, e + 1)
                    if e:
                        pool.wait_ge(scattered[(e - 1) % 2], 16 * KT * ((e - 1) // 2 + 1))
                        pool.sem_inc(o_free, 1)
                    for t in range(KT):
                        pool.indirect_dma_start(dst,
                                                bass.IndirectOffsetOnAxis(ap=tokens[:, e, t:t + 1], axis=0),
                                                o[:, e % 2, t, :], None, compute_op=ALU.add
                                                ).then_inc(scattered[e % 2], 16)
                pool.wait_ge(scattered[(E - 1) % 2], 16 * KT * TWO)
                pool.wait_ge(scattered[(E - 2) % 2], 16 * KT * TWO)

            @block.vector
            def _(dve):
                with dve.Fori(0, E // AHEAD) as m:
                    for n in range(AHEAD):
                        r = n % 2
                        dve.wait_ge(o_summed, AHEAD * m + n + 1)
                        dve.wait_ge(o_free, AHEAD * m + n + 1)
                        dve.wait_ge(gathered[n], 16 * KT * (m + 1))
                        dve.tensor_tensor(
                            o[:, r],
                            psum[:, OUT + r, :].rearrange("p (t d) -> p t d", d=DM),
                            b2_all[:, bass.ds(AHEAD * m + n, 1), :].broadcast_to([P, KT, DM]),
                            ALU.add).then_inc(o_biased, 1)
                        dve.wait_ge(o_biased, AHEAD * m + n + 1)
                        for t in range(KT):
                            last = dve.tensor_scalar(o[:, r, t, :], o[:, r, t, :],
                                                     got[:, n, t, bass.ds(DM + AHEAD * m + n, 1)], None,
                                                     ALU.mult)
                        last.then_inc(o_ready, 1)

            @block.scalar
            def _(act):
                with act.Fori(0, TWO) as m:
                    for r in range(2):
                        act.wait_ge(y_turned, 2 * m + r + 1)
                        act.activation(y_T[:, r, :], psum[:, YT + r, :], ACT.Identity, bias=gamma[:, 1:2],
                                       scale=gamma[:, 0:1]).then_inc(y_ready, 1)
                        for q in range(FB):
                            act.wait_ge(hidden_summed, FB * (2 * m + r) + q + 1)
                            act.activation(hidden[:, r, q, :], psum[:, HID + q, :],
                                           ACT.Gelu_apprx_tanh,
                                           bias=b1_T[:, bass.ds(FB * (2 * m + r) + q, 1)]
                                           ).then_inc(hidden_ready, 1)

            @block.tensor
            def _(pe):
                def turn_rows(e):
                    pe.wait_ge(gathered[e % AHEAD], 16 * KT * (e // AHEAD + 1))
                    if e >= 2:
                        pe.wait_ge(y_ready, e - 1)
                    for t in range(KT):
                        last = pe.transpose(psum[:, YT + e % 2, t * P:(t + 1) * P],
                                            got[:, e % AHEAD, t, 0:DM], ident[:])
                    last.then_inc(y_turned, 1)

                turn_rows(0)
                for e in range(E):
                    r = e % 2
                    pe.wait_ge(y_ready, e + 1)
                    for q in range(FB):
                        if e:
                            pe.wait_ge(hidden_ready, FB * (e - 1) + q + 1)
                        pe.matmul(psum[:, HID + q, :], w1_T[:, e, q * P:(q + 1) * P], y_T[:, r, :],
                                  start=True, stop=True).then_inc(hidden_summed, 1)
                    if e + 1 < E:
                        turn_rows(e + 1)
                    if e >= 2:
                        pe.wait_ge(o_biased, e - 1)
                    pe.wait_ge(hidden_ready, FB * (e + 1))
                    for t in range(KT):
                        for q in range(FB):
                            last = pe.matmul(psum[:, OUT + r, t * DM:(t + 1) * DM],
                                             hidden[:, r, q, t * P:(t + 1) * P], w2_T[:, e, q, :],
                                             start=(q == 0), stop=(q == FB - 1))
                    last.then_inc(o_summed, 1)


def attention(nc, X, ident, source, wq, wk, wv, wo):
    HD, DM = wq.shape
    BATCH = 2
    TILES = X.shape[1]
    TB = TILES // BATCH
    T = TILES * P
    NB = T // BANK
    SCALE = (3.0 / HD) ** 0.5
    with nc.cleanup_on_exit(), ExitStack() as ctx:
        def sb(what, shape, dt=F32):
            return ctx.enter_context(nc.sbuf_tensor(f"a_{what}", shape, dt))

        def sem(what):
            return nc.alloc_semaphore(f"a_{what}")

        psum = ctx.enter_context(nc.psum_tensor("a_psum", [P, 8, BANK], F32))
        stats = sb("stats", [P, TILES, 6])
        moments = sb("moments", [P, TILES, 2])
        rstd = sb("rstd", [P, TILES])
        shift = sb("shift", [P, TILES])
        f = sb("f", [P, TILES, DM])
        f_T = sb("f_T", [P, T])
        q_w = sb("q_w", [HD, DM])
        kv_w = sb("kv_w", [HD, 2, DM])
        o_w = sb("o_w", [DM, HD])
        kv_T = sb("kv_T", [P, 2, HD])
        o_T = sb("o_T", [HD, DM])
        gram = sb("gram", [P, BATCH, DM])
        gv = sb("gv", [P, BATCH, HD])
        energy_T = sb("energy_T", [HD, BATCH, HD])
        eo = sb("eo", [HD, BATCH, DM])
        mix = sb("mix", [P, BATCH, DM])

        x_loaded = [sem(f"x_loaded{n}") for n in range(4)]
        loaded = sem("loaded")
        chain = sem("chain")
        variance = sem("variance")
        std_done = sem("std_done")
        ln_ready = sem("ln_ready")
        f_ready = sem("f_ready")
        turned = sem("turned")
        fT_ready = sem("fT_ready")
        small_turned = sem("small_turned")
        small_ready = sem("small_ready")
        gram_summed = sem("gram_summed")
        link = sem("link")
        linked = sem("linked")
        out_ready = sem("out_ready")
        added = sem("added")
        block = ctx.enter_context(nc.Block())
        QT = TILES // 4

        @block.sync
        def _(sp):
            for n in range(4):
                sp.dma_start(X[:, n * QT:(n + 1) * QT, :],
                             source[n * QT * P:(n + 1) * QT * P, :].rearrange("(i p) d -> p i d", p=P)
                             ).then_inc(x_loaded[n], 16)
            for out, what in ((q_w[:], wq), (kv_w[:, 0, :], wk), (kv_w[:, 1, :], wv), (o_w[:], wo)):
                sp.dma_start(out, what).then_inc(loaded, 16)

        @block.vector
        def _(dve):
            for i in range(TILES):
                if i % QT == 0:
                    dve.wait_ge(x_loaded[i // QT], 16)
                dve.bn_stats(stats[:, i, :], X[:, i, :]).then_inc(chain, 1)
            dve.wait_ge(chain, TILES)
            for i in range(TILES):
                dve.bn_aggr(moments[:, i, :], stats[:, i, :]).then_inc(chain, 1)
            dve.wait_ge(chain, 2 * TILES)
            dve.tensor_scalar(rstd[:], moments[:, :, 1], LN_EPS, None, ALU.add).then_inc(variance, 1)
            dve.wait_ge(std_done, 1)
            dve.reciprocal(rstd[:], rstd[:]).then_inc(ln_ready, 1)
            dve.wait_ge(ln_ready, 1)
            dve.scalar_tensor_tensor(out=shift[:], in0=moments[:, :, 0], scalar=-1.0, in1=rstd[:],
                                     op0=ALU.mult, op1=ALU.mult).then_inc(ln_ready, 1)
            dve.wait_ge(ln_ready, 2)
            for i in range(TILES):
                dve.tensor_scalar(f[:, i, :], X[:, i, :], rstd[:, i:i + 1], shift[:, i:i + 1],
                                  ALU.mult, ALU.add).then_inc(f_ready, 1)
            dve.wait_ge(small_turned, 3)
            dve.tensor_copy(kv_T[:], psum[:, 7, 0:2 * HD].rearrange("p (a h) -> p a h", a=2)
                            ).then_inc(small_ready, 1)
            dve.tensor_copy(o_T[:], psum[0:HD, 7, 2 * HD:2 * HD + DM]).then_inc(small_ready, 1)
            n = 0
            for b in range(BATCH):
                dve.wait_ge(gram_summed, b + 1)
                dve.tensor_copy(gram[:, b, :], psum[:, 4 + b, 0:DM]).then_inc(linked, 1)
                for where in (gv[:, b, :], energy_T[:, b, :], eo[:, b, :], mix[:, b, :]):
                    rows, width = where.shape
                    dve.wait_ge(link, n + 1)
                    if n % 4 == 2:
                        dve.tensor_scalar(where, psum[0:rows, 6, 0:width], SCALE, None,
                                          ALU.mult).then_inc(linked, 1)
                    else:
                        dve.tensor_copy(where, psum[0:rows, 6, 0:width]).then_inc(linked, 1)
                    n += 1
            for g in range(NB):
                dve.wait_ge(out_ready, g + 1)
                rows = X[:, 4 * g:4 * g + 4, :].rearrange("p i d -> p (i d)")
                dve.tensor_tensor(rows, rows, psum[:, g % 4, :], ALU.add).then_inc(added, 1)

        @block.scalar
        def _(act):
            act.wait_ge(variance, 1)
            act.activation(rstd[:], rstd[:], ACT.Sqrt).then_inc(std_done, 1)
            for g in range(NB):
                act.wait_ge(turned, g + 1)
                act.copy(f_T[:, g * BANK:(g + 1) * BANK], psum[:, g % 4, :]).then_inc(fT_ready, 1)

        @block.tensor
        def _(pe):
            pe.wait_ge(loaded, 16 * 4)
            for n in range(2):
                pe.transpose(psum[:, 7, n * HD:(n + 1) * HD], kv_w[:, n, :],
                             ident[0:HD, 0:HD]).then_inc(small_turned, 1)
            pe.transpose(psum[0:HD, 7, 2 * HD:2 * HD + DM], o_w[:], ident[:]).then_inc(small_turned, 1)
            for g in range(NB):
                if g >= 4:
                    pe.wait_ge(fT_ready, g - 3)
                for i in range(4):
                    tile = 4 * g + i
                    pe.wait_ge(f_ready, tile + 1)
                    last = pe.transpose(psum[:, g % 4, i * P:(i + 1) * P], f[:, tile, :], ident[:])
                    b, first = divmod(tile, TB)
                    gram_last = pe.matmul(psum[:, 4 + b, 0:DM], f[:, tile, :], f[:, tile, :],
                                          start=(first == 0), stop=(first == TB - 1))
                    if first == TB - 1:
                        gram_last.then_inc(gram_summed, 1)
                last.then_inc(turned, 1)
            pe.wait_ge(small_ready, 2)
            n = 0
            for b in range(BATCH):
                for out, left, right in (
                    (psum[:, 6, 0:HD], gram[:, b, :], kv_T[:, 1, :]),
                    (psum[0:HD, 6, 0:HD], gv[:, b, :], kv_T[:, 0, :]),
                    (psum[0:HD, 6, 0:DM], energy_T[:, b, :], o_T[:]),
                    (psum[:, 6, 0:DM], q_w[:], eo[:, b, :]),
                ):
                    pe.wait_ge(linked, n + b + 1)
                    pe.matmul(out, left, right, start=True, stop=True).then_inc(link, 1)
                    n += 1
            pe.wait_ge(linked, 5 * BATCH)
            pe.wait_ge(fT_ready, NB)
            for g in range(NB):
                if g >= 4:
                    pe.wait_ge(added, g - 3)
                for i in range(4):
                    tile = 4 * g + i
                    last = pe.matmul(psum[:, g % 4, i * P:(i + 1) * P], f_T[:, tile * P:(tile + 1) * P],
                                     mix[:, tile // TB, :], start=True, stop=True)
                last.then_inc(out_ready, 1)


def build(nc, inputs, out):
    mixer = {k[len("L0_attn_a_"):]: v for k, v in inputs.items() if k.startswith("L0_attn_a_")}
    linear = {k[len("L0_attn_b_"):]: v for k, v in inputs.items() if k.startswith("L0_attn_b_")}
    experts = {k[len("L0_ffn_"):]: v for k, v in inputs.items() if k.startswith("L0_ffn_")}
    BATCH, L, DM = mixer["x"].shape
    T = BATCH * L
    between = nc.dram_tensor("between", [T, DM], F32, kind="Internal").ap()
    with ExitStack() as ctx:
        X = ctx.enter_context(nc.sbuf_tensor("X", [P, T // P, DM], F32))
        ident = ctx.enter_context(nc.sbuf_tensor("ident", [P, P], F32))
        identity(nc, ident)
        mamba(nc, X, ident, **mixer)
        E, FF, _ = experts["fc1s"].shape
        shared = {name: ctx.enter_context(nc.sbuf_tensor(f"shared_{name}", shape, F32))
                  for name, shape in (("gamma", [P, 2]), ("b1_T", [P, E * FF // P]),
                                      ("b2_all", [P, E, DM]), ("gate_T", [P, E]),
                                      ("w1_T", [P, E, FF]), ("w2_T", [P, E, FF // P, DM]))}
        moe(nc, X, ident, shared, "f1", between, True, **experts)
        attention(nc, X, ident, between, **linear)
        moe(nc, X, ident, shared, "f2", out.rearrange("b l d -> (b l) d"), False, **experts)


_INS = ["L0_attn_a_x", "L0_attn_a_W_in", "L0_attn_a_conv_w", "L0_attn_a_conv_b", "L0_attn_a_A_log",
        "L0_attn_a_D", "L0_attn_a_W_x", "L0_attn_a_W_dt", "L0_attn_a_b_dt", "L0_attn_a_W_out",
        "L0_attn_b_wq", "L0_attn_b_wk", "L0_attn_b_wv", "L0_attn_b_wo",
        "L0_ffn_gate_w", "L0_ffn_ln_gamma", "L0_ffn_ln_beta", "L0_ffn_fc1s", "L0_ffn_b1s",
        "L0_ffn_fc2s", "L0_ffn_b2s"]


def kernel(**inputs):
    import numpy as _np
    import concourse.bacc as _bacc
    from concourse.bass_utils import run_bass_kernel_spmd as _run

    nc = _bacc.Bacc("TRN2", target_bir_lowering=False, num_devices=1)
    arrays, args = {}, {}
    for name in _INS:
        a = _np.ascontiguousarray(inputs[name])
        arrays[f"in_{name}"] = a
        args[name] = nc.dram_tensor(f"in_{name}", a.shape, mybir.dt.from_np(a.dtype),
                                    kind="ExternalInput").ap()
    out = nc.dram_tensor("out_0", arrays["in_L0_attn_a_x"].shape, F32, kind="ExternalOutput").ap()
    build(nc, args, out)
    r = _run(nc, [arrays], core_ids=[0])
    return r.results[0]["out_0"]
```

```python
from contextlib import ExitStack

import concourse.bass as bass
from concourse import mybir

F32 = mybir.dt.float32
F32R = mybir.dt.float32r
BF16 = mybir.dt.bfloat16
F16 = mybir.dt.float16
I32 = mybir.dt.int32
ACT = mybir.ActivationFunctionType
ALU = mybir.AluOpType

P = 128
BANK = 512
LN_EPS = 1e-5


def layer_norm_constants(dve, chain, at, stats, moments, source, tiles):
    for i in range(tiles):
        dve.bn_stats(stats[:, i, :], source(i)).then_inc(chain, 1)
    dve.wait_ge(chain, at + tiles)
    for i in range(tiles):
        dve.bn_aggr(moments[:, i, :], stats[:, i, :]).then_inc(chain, 1)
    dve.wait_ge(chain, at + 2 * tiles)
    return at + 2 * tiles


def mamba(nc, X, ident, x, W_in, conv_w, conv_b, A_log, D, W_x, W_dt, b_dt, W_out):
    BATCH, L, DM = x.shape
    KC, _, CH = conv_w.shape
    NS = A_log.shape[1]
    R = W_dt.shape[0]
    KB = CH // P
    TILES = L // P
    CHUNK = 1024
    NCHUNK = L // CHUNK
    CT = CHUNK // P
    TB = CHUNK // BANK
    RING = 4
    CHUNKS = BATCH * NCHUNK
    STATES = CHUNKS * NS
    STEPS = STATES * KB
    LEFT = 1
    B_AT, LOW_AT, C_AT = 64, 96, 96
    assert NCHUNK == 2 and BATCH == 2 and R <= B_AT and KB == TB == 2

    with nc.cleanup_on_exit(), ExitStack() as ctx:
        def sb(name, shape, dt=F32):
            return ctx.enter_context(nc.sbuf_tensor(name, shape, dt))

        def sem(name):
            return nc.alloc_semaphore(name)

        psum = ctx.enter_context(nc.psum_tensor("m_psum", [P, 8, BANK], F32))
        Y, BCAST, PIECE = 0, 4, 6

        w_z = sb("w_z", [P, CH])
        w_tap = sb("w_tap", [P, KC, CH])
        w_x = sb("w_x", [P, KB, R + 2 * NS])
        w_all = sb("w_all", [P, KB, P])
        w_dt = sb("w_dt", [R, CH])
        w_out = sb("w_out", [P, KB, DM])
        chan = sb("chan", [P, 3, KB])
        decay_rate = sb("decay_rate", [P, KB, NS])
        pick_r = sb("pick_r", [P, NS, P], F32R)
        stats = sb("m_stats", [P, BATCH * TILES, 6])
        moments = sb("m_moments", [P, BATCH * TILES, 2])
        rstd = sb("m_rstd", [P, BATCH * TILES])
        shift = sb("m_shift", [P, BATCH * TILES])
        xn_T = sb("xn_T", [P, BATCH * L])
        u = sb("u", [P, NCHUNK, KB, CHUNK])
        z = sb("z", [P, NCHUNK, KB, CHUNK])
        dt = sb("dt", [P, NCHUNK, KB, CHUNK])
        dtu = sb("dtu", [P, NCHUNK, KB, CHUNK])
        b_split = sb("b_split", [P, NCHUNK, CHUNK], F32R)
        low_c = sb("low_c", [P, CHUNK])
        low = low_c[0:R]
        c_rows = low_c[C_AT:C_AT + NS]
        carry = sb("carry", [P, NS, KB])
        decay = sb("decay", [P, RING, CHUNK])
        state = sb("state", [P, RING, CHUNK])
        drive = sb("drive", [P, RING, CHUNK])
        product = sb("product", [P, RING, CHUNK])
        c_all = sb("c_all", [P, RING, CHUNK])
        xn = decay[:].rearrange("p r (t d) -> p (r t) d", d=DM)
        pick = state[:, 0:2, :].rearrange("p a (s q) -> p (a s) q", q=P)
        w_u = drive[:, 0, 0:CH]
        taps = drive[:, 1, 0:KC * CH].rearrange("p (j c) -> p j c", j=KC)
        c_dram = nc.dram_tensor("c_dram", [NCHUNK, NS, CHUNK], F32, kind="Internal").ap()

        x_loaded = [sem(f"x_loaded{g}") for g in range(CHUNKS)]
        u_weights = sem("u_weights")
        w_loaded = sem("w_loaded")
        constants = sem("m_constants")
        taps_ready = sem("taps_ready")
        w_all_ready = sem("w_all_ready")
        rate_exp = sem("rate_exp")
        rate_ready = sem("rate_ready")
        dve_chain = sem("m_dve_chain")
        variance = sem("variance")
        std_done = sem("std_done")
        normed = sem("normed")
        turned = sem("turned")
        xnT_ready = sem("xnT_ready")
        u_summed = sem("u_summed")
        u_ready = sem("u_ready")
        z_summed = sem("z_summed")
        z_ready = sem("z_ready")
        mixed_summed = sem("mixed_summed")
        low_ready = sem("low_ready")
        c_taken = sem("c_taken")
        c_stored = sem("c_stored")
        b_high = sem("b_high")
        b_ready = sem("b_ready")
        v_summed = sem("v_summed")
        v_ready = sem("v_ready")
        clamped = sem("clamped")
        dt_exp = sem("dt_exp")
        dt_log = sem("dt_log")
        dt_ready = sem("dt_ready")
        dtu_ready = sem("dtu_ready")
        b_bcast = sem("b_bcast")
        c_loaded = [sem(f"c_loaded{r}") for r in range(RING)]
        decay_ready = sem("decay_ready")
        drive_ready = sem("drive_ready")
        scanned = sem("scanned")
        carried = sem("carried")
        product_ready = sem("product_ready")
        summed = sem("summed")
        y_read = sem("y_read")
        gated = sem("gated")
        projected = sem("projected")
        added = sem("added")

        block = ctx.enter_context(nc.Block())

        def pieces(with_out):
            blocks = [(k, t) for k in range(KB) for t in range(TB)]
            by_time = [(k, t) for t in range(TB) for k in range(KB)]
            order = [(("u", k, t), KC) for k, t in by_time]
            order += [(("mixed", t), KB) for t in range(TB)]
            if with_out:
                order += [(("out", t), 2) for t in range(TB)]
            order += [(("v", k, t), 1) for k, t in blocks]
            order += [(("z", k, t), 1) for k, t in by_time]
            return order

        def index_of(piece):
            kind, index = piece[0], piece[1:]
            if kind in ("u", "z"):
                return index[1] * KB + index[0]
            return index[0] * TB + index[1] if kind == "v" else index[0]

        FIRST = sorted(pieces(False), key=lambda p: (
            (p[0][2], "uz".index(p[0][0])) if p[0][0] in "uz" else (TB, 0)))
        assert FIRST[0][0] == ("u", 0, 0) and FIRST[8][0] == ("mixed", 0)
        UNITS = [2, 3, 3, 3, 3, 2, 2, 2, 2, 2, 2, 2, 1, 1, 1, 1]
        due, unit_due = {}, {}
        at_state = [s for s, count in enumerate(UNITS) for _ in range(count)]
        for piece, cost in pieces(True):
            for i in range(cost):
                due[piece] = unit_due[piece, i] = at_state[len(unit_due)]
        V_DUE = due["v", KB - 1, TB - 1]
        SOFTEN, RAISE = 2, 2
        EARLY = CHUNK // BANK + 1
        LAG = 3

        def starts_batch(g):
            return g % NCHUNK == 0

        def carry_count(n):
            g, at = divmod(n, NS * KB)
            return (g // NCHUNK) * NS * KB + at + 1

        @block.sync
        def _(sp):
            for g in range(CHUNKS):
                b, c = divmod(g, NCHUNK)
                sp.dma_start(X[:, g * CT:(g + 1) * CT, :],
                             x[b, c * CHUNK:(c + 1) * CHUNK].rearrange("(i p) d -> p i d", p=P)
                             ).then_inc(x_loaded[g], 16)
            for out, source in ((w_x[:], W_x.rearrange("(k p) n -> p k n", p=P)),
                                (w_dt[:], W_dt),
                                (w_out[:], W_out.rearrange("(k p) n -> p k n", p=P)),
                                (decay_rate[:], A_log.rearrange("(k p) s -> p k s", p=P))):
                sp.dma_start(out, source).then_inc(w_loaded, 16)
            with nc.allow_non_contiguous_dma(reason="a few scalars of each channel"):
                for n, source in enumerate((conv_b, D, b_dt)):
                    sp.dma_start(chan[:, n, :], source.rearrange("(k p) -> p k", p=P)
                                 ).then_inc(w_loaded, 16)

            for q in range(STATES):
                g, s = divmod(q, NS)
                if s == 0:
                    sp.wait_ge(c_stored, 16 * (g + 1))
                if q >= RING:
                    sp.wait_ge(product_ready, KB * (q - RING + 1))
                sp.dma_start(c_all[:, q % RING, :], c_dram[g % 2, s:s + 1, :].broadcast_to([P, CHUNK])
                             ).then_inc(c_loaded[q % RING], 16)

        @block.gpsimd
        def _(pool):
            pool.memset(w_all[:], 0.0).then_inc(constants, 1)
            pool.memset(pick, 0.0).then_inc(constants, 1)
            for n, base in enumerate((-B_AT, -LOW_AT)):
                pool.wait_ge(constants, 2 + n)
                pool.affine_select(out=pick, in_=pick, compare_op=ALU.not_equal, fill=1.0,
                                   base=base, pattern=[[-1, NS], [0, P]],
                                   channel_multiplier=1).then_inc(constants, 1)
            pool.wait_ge(u_weights, 16 * 3)
            for j in range(KC):
                pool.tensor_tensor(w_tap[:, j, :], w_u, taps[:, j, :], ALU.mult).then_inc(taps_ready, 1)
            pool.wait_ge(constants, 4)
            pool.wait_ge(taps_ready, KC)
            pool.tensor_copy(pick_r[B_AT:P], pick[B_AT:P]).then_inc(constants, 1)

            pool.wait_ge(constants, 5)

            def dt_times_u(g, k):
                pool.wait_ge(dt_ready, KB * g + k + 1)
                pool.wait_ge(u_ready, KB * TB * g + KB * (TB - 1) + k + 1)
                pool.tensor_tensor(dtu[:, g % 2, k, :], dt[:, g % 2, k, :], u[:, g % 2, k, :],
                                   ALU.mult).then_inc(dtu_ready, 1)

            for n in range(STEPS):
                q, k = divmod(n, KB)
                g, s = divmod(q, NS)
                if s == V_DUE + RAISE + 1 and g + 1 < CHUNKS:
                    dt_times_u(g + 1, k)
                if k == 0:
                    pool.wait_ge(c_loaded[q % RING], 16 * (q // RING + 1))
                pool.wait_ge(scanned, n + 1)
                if n >= RING:
                    pool.wait_ge(summed, n - RING + 1)
                pool.tensor_tensor(product[:, n % RING, :], state[:, n % RING, :],
                                   c_all[:, q % RING, :], ALU.mult).then_inc(product_ready, 1)

        @block.scalar
        def _(act):
            act.dma_start(w_u, W_in[:, 0:CH]).then_inc(u_weights, 16)
            act.dma_start(w_z[:], W_in[:, CH:2 * CH]).then_inc(u_weights, 16)
            act.dma_start(taps, conv_w.rearrange("j o c -> o j c").broadcast_to([P, KC, CH])
                          ).then_inc(u_weights, 16)

            def std(first, end):
                act.wait_ge(variance, end)
                part = rstd[:, first * CT:end * CT]
                act.activation(part, part, ACT.Sqrt).then_inc(std_done, 1)

            def take_turned(g):
                act.wait_ge(turned, g + 1)
                act.copy(xn_T[:, g * BANK:(g + 1) * BANK], psum[:, g % 4, :]).then_inc(xnT_ready, 1)

            def take(piece, number, g):
                buf = g % 2
                bank = psum[:, PIECE + number % 2, :]
                kind, index = piece[0], piece[1:]
                span = slice(index[-1] * BANK, (index[-1] + 1) * BANK)
                i = index_of(piece)
                if kind == "u":
                    act.wait_ge(u_summed, KB * TB * g + i + 1)
                    act.activation(u[:, buf, index[0], span], bank, ACT.Silu,
                                   bias=chan[:, 0, index[0]:index[0] + 1]).then_inc(u_ready, 1)
                elif kind == "z":
                    act.wait_ge(z_summed, KB * TB * g + i + 1)
                    act.activation(z[:, buf, index[0], span], bank, ACT.Silu).then_inc(z_ready, 1)
                elif kind == "v":
                    act.wait_ge(v_summed, KB * TB * g + i + 1)
                    act.activation(dtu[:, buf, index[0], span], bank, ACT.Identity,
                                   bias=chan[:, 2, index[0]:index[0] + 1]).then_inc(v_ready, 1)
                elif kind == "mixed":
                    act.wait_ge(mixed_summed, TB * g + i + 1)
                    act.copy(low[:, span], bank[0:R]).then_inc(low_ready, 1)
                    act.copy(b_split[B_AT:B_AT + 32, buf, span], bank[B_AT:B_AT + 32]).then_inc(b_high, 1)
                    act.copy(c_rows[:, span], bank[C_AT:C_AT + NS]).then_inc(c_taken, 1)

            def store_c(g):
                act.wait_ge(c_taken, TB * (g + 1))
                act.dma_start(c_dram[g % 2], c_rows).then_inc(c_stored, 16)

            def soften(g):
                for k in range(KB):
                    act.wait_ge(clamped, KB * g + k + 1)
                    act.activation(dt[:, g % 2, k, :], dt[:, g % 2, k, :], ACT.Exp).then_inc(dt_exp, 1)
                for k in range(KB):
                    act.wait_ge(dt_exp, KB * g + k + 1)
                    act.activation(dt[:, g % 2, k, :], dt[:, g % 2, k, :], ACT.Ln,
                                   bias=1.0).then_inc(dt_log, 1)

            std(0, 1)
            take_turned(0)
            take_turned(1)
            std(1, CHUNKS)
            act.wait_ge(w_loaded, 16 * 7)
            for number, (piece, _) in enumerate(FIRST):
                if piece == ("u", 0, 1):
                    take_turned(2)
                take(piece, number, 0)
                if piece == ("mixed", TB - 1):
                    store_c(0)
            act.activation(decay_rate[:], decay_rate[:], ACT.Exp).then_inc(rate_exp, 1)
            soften(0)

            act.wait_ge(rate_ready, 1)
            for n in range(STEPS):
                q, k = divmod(n, KB)
                g, s = divmod(q, NS)
                if s == 0 and k == 0:
                    act.wait_ge(dt_ready, KB * (g + 1))
                before = n - RING
                if before >= 0:
                    act.wait_ge(scanned, before + 1)
                    if starts_batch(before // (NS * KB)):
                        last_s, last_k = divmod(before % (NS * KB), KB)
                        act.copy(carry[:, last_s, last_k:last_k + 1],
                                 state[:, n % RING, CHUNK - 1:CHUNK]).then_inc(carried, 1)
                act.activation(decay[:, n % RING, :], dt[:, g % 2, k, :], ACT.Exp,
                               scale=decay_rate[:, k, s:s + 1]).then_inc(decay_ready, 1)
                if k == 0 or g + 1 == CHUNKS:
                    continue
                for number, (piece, _) in enumerate(pieces(g > 0)):
                    at = due[piece]
                    if piece[0] == "z":
                        at = due["z", KB - 1, piece[2]]
                    if at != s or piece[0] == "out":
                        continue
                    if piece == ("u", 0, 0) and g:
                        act.wait_ge(gated, KB * g)
                    if piece == ("mixed", 0):
                        act.wait_ge(c_stored, 16 * (g + 1))
                    if piece == ("z", 0, 0) and g:
                        act.wait_ge(projected, TB * g)
                    take(piece, number, g + 1)
                    if piece == ("mixed", TB - 1):
                        store_c(g + 1)
                if s == V_DUE + SOFTEN:
                    soften(g + 1)

        @block.vector
        def _(dve):
            at = 0

            def token_stats(g, at):
                dve.wait_ge(x_loaded[g], 16)
                tiles = slice(g * CT, (g + 1) * CT)
                at = layer_norm_constants(dve, dve_chain, at, stats[:, tiles, :], moments[:, tiles, :],
                                          lambda i: X[:, g * CT + i, :], CT)
                dve.tensor_scalar(rstd[:, tiles], moments[:, tiles, 1], LN_EPS, None,
                                  ALU.add).then_inc(variance, 1)
                return at

            def normalise(first, end, at):
                tiles = slice(first * CT, end * CT)
                dve.wait_ge(std_done, 2 if first else 1)
                dve.reciprocal(rstd[:, tiles], rstd[:, tiles]).then_inc(dve_chain, 1)
                dve.wait_ge(dve_chain, at + 1)
                dve.scalar_tensor_tensor(out=shift[:, tiles], in0=moments[:, tiles, 0], scalar=-1.0,
                                         in1=rstd[:, tiles], op0=ALU.mult,
                                         op1=ALU.mult).then_inc(dve_chain, 1)
                dve.wait_ge(dve_chain, at + 2)
                for i in range(first * CT, end * CT):
                    dve.tensor_scalar(xn[:, i, :], X[:, i, :], rstd[:, i:i + 1], shift[:, i:i + 1],
                                      ALU.mult, ALU.add).then_inc(normed, 1)
                return at + 2

            at = normalise(0, 1, token_stats(0, at))
            for g in range(1, CHUNKS):
                at = token_stats(g, at)
            at = normalise(1, CHUNKS, at)
            dve.wait_ge(w_loaded, 16 * 7)
            dve.wait_ge(constants, 1)
            for k in range(KB):
                for first, of, width in ((0, 0, R), (B_AT, R, NS), (C_AT, R + NS, NS)):
                    last = dve.tensor_copy(w_all[:, k, first:first + width], w_x[:, k, of:of + width])
            last.then_inc(w_all_ready, 1)

            def split_b(g, t):
                span = slice(t * BANK, (t + 1) * BANK)
                number = KB * TB + t
                dve.wait_ge(b_high, TB * g + t + 1)
                dve.tensor_tensor(b_split[LOW_AT:LOW_AT + 32, g % 2, span],
                                  psum[B_AT:B_AT + 32, PIECE + number % 2, :],
                                  b_split[B_AT:B_AT + 32, g % 2, span].bitcast(F32),
                                  ALU.subtract).then_inc(b_ready, 1)

            def clamp(g, k):
                dve.wait_ge(v_ready, KB * TB * g + TB * (k + 1))
                dve.tensor_scalar(dt[:, g % 2, k, :], dtu[:, g % 2, k, :], 40.0, None,
                                  ALU.min).then_inc(clamped, 1)

            def raise_dt(g, k):
                dve.wait_ge(dt_log, KB * g + k + 1)
                dve.tensor_tensor(dt[:, g % 2, k, :], dt[:, g % 2, k, :], dtu[:, g % 2, k, :],
                                  ALU.max).then_inc(dt_ready, 1)

            for t in range(TB):
                split_b(0, t)
            for k in range(KB):
                clamp(0, k)
            dve.wait_ge(rate_exp, 1)
            dve.tensor_scalar(decay_rate[:], decay_rate[:], -1.0, None, ALU.mult).then_inc(rate_ready, 1)
            for g in range(EARLY, BATCH * L // BANK):
                dve.wait_ge(turned, g + 1)
                dve.tensor_copy(xn_T[:, g * BANK:(g + 1) * BANK], psum[:, g % 4, :]).then_inc(xnT_ready, 1)
            for k in range(KB):
                raise_dt(0, k)
                dve.wait_ge(dt_ready, k + 1)
                dve.tensor_tensor(dtu[:, 0, k, :], dt[:, 0, k, :], u[:, 0, k, :],
                                  ALU.mult).then_inc(dtu_ready, 1)

            def force(n):
                q, k = divmod(n, KB)
                g, s = divmod(q, NS)
                dve.wait_ge(b_bcast, q + 1)
                if s == 0:
                    dve.wait_ge(dtu_ready, KB * g + k + 1)
                if n >= RING:
                    dve.wait_ge(scanned, n - RING + 1)
                dve.tensor_tensor(
                    drive[:, n % RING, :].rearrange("p (a t) -> p a t", t=BANK),
                    psum[:, BCAST:BCAST + TB, :],
                    dtu[:, g % 2, k, :].rearrange("p (a t) -> p a t", t=BANK),
                    ALU.mult).then_inc(drive_ready, 1)

            def scan(n):
                q, k = divmod(n, KB)
                g, s = divmod(q, NS)
                before = n - RING
                dve.wait_ge(decay_ready, n + 1)
                dve.wait_ge(drive_ready, n + 1)
                if before >= 0:
                    dve.wait_ge(product_ready, before + 1)
                    if starts_batch(before // (NS * KB)):
                        dve.wait_ge(carried, carry_count(before))
                if not starts_batch(g) and before >= 0 and not starts_batch(before // (NS * KB)):
                    dve.wait_ge(carried, carry_count(n - NS * KB))
                dve.tensor_tensor_scan(state[:, n % RING, :], decay[:, n % RING, :],
                                       drive[:, n % RING, :],
                                       0.0 if starts_batch(g) else carry[:, s, k:k + 1],
                                       ALU.mult, ALU.add).then_inc(scanned, 1)

            def gate(g):
                buf = g % 2
                for k in range(KB):
                    dve.wait_ge(summed, KB * NS * (g + 1) - KB + k + 1)
                    dve.scalar_tensor_tensor(
                        out=u[:, buf, k, :].rearrange("p (a t) -> p a t", t=BANK),
                        in0=u[:, buf, k, :].rearrange("p (a t) -> p a t", t=BANK),
                        scalar=chan[:, 1, k:k + 1], in1=psum[:, Y + TB * k:Y + TB * (k + 1), :],
                        op0=ALU.mult, op1=ALU.add).then_inc(y_read, 1)
                for k in range(KB):
                    dve.wait_ge(y_read, KB * g + k + 1)
                    if k == 0:
                        dve.wait_ge(z_ready, KB * TB * (g + 1))
                    dve.tensor_tensor(z[:, buf, k, :], u[:, buf, k, :], z[:, buf, k, :],
                                      ALU.mult).then_inc(gated, 1)

            def add(g, t, number):
                dve.wait_ge(projected, TB * g + t + 1)
                first = CT * g + CT // TB * t
                rows = X[:, first:first + CT // TB, :]
                dve.tensor_tensor(rows, rows, psum[:, PIECE + number % 2, :].rearrange(
                    "p (t d) -> p t d", d=DM), ALU.add).then_inc(added, 1)

            for k in range(KB):
                force(k)
            for q in range(STATES):
                g, s = divmod(q, NS)
                if q + 1 < STATES:
                    for k in range(KB):
                        force(KB * (q + 1) + k)
                for k in range(KB):
                    scan(KB * q + k)
                if g and s == 1:
                    gate(g - 1)
                for t in range(TB):
                    if g + 1 < CHUNKS and s == due["mixed", t]:
                        split_b(g + 1, t)
                    if g and s == due["out", t]:
                        add(g - 1, t, KB * TB + TB + t)
                if g + 1 < CHUNKS:
                    for k in range(KB):
                        if s == V_DUE - 1 + k:
                            clamp(g + 1, k)
                    if s == V_DUE + RAISE:
                        for k in range(KB):
                            raise_dt(g + 1, k)
            g = CHUNKS - 1
            buf = g % 2
            dve.wait_ge(summed, STEPS)
            dve.wait_ge(z_ready, KB * TB * CHUNKS)
            for t in range(TB):
                span = slice(t * BANK, (t + 1) * BANK)
                for k in range(KB):
                    dve.scalar_tensor_tensor(
                        out=u[:, buf, k, span], in0=u[:, buf, k, span], scalar=chan[:, 1, k:k + 1],
                        in1=psum[:, Y + TB * k + t, :], op0=ALU.mult, op1=ALU.add).then_inc(y_read, 1)
                for k in range(KB):
                    dve.wait_ge(y_read, KB * (g + t) + k + 1)
                    dve.tensor_tensor(z[:, buf, k, span], u[:, buf, k, span], z[:, buf, k, span],
                                      ALU.mult).then_inc(gated, 1)
            for t in range(TB):
                add(g, t, t)

        @block.tensor
        def _(pe):
            def turn(g):
                if g >= 4:
                    pe.wait_ge(xnT_ready, g - 3)
                for i in range(4):
                    pe.wait_ge(normed, 4 * g + i + 1)
                    last = pe.transpose(psum[:, g % 4, i * P:(i + 1) * P], xn[:, 4 * g + i, :], ident[:])
                last.then_inc(turned, 1)

            def wait_read(piece, g):
                kind, index = piece[0], piece[1:]
                i = index_of(piece)
                if kind == "u":
                    pe.wait_ge(u_ready, KB * TB * g + i + 1)
                elif kind == "z":
                    pe.wait_ge(z_ready, KB * TB * g + i + 1)
                elif kind == "v":
                    pe.wait_ge(v_ready, KB * TB * g + i + 1)
                elif kind == "mixed":
                    pe.wait_ge(low_ready, TB * g + i + 1)
                    pe.wait_ge(c_taken, TB * g + i + 1)
                    pe.wait_ge(b_ready, TB * g + i + 1)

            def project(bank, g, t, half):
                out = psum[:, PIECE + bank, :]
                pe.wait_ge(gated, KB * (g + 1 + (t if g + 1 == CHUNKS else 0)))
                for i in range(2 * half, 2 * half + 2):
                    tile = CT // TB * t + i
                    for k in range(KB):
                        last = pe.matmul(out[:, i * DM:(i + 1) * DM],
                                         z[:, g % 2, k, tile * P:(tile + 1) * P], w_out[:, k, :],
                                         start=(k == 0), stop=(k == KB - 1))
                if half:
                    last.then_inc(projected, 1)

            def unit(piece, number, i, g):
                first_token, buf = g * CHUNK, g % 2
                out = psum[:, PIECE + number % 2, :]
                kind, index = piece[0], piece[1:]
                t = index[-1]
                if kind == "u":
                    k = index[0]
                    at_start = starts_batch(g) and t == 0
                    at_end = starts_batch(g + 1) and t == TB - 1
                    j = ((1, 0, 2, 3) if at_start else (1, 2, 3, 0))[i]
                    first = first_token + t * BANK + j - LEFT
                    lo = LEFT - j if at_start and j < LEFT else 0
                    hi = BANK - (j - LEFT) if at_end and j > LEFT else BANK
                    ins = pe.matmul(out[:, lo:hi], w_tap[:, j, k * P:(k + 1) * P],
                                    xn_T[:, first + lo:first + hi],
                                    start=(i == 0), stop=(i == KC - 1))
                    if i == KC - 1:
                        ins.then_inc(u_summed, 1)
                elif kind == "z":
                    first = first_token + t * BANK
                    pe.matmul(out, w_z[:, index[0] * P:(index[0] + 1) * P], xn_T[:, first:first + BANK],
                              start=True, stop=True).then_inc(z_summed, 1)
                elif kind == "mixed":
                    pe.wait_ge(u_ready, KB * TB * g + KB * t + i + 1)
                    ins = pe.matmul(out, w_all[:, i, :], u[:, buf, i, t * BANK:(t + 1) * BANK],
                                    start=(i == 0), stop=(i == KB - 1))
                    if i == KB - 1:
                        ins.then_inc(mixed_summed, 1)
                elif kind == "v":
                    pe.wait_ge(low_ready, TB * g + t + 1)
                    pe.matmul(out, w_dt[:, index[0] * P:(index[0] + 1) * P],
                              low[:, t * BANK:(t + 1) * BANK], start=True,
                              stop=True).then_inc(v_summed, 1)

            for g in range(EARLY - 1):
                turn(g)
            pe.wait_ge(taps_ready, KC)
            pe.wait_ge(w_loaded, 16 * 7)
            for number, (piece, cost) in enumerate(FIRST):
                if number >= 2:
                    wait_read(FIRST[number - 2][0], 0)
                if piece == ("u", 0, 1):
                    turn(EARLY - 1)
                if piece[0] == "u":
                    pe.wait_ge(xnT_ready, piece[2] + 2)
                if piece[0] == "mixed":
                    pe.wait_ge(w_all_ready, 1)
                    pe.wait_ge(constants, 5)
                for i in range(cost):
                    unit(piece, number, i, 0)
            for g in range(EARLY, BATCH * L // BANK):
                turn(g)

            def sum_state(n):
                q, k = divmod(n, KB)
                g, s = divmod(q, NS)
                if s == 0 and g:
                    pe.wait_ge(y_read, KB * (g - 1) + k + 1)
                pe.wait_ge(product_ready, n + 1)
                for h in range(TB):
                    last = pe.matmul(psum[:, Y + TB * k + h, :], ident[:],
                                     product[:, n % RING, h * BANK:(h + 1) * BANK],
                                     start=(s == 0), stop=(s == NS - 1))
                last.then_inc(summed, 1)

            def prepare(g, s, half):
                mine = [(number, piece, i) for number, (piece, cost) in enumerate(pieces(g > 0))
                        for i in range(cost) if unit_due[piece, i] == s
                        and (g + 1 < CHUNKS or piece[0] == "out")]
                middle = (len(mine) + 1) // 2
                for number, piece, i in mine[middle:] if half else mine[:middle]:
                    if i == 0 and number < 2:
                        wait_read(("z", number, TB - 1) if g else FIRST[-2 + number][0], g)
                    elif i == 0 and g + 1 < CHUNKS:
                        before = pieces(g > 0)[number - 2][0]
                        if before[0] == "out":
                            pe.wait_ge(added, TB * (g - 1) + before[1] + 1)
                        else:
                            wait_read(before, g + 1)
                    if piece[0] == "out":
                        project(number % 2, g - 1, piece[1], i)
                    else:
                        unit(piece, number, i, g + 1)

            pe.wait_ge(xnT_ready, BATCH * L // BANK)
            for q in range(STATES + LAG):
                g, s = divmod(q, NS)
                if q < STATES:
                    if q:
                        pe.wait_ge(drive_ready, KB * q)
                    if s == 0:
                        pe.wait_ge(b_ready, TB * (g + 1))
                    for h in range(TB):
                        last = pe.matmul(psum[:, BCAST + h, :], pick_r[B_AT:P, s, :],
                                         b_split[B_AT:P, g % 2, h * BANK:(h + 1) * BANK],
                                         start=True, stop=True)
                    last.then_inc(b_bcast, 1)
                for k in range(KB):
                    if q >= LAG:
                        sum_state(KB * (q - LAG) + k)
                    if q < STATES:
                        prepare(g, s, k)
            for t in range(TB):
                pe.wait_ge(added, TB * (CHUNKS - 2) + t + 1)
                for half in range(2):
                    project(t, CHUNKS - 1, t, half)


def identity(nc, ident):
    with nc.semaphore("ident_zero") as zeroed, nc.Block() as block:
        @block.gpsimd
        def _(pool):
            pool.memset(ident[:], 0.0).then_inc(zeroed, 1)
            pool.wait_ge(zeroed, 1)
            pool.affine_select(out=ident[:], in_=ident[:], compare_op=ALU.not_equal, fill=1.0, base=0,
                               pattern=[[-1, P]], channel_multiplier=1).then_inc(zeroed, 1)
            pool.wait_ge(zeroed, 2)


def moe(nc, X, ident, shared, name, dst, first_use, gate_w, ln_gamma, ln_beta, fc1s, b1s, fc2s, b2s):
    E, FF, DM = fc1s.shape
    TILES = X.shape[1]
    T = TILES * P
    K = T // E
    KT = K // P
    FB = FF // P
    J = P // E
    SPAN = T // J
    HALVES = SPAN // P
    PAIRS = HALVES * P
    ROW = DM + E
    NB = T // BANK
    STEPS = 13
    WAYS = 4
    LO = 32
    HI = K // LO
    FAR = float(4 * K)
    MIDDLE = T // 2
    AHEAD = 4
    GROUPS = 2
    assert MIDDLE <= 2048 and HALVES == 2

    dram = lambda what, shape: nc.dram_tensor(f"{name}_{what}", shape, F32, kind="Internal").ap()
    table = dram("table", [T, ROW])
    score_dram = dram("score_dram", [E, T])
    gamma, b1_T, b2_all, gate_T, w1_T, w2_T = (
        shared[key] for key in ("gamma", "b1_T", "b2_all", "gate_T", "w1_T", "w2_T"))

    with nc.cleanup_on_exit(), ExitStack() as keep:
        tokens = keep.enter_context(nc.sbuf_tensor(f"{name}_tokens", [P, E, KT], I32))
        got = keep.enter_context(nc.sbuf_tensor(f"{name}_got", [P, AHEAD, KT, ROW], F32))
        gathered = [nc.alloc_semaphore(f"{name}_gathered{r}") for r in range(AHEAD)]

        def gather(pool, e):
            for t in range(KT):
                pool.indirect_dma_start(got[:, e % AHEAD, t, :], None, table,
                                        bass.IndirectOffsetOnAxis(ap=tokens[:, e, t:t + 1], axis=0)
                                        ).then_inc(gathered[e % AHEAD], 16)

        with nc.cleanup_on_exit(), ExitStack() as ctx:
            def sb(what, shape, dt=F32):
                return ctx.enter_context(nc.sbuf_tensor(f"{name}_{what}", shape, dt))

            def sem(what):
                return nc.alloc_semaphore(f"{name}_{what}")

            psum = ctx.enter_context(nc.psum_tensor(f"{name}_psum1", [P, 8, BANK], F32))
            COUNTS, PLACES, LISTS, SCORES, W_TURN, SMALL = 0, 1, 2, 4, 5, 7
            SCORE_BANKS = 3
            HT = TILES // 2
            stats = sb("stats", [P, TILES, 6])
            moments = sb("moments", [P, TILES, 2])
            rstd = sb("rstd", [P, TILES])
            shift = sb("shift", [P, TILES])
            again = sb("again", [P, TILES])
            rstd2 = sb("rstd2", [P, TILES])
            shift2 = sb("shift2", [P, TILES])
            f = sb("f", [P, TILES, DM])
            f_T = sb("f_T", [P, T])
            rows = sb("rows", [P, TILES, ROW])
            score = sb("score", [E, T])
            if first_use:
                gate_raw = sb("gate_raw", [E, DM])
                b1_raw = sb("b1_raw", [E * FB, P])
                w1_raw = sb("w1_raw", [P, E, FB, DM])
                w2_raw = sb("w2_raw", [P, E, FF])
            search = sb("search", [P, SPAN])
            same = sb("same", [P, P])
            before = sb("before", [P, P])
            same_b = sb("same_b", [P, P], BF16)
            before_b = sb("before_b", [P, P], BF16)
            steps = sb("steps", [P, (STEPS + 1) * WAYS])
            bounds = sb("bounds", [P, WAYS])
            following = sb("following", [P, WAYS])
            hits = sb("hits", [P, WAYS - 1, SPAN], BF16)
            count = sb("count", [P, WAYS - 1], BF16)
            passed = sb("passed", [P, WAYS - 1])
            passes = sb("passes", [P, 1])
            ones = sb("ones", [P, SPAN])
            above = sb("above", [P, 2, SPAN])
            rank = sb("rank", [P, 2, SPAN])
            row_count = sb("row_count", [P, 2], BF16)
            offset = sb("offset", [P, 2])
            place = sb("place", [P, SPAN])
            place_T = sb("place_T", [P, PAIRS], I32)
            low_i = sb("low_i", [P, PAIRS], I32)
            high_i = sb("high_i", [P, PAIRS], I32)
            low = sb("low_h", [P, PAIRS], F16)
            high = sb("high_h", [P, PAIRS], F16)
            token_i = sb("token_i", [P, PAIRS], I32)
            token = sb("token", [P, PAIRS], F16)
            one_low = sb("one_low", [P, LO, PAIRS], F16)
            token_high = sb("token_high", [P, HI, PAIRS], F16)

            loaded = sem("loaded")
            w_loaded = sem("w_loaded")
            chain = sem("chain")
            variance = sem("variance")
            std_done = sem("std_done")
            ln_ready = sem("ln_ready")
            variance2 = sem("variance2")
            std2_done = sem("std2_done")
            ln2_ready = sem("ln2_ready")
            f_first = sem("f_first")
            f_second = sem("f_second")
            base_ready = sem("base_ready")
            rows_ready = sem("rows_ready")
            f_turned = sem("f_turned")
            fT_ready = sem("fT_ready")
            small_turned = sem("small_turned")
            small_ready = sem("small_ready")
            w_turned = sem("w_turned")
            w_taken = sem("w_taken")
            gated = sem("gated")
            tanh_done = sem("tanh_done")
            score_ready = sem("score_ready")
            score_turned = sem("score_turned")
            weights_ready = sem("weights_ready")
            score_stored = sem("score_stored")
            search_loaded = sem("search_loaded")
            stored = sem("stored")
            made = sem("made")
            cast = sem("cast")
            steps_made = sem("steps_made")
            counted = sem("counted")
            totalled = sem("totalled")
            passes_ready = sem("passes_ready")
            following_ready = sem("following_ready")
            moved = sem("moved")
            link = sem("link")
            rowed = sem("rowed")
            offsets = sem("offsets")
            placed = sem("placed")
            place_turned = sem("place_turned")
            split_ready = sem("split_ready")
            one_hot = sem("one_hot")
            high_hot = sem("high_hot")
            listed = sem("listed")
            tokens_ready = sem("tokens_ready")
            block = ctx.enter_context(nc.Block())

            def pairs_of(tile, group, *index):
                view = tile[(slice(None), *index, slice(None))].rearrange("p (h m) -> p h m", h=HALVES)
                return view[:, :, group * P // GROUPS:(group + 1) * P // GROUPS]

            @block.sync
            def _(sp):
                if first_use:
                    sp.dma_start(gate_raw[:], gate_w).then_inc(loaded, 16)
                    sp.dma_start(b1_raw[:], b1s.rearrange("e (q f) -> (e q) f", f=P)).then_inc(loaded, 16)
                    with nc.allow_non_contiguous_dma(reason="one scalar of each channel"):
                        for n, source in enumerate((ln_gamma, ln_beta)):
                            sp.dma_start(gamma[:, n:n + 1],
                                         source.rearrange("(p o) -> p o", o=1)).then_inc(loaded, 16)
                    sp.dma_start(b2_all[:].rearrange("p e d -> p (e d)"),
                                 b2s.rearrange("(o e) d -> o (e d)", o=1).broadcast_to([P, E * DM])
                                 ).then_inc(loaded, 16)
                    sp.dma_start(w1_raw[:].rearrange("p e q d -> p (e q) d"),
                                 fc1s.rearrange("e (q p) d -> p (e q) d", p=P)).then_inc(w_loaded, 16)
                    sp.dma_start(w2_raw[:], fc2s.rearrange("e d f -> d e f")).then_inc(w_loaded, 16)
                sp.wait_ge(score_ready, NB)
                sp.dma_start(score_dram, score[:]).then_inc(score_stored, 16)
                sp.wait_ge(score_stored, 16)
                sp.dma_start(search[:], score_dram.rearrange("e (j t) -> (e j) t", j=J)
                             ).then_inc(search_loaded, 16)
                sp.wait_ge(base_ready, 4)
                sp.dma_start(dst.rearrange("(i p) d -> p i d", p=P), f[:]).then_inc(stored, 16)
                sp.wait_ge(rows_ready, TILES)
                sp.wait_ge(weights_ready, 1)
                sp.dma_start(table.rearrange("(i p) d -> p i d", p=P), rows[:]).then_inc(stored, 16)
                sp.wait_ge(stored, 32)
                if first_use:
                    sp.wait_ge(loaded, 16 * 5)

            @block.gpsimd
            def _(pool):
                for i in range(STEPS):
                    for way in range(WAYS):
                        pool.memset(steps[:, i * WAYS + way:i * WAYS + way + 1], way * 2.0 ** (-1 - 2 * i))
                pool.memset(steps[:, STEPS * WAYS:], 0.0).then_inc(steps_made, 1)
                pool.memset(same[:], 1.0).then_inc(made, 1)
                view = same[:].rearrange("p (e j) -> p e j", j=J)
                pool.wait_ge(made, 1)
                pool.affine_select(out=view, in_=view, compare_op=ALU.is_ge, fill=0.0, base=0,
                                   pattern=[[-J, E], [0, J]], channel_multiplier=1).then_inc(made, 1)
                pool.wait_ge(made, 2)
                pool.affine_select(out=view, in_=view, compare_op=ALU.is_ge, fill=0.0, base=J - 1,
                                   pattern=[[J, E], [0, J]], channel_multiplier=-1).then_inc(made, 1)
                pool.wait_ge(made, 3)
                pool.affine_select(out=before[:], in_=same[:], compare_op=ALU.is_ge, fill=0.0, base=-1,
                                   pattern=[[1, P]], channel_multiplier=-1).then_inc(made, 1)
                pool.memset(ones[:], 1.0).then_inc(made, 1)
                pool.iota(token_i[:], pattern=[[P, HALVES], [0, E], [SPAN, J]], base=-MIDDLE,
                          channel_multiplier=1).then_inc(made, 1)
                pool.wait_ge(made, 6)
                pool.tensor_copy(same_b[:], same[:]).then_inc(cast, 1)
                pool.tensor_copy(before_b[:], before[:]).then_inc(cast, 1)
                pool.tensor_copy(token[:], token_i[:]).then_inc(cast, 1)
                quarter = TILES // 4
                for n in range(4):
                    part = slice(n * quarter, (n + 1) * quarter)
                    pool.wait_ge(f_turned, (n + 1) * quarter // 4)
                    pool.tensor_tensor(f[:, part, :], X[:, part, :], f[:, part, :],
                                       ALU.add).then_inc(base_ready, 1)
                pool.wait_ge(stored, 32)
                pool.wait_ge(tokens_ready, P // LO)
                gather(pool, 0)

            @block.scalar
            def _(act):
                def roots(h):
                    part = slice(h * HT, (h + 1) * HT)
                    act.wait_ge(variance, h + 1)
                    act.activation(rstd[:, part], rstd[:, part], ACT.Sqrt).then_inc(std_done, 1)
                    act.wait_ge(variance2, h + 1)
                    act.activation(again[:, part], again[:, part], ACT.Sqrt).then_inc(std2_done, 1)

                def take_turned(g):
                    act.wait_ge(f_turned, g + 1)
                    act.copy(f_T[:, g * BANK:(g + 1) * BANK], psum[:, g % 4, :]).then_inc(fT_ready, 1)

                def tanh(g):
                    act.wait_ge(gated, g + 1)
                    act.activation(score[:, g * BANK:(g + 1) * BANK],
                                   psum[0:E, SCORES + g % SCORE_BANKS, :], ACT.Tanh).then_inc(tanh_done, 1)

                def normalise(first, end):
                    for i in range(first, end):
                        act.activation(f[:, i, :], X[:, i, :], ACT.Identity, bias=shift[:, i:i + 1],
                                       scale=rstd[:, i:i + 1]).then_inc(f_first, 1)

                roots(0)
                act.wait_ge(ln_ready, 2)
                normalise(0, HT // 2)
                take_turned(0)
                normalise(HT // 2, 3 * HT // 4)
                take_turned(1)
                roots(1)
                normalise(3 * HT // 4, HT)
                for g in range(2, NB):
                    take_turned(g)
                    tanh(g - 2)
                tanh(NB - 2)
                tanh(NB - 1)
                act.wait_ge(ln2_ready, 2)
                for i in range(TILES):
                    act.activation(rows[:, i, 0:DM], X[:, i, :], ACT.Identity, bias=shift2[:, i:i + 1],
                                   scale=rstd2[:, i:i + 1]).then_inc(rows_ready, 1)
                    if first_use and i % 2:
                        n = i // 2
                        e, layer = divmod(n, 2)
                        act.wait_ge(w_turned, n + 1)
                        where = w2_T[:, e].rearrange("p q d -> p (q d)") if layer else w1_T[:, e, :]
                        act.copy(where, psum[:, W_TURN + n % 2, :]).then_inc(w_taken, 1)

            @block.vector
            def _(dve):
                def round_score(g):
                    dve.wait_ge(tanh_done, g + 1)
                    part = score[:, g * BANK:(g + 1) * BANK]
                    dve.tensor_scalar(part, part, 1.0, -1.0, ALU.add, ALU.add).then_inc(score_ready, 1)

                at = 0
                for h in range(2):
                    part = slice(h * HT, (h + 1) * HT)
                    at = layer_norm_constants(dve, chain, at, stats[:, part, :], moments[:, part, :],
                                              lambda i: X[:, h * HT + i, :], HT)
                    dve.tensor_scalar(rstd[:, part], moments[:, part, 1], LN_EPS, None,
                                      ALU.add).then_inc(variance, 1)
                    dve.wait_ge(std_done, h + 1)
                    dve.reciprocal(rstd[:, part], rstd[:, part]).then_inc(ln_ready, 1)
                    dve.wait_ge(ln_ready, 2 * h + 1)
                    dve.scalar_tensor_tensor(out=shift[:, part], in0=moments[:, part, 0], scalar=-1.0,
                                             in1=rstd[:, part], op0=ALU.mult,
                                             op1=ALU.mult).then_inc(ln_ready, 1)
                    dve.tensor_tensor(again[:, part], rstd[:, part], rstd[:, part],
                                      ALU.mult).then_inc(chain, 1)
                    dve.wait_ge(chain, at + 1)
                    dve.tensor_tensor(again[:, part], again[:, part], moments[:, part, 1],
                                      ALU.mult).then_inc(chain, 1)
                    dve.wait_ge(chain, at + 2)
                    dve.tensor_scalar(again[:, part], again[:, part], LN_EPS, None,
                                      ALU.add).then_inc(variance2, 1)
                    at = at + 2
                    if first_use and h == 0:
                        dve.wait_ge(small_turned, 2)
                        dve.tensor_copy(gate_T[:], psum[:, SMALL, 0:E]).then_inc(small_ready, 1)
                        dve.tensor_copy(b1_T[:], psum[:, SMALL, P:P + E * FB]).then_inc(small_ready, 1)
                dve.wait_ge(ln_ready, 4)
                for i in range(HT, TILES):
                    dve.tensor_scalar(f[:, i, :], X[:, i, :], rstd[:, i:i + 1], shift[:, i:i + 1],
                                      ALU.mult, ALU.add).then_inc(f_second, 1)
                dve.wait_ge(std2_done, 2)
                dve.reciprocal(again[:], again[:]).then_inc(chain, 1)
                dve.wait_ge(chain, at + 1)
                dve.tensor_tensor(rstd2[:], rstd[:], again[:], ALU.mult).then_inc(ln2_ready, 1)
                dve.tensor_tensor(shift2[:], shift[:], again[:], ALU.mult).then_inc(ln2_ready, 1)
                for g in range(NB):
                    round_score(g)
                dve.wait_ge(score_turned, TILES)
                dve.tensor_scalar(rows[:, :, DM:ROW],
                                  psum[:, SMALL, 0:TILES * E].rearrange("p (i e) -> p i e", e=E), 1.0, 0.5,
                                  ALU.add, ALU.mult).then_inc(weights_ready, 1)

                dve.wait_ge(steps_made, 1)
                dve.tensor_scalar(bounds[:], steps[:, 0:WAYS], -1.0, None, ALU.add).then_inc(moved, 1)
                dve.wait_ge(search_loaded, 16)
                def quarter(i):
                    dve.wait_ge(moved, i + 1)
                    for way in range(1, WAYS):
                        last = dve.tensor_scalar(hits[:, way - 1, :], search[:], bounds[:, way:way + 1],
                                                 None, ALU.is_ge, ALU.add,
                                                 accum_out=count[:, way - 1:way])
                    last.then_inc(counted, 1)
                    dve.tensor_scalar(following[:], steps[:, bass.ds(WAYS * i + WAYS, WAYS)],
                                      bounds[:, 0:1], None, ALU.add).then_inc(following_ready, 1)
                    dve.wait_ge(totalled, i + 1)
                    dve.tensor_scalar(passed[:], psum[:, COUNTS, 0:WAYS - 1], K - 0.5, None, ALU.is_ge,
                                      ALU.add, accum_out=passes[:]).then_inc(passes_ready, 1)
                    dve.wait_ge(passes_ready, i + 1)
                    dve.wait_ge(following_ready, i + 1)
                    dve.scalar_tensor_tensor(out=bounds[:], in0=passes[:].broadcast_to([P, WAYS]),
                                             scalar=steps[:, bass.ds(WAYS * i + 1, 1)],
                                             in1=following[:], op0=ALU.mult,
                                             op1=ALU.add).then_inc(moved, 1)

                quarter(0)
                with dve.Fori(0, (STEPS - 1) // 4) as m:
                    for n in range(4):
                        quarter(4 * m + n + 1)
                dve.wait_ge(moved, STEPS + 1)

                dve.tensor_scalar(above[:, 0, :], search[:], bounds[:, 0:1], None,
                                  ALU.is_gt).then_inc(link, 1)
                dve.tensor_scalar(above[:, 1, :], search[:], bounds[:, 0:1], None,
                                  ALU.is_equal).then_inc(link, 1)
                dve.wait_ge(cast, 3)
                for n in range(2):
                    dve.wait_ge(link, n + 1)
                    dve.tensor_tensor_scan(rank[:, n, :], ones[:], above[:, n, :], 0.0, ALU.mult,
                                           ALU.add).then_inc(link, 1)
                dve.wait_ge(link, 4)
                dve.tensor_copy(row_count[:], rank[:, :, SPAN - 1]).then_inc(rowed, 1)
                dve.wait_ge(offsets, 1)
                dve.tensor_scalar(offset[:], psum[:, COUNTS, 8:10], -1.0 - FAR, None,
                                  ALU.add).then_inc(link, 1)
                dve.wait_ge(link, 5)
                dve.tensor_tensor(offset[:, 1:2], offset[:, 1:2], psum[:, COUNTS, 16:17],
                                  ALU.add).then_inc(link, 1)
                dve.wait_ge(link, 6)
                for n in range(2):
                    dve.scalar_tensor_tensor(out=rank[:, n, :], in0=rank[:, n, :],
                                             scalar=offset[:, n:n + 1], in1=above[:, n, :],
                                             op0=ALU.add, op1=ALU.mult).then_inc(link, 1)
                dve.wait_ge(link, 8)
                dve.scalar_tensor_tensor(out=place[:], in0=rank[:, 0, :], scalar=FAR, in1=rank[:, 1, :],
                                         op0=ALU.add, op1=ALU.add).then_inc(placed, 1)
                dve.wait_ge(place_turned, 1)
                dve.tensor_copy(place_T[:], psum[:, PLACES, 0:PAIRS]).then_inc(link, 1)
                dve.wait_ge(link, 9)
                dve.tensor_scalar(high_i[:], place_T[:], LO.bit_length() - 1, None,
                                  ALU.logical_shift_right).then_inc(link, 1)
                dve.tensor_scalar(low_i[:], place_T[:], LO - 1, None, ALU.bitwise_and).then_inc(link, 1)
                dve.wait_ge(link, 10)
                dve.tensor_copy(high[:], high_i[:]).then_inc(split_ready, 1)
                dve.wait_ge(link, 11)
                dve.tensor_copy(low[:], low_i[:]).then_inc(split_ready, 1)
                dve.wait_ge(split_ready, 2)
                for h in range(HI):
                    dve.tensor_scalar(token_high[:, h, :], high[:], float(h), None,
                                      ALU.is_equal).then_inc(high_hot, 1)
                dve.wait_ge(high_hot, HI)
                dve.tensor_tensor(token_high[:], token_high[:],
                                  token[:].unsqueeze(1).broadcast_to([P, HI, PAIRS]), ALU.mult)
                for group in range(GROUPS):
                    for n in range(LO):
                        last = dve.tensor_scalar(pairs_of(one_low, group, n), pairs_of(low, group),
                                                 float(n), None, ALU.is_equal)
                    last.then_inc(one_hot, 1)
                for group in range(GROUPS):
                    dve.wait_ge(listed, group + 1)
                    experts = slice(group * E // GROUPS, (group + 1) * E // GROUPS)
                    lists = psum[0:LO, LISTS + group, 0:E // GROUPS * HI].rearrange(
                        "p (e h) -> p e h", h=HI)
                    for q in range(P // LO):
                        dve.tensor_scalar(tokens[q * LO:(q + 1) * LO, experts, :],
                                          lists[:, :, q:HI:P // LO], float(MIDDLE), None,
                                          ALU.add).then_inc(tokens_ready, 1)
                dve.wait_ge(tokens_ready, GROUPS * P // LO)

            @block.tensor
            def _(pe):
                def turn_weights(n):
                    e, layer = divmod(n, 2)
                    if n >= 2:
                        pe.wait_ge(w_taken, n - 1)
                    for q in range(FB):
                        raw = w2_raw[:, e, q * P:(q + 1) * P] if layer else w1_raw[:, e, q, :]
                        last = pe.transpose(psum[:, W_TURN + n % 2, q * P:(q + 1) * P], raw, ident[:])
                    last.then_inc(w_turned, 1)

                if first_use:
                    pe.wait_ge(loaded, 16 * 5)
                    pe.transpose(psum[:, SMALL, 0:E], gate_raw[:], ident[0:E, 0:E]
                                 ).then_inc(small_turned, 1)
                    pe.transpose(psum[:, SMALL, P:P + E * FB], b1_raw[:],
                                 ident[0:E * FB, 0:E * FB]).then_inc(small_turned, 1)
                for g in range(NB + 1):
                    if g < NB:
                        if g >= 4:
                            pe.wait_ge(fT_ready, g - 3)
                        for i in range(4):
                            tile = 4 * g + i
                            pe.wait_ge(f_first if tile < HT else f_second, tile % HT + 1)
                            last = pe.transpose(psum[:, g % 4, i * P:(i + 1) * P], f[:, 4 * g + i, :],
                                                ident[:])
                        last.then_inc(f_turned, 1)
                    if g:
                        if first_use and g == 1:
                            pe.wait_ge(small_ready, 2)
                        pe.wait_ge(fT_ready, g)
                        if g > SCORE_BANKS:
                            pe.wait_ge(tanh_done, g - SCORE_BANKS)
                        pe.matmul(psum[0:E, SCORES + (g - 1) % SCORE_BANKS, :], gate_T[:],
                                  f_T[:, (g - 1) * BANK:g * BANK], start=True, stop=True).then_inc(gated, 1)
                for i in range(TILES):
                    pe.wait_ge(score_ready, i // 4 + 1)
                    last = pe.transpose(psum[:, SMALL, i * E:(i + 1) * E], score[:, i * P:(i + 1) * P],
                                        ident[0:E, 0:E])
                    last.then_inc(score_turned, 1)
                pe.wait_ge(cast, 3)

                def total(i):
                    pe.wait_ge(counted, i + 1)
                    pe.matmul(psum[:, COUNTS, 0:WAYS - 1], same_b[:], count[:], start=True,
                              stop=True).then_inc(totalled, 1)

                if first_use:
                    pe.wait_ge(w_loaded, 32)
                    for n in range(2 * E - STEPS):
                        turn_weights(n)
                    for i in range(STEPS):
                        total(i)
                        turn_weights(2 * E - STEPS + i)
                else:
                    with pe.Fori(0, STEPS) as i:
                        total(i)
                pe.wait_ge(rowed, 1)
                pe.matmul(psum[:, COUNTS, 8:10], before_b[:], row_count[:], start=True, stop=True)
                pe.matmul(psum[:, COUNTS, 16:17], same_b[:], row_count[:, 0:1], start=True,
                          stop=True).then_inc(offsets, 1)
                pe.wait_ge(placed, 1)
                for h in range(HALVES):
                    last = pe.transpose(psum[:, PLACES, h * P:(h + 1) * P], place[:, h * P:(h + 1) * P],
                                        ident[:])
                last.then_inc(place_turned, 1)
                for group in range(GROUPS):
                    pe.wait_ge(one_hot, group + 1)
                    for n in range(E // GROUPS):
                        e = group * E // GROUPS + n
                        pairs = [h * P + e * J + j for h in range(HALVES) for j in range(J)]
                        for pair in pairs:
                            last = pe.matmul(psum[0:LO, LISTS + group, n * HI:(n + 1) * HI],
                                             one_low[:, :, pair], token_high[:, :, pair],
                                             start=(pair == pairs[0]), stop=(pair == pairs[-1]))
                    last.then_inc(listed, 1)

        with nc.cleanup_on_exit(), ExitStack() as ctx:
            def sb(what, shape, dt=F32):
                return ctx.enter_context(nc.sbuf_tensor(f"{name}_{what}", shape, dt))

            def sem(what):
                return nc.alloc_semaphore(f"{name}_{what}")

            psum = ctx.enter_context(nc.psum_tensor(f"{name}_psum3", [P, 8, BANK], F32))
            YT, HID, OUT = 0, 2, 6
            y_T = sb("y_T", [P, 2, K])
            hidden = sb("hidden", [P, 2, FB, K])
            o = sb("o", [P, AHEAD, KT, DM])
            y_turned = sem("y_turned")
            y_ready = sem("y_ready")
            hidden_summed = sem("hidden_summed")
            hidden_ready = sem("hidden_ready")
            o_summed = sem("o_summed")
            o_biased = sem("o_biased")
            o_ready = sem("o_ready")
            o_free = sem("o_free")
            scattered = [sem(f"scattered{r}") for r in range(2)]
            block = ctx.enter_context(nc.Block())
            TWO = E // 2

            @block.gpsimd
            def _(pool):
                for e in range(1, AHEAD - 1):
                    gather(pool, e)
                pool.sem_inc(o_free, AHEAD)
                for e in range(E):
                    if e + AHEAD - 1 < E:
                        gather(pool, e + AHEAD - 1)
                    pool.wait_ge(o_ready, e + 1)
                    if e:
                        pool.wait_ge(scattered[(e - 1) % 2], 16 * KT * ((e - 1) // 2 + 1))
                        pool.sem_inc(o_free, 1)
                    for t in range(KT):
                        pool.indirect_dma_start(dst,
                                                bass.IndirectOffsetOnAxis(ap=tokens[:, e, t:t + 1], axis=0),
                                                o[:, e % AHEAD, t, :], None, compute_op=ALU.add
                                                ).then_inc(scattered[e % 2], 16)
                pool.wait_ge(scattered[(E - 1) % 2], 16 * KT * TWO)
                pool.wait_ge(scattered[(E - 2) % 2], 16 * KT * TWO)

            @block.vector
            def _(dve):
                def scale_rows(e, r):
                    dve.wait_ge(y_turned, e + 1)
                    dve.tensor_scalar(y_T[:, r, :], psum[:, YT + r, :], gamma[:, 0:1], gamma[:, 1:2],
                                      ALU.mult, ALU.add).then_inc(y_ready, 1)

                scale_rows(0, 0)
                with dve.Fori(0, E // AHEAD) as m:
                    for n in range(AHEAD):
                        r = n % 2
                        scale_rows(AHEAD * m + n + 1, 1 - r)
                        dve.wait_ge(o_summed, AHEAD * m + n + 1)
                        dve.wait_ge(o_free, AHEAD * m + n + 1)
                        dve.wait_ge(gathered[n], 16 * KT * (m + 1))
                        dve.tensor_tensor(
                            o[:, n],
                            psum[:, OUT + r, :].rearrange("p (t d) -> p t d", d=DM),
                            b2_all[:, bass.ds(AHEAD * m + n, 1), :].broadcast_to([P, KT, DM]),
                            ALU.add).then_inc(o_biased, 1)
                        dve.wait_ge(o_biased, AHEAD * m + n + 1)
                        for t in range(KT):
                            last = dve.tensor_scalar(o[:, n, t, :], o[:, n, t, :],
                                                     got[:, n, t, bass.ds(DM + AHEAD * m + n, 1)], None,
                                                     ALU.mult)
                        last.then_inc(o_ready, 1)

            @block.scalar
            def _(act):
                act.preload_act_table(ACT.Gelu_apprx_tanh)
                with act.Fori(0, TWO) as m:
                    for r in range(2):
                        for q in range(FB):
                            act.wait_ge(hidden_summed, FB * (2 * m + r) + q + 1)
                            act.activation(hidden[:, r, q, :], psum[:, HID + q, :],
                                           ACT.Gelu_apprx_tanh,
                                           bias=b1_T[:, bass.ds(FB * (2 * m + r) + q, 1)]
                                           ).then_inc(hidden_ready, 1)

            @block.tensor
            def _(pe):
                def turn_rows(e):
                    if e < E:
                        pe.wait_ge(gathered[e % AHEAD], 16 * KT * (e // AHEAD + 1))
                    if e >= 2:
                        pe.wait_ge(y_ready, e - 1)
                    slot = min(e, E - 1) % AHEAD
                    for t in range(KT):
                        last = pe.transpose(psum[:, YT + e % 2, t * P:(t + 1) * P],
                                            got[:, slot, t, 0:DM], ident[:])
                    last.then_inc(y_turned, 1)

                def second_layer(e):
                    r = e % 2
                    if e >= 2:
                        pe.wait_ge(o_biased, e - 1)
                    pe.wait_ge(hidden_ready, FB * (e + 1))
                    for t in range(KT):
                        for q in range(FB):
                            last = pe.matmul(psum[:, OUT + r, t * DM:(t + 1) * DM],
                                             hidden[:, r, q, t * P:(t + 1) * P], w2_T[:, e, q, :],
                                             start=(q == 0), stop=(q == FB - 1))
                    last.then_inc(o_summed, 1)

                turn_rows(0)
                for e in range(E):
                    r = e % 2
                    pe.wait_ge(y_ready, e + 1)
                    for q in range(FB):
                        if e:
                            pe.wait_ge(hidden_ready, FB * (e - 1) + q + 1)
                        pe.matmul(psum[:, HID + q, :], w1_T[:, e, q * P:(q + 1) * P], y_T[:, r, :],
                                  start=True, stop=True).then_inc(hidden_summed, 1)
                    if e:
                        turn_rows(e + 1)
                    second_layer(e)
                    if e == 0:
                        turn_rows(1)


def attention(nc, X, ident, source, wq, wk, wv, wo):
    HD, DM = wq.shape
    BATCH = 2
    TILES = X.shape[1]
    TB = TILES // BATCH
    T = TILES * P
    NB = T // BANK
    SCALE = (3.0 / HD) ** 0.5
    with nc.cleanup_on_exit(), ExitStack() as ctx:
        def sb(what, shape, dt=F32):
            return ctx.enter_context(nc.sbuf_tensor(f"a_{what}", shape, dt))

        def sem(what):
            return nc.alloc_semaphore(f"a_{what}")

        psum = ctx.enter_context(nc.psum_tensor("a_psum", [P, 8, BANK], F32))
        stats = sb("stats", [P, TILES, 6])
        moments = sb("moments", [P, TILES, 2])
        rstd = sb("rstd", [P, TILES])
        shift = sb("shift", [P, TILES])
        f = sb("f", [P, TILES, DM])
        f_T = sb("f_T", [P, T])
        q_w = sb("q_w", [HD, DM])
        kv_w = sb("kv_w", [HD, 2, DM])
        o_w = sb("o_w", [DM, HD])
        kv_T = sb("kv_T", [P, 2, HD])
        o_T = sb("o_T", [HD, DM])
        gram = sb("gram", [P, BATCH, DM])
        gv = sb("gv", [P, BATCH, HD])
        energy_T = sb("energy_T", [HD, BATCH, HD])
        eo = sb("eo", [HD, BATCH, DM])
        mix = sb("mix", [P, BATCH, DM])

        x_loaded = [sem(f"x_loaded{n}") for n in range(4)]
        loaded = sem("loaded")
        chain = sem("chain")
        variance = sem("variance")
        std_done = sem("std_done")
        ln_ready = sem("ln_ready")
        f_first = sem("f_first")
        f_second = sem("f_second")
        turned = sem("turned")
        fT_ready = sem("fT_ready")
        small_turned = sem("small_turned")
        small_ready = sem("small_ready")
        gram_summed = sem("gram_summed")
        link = sem("link")
        linked = sem("linked")
        out_ready = sem("out_ready")
        added = sem("added")
        block = ctx.enter_context(nc.Block())
        QT = TILES // 4

        @block.sync
        def _(sp):
            for n in range(4):
                sp.dma_start(X[:, n * QT:(n + 1) * QT, :],
                             source[n * QT * P:(n + 1) * QT * P, :].rearrange("(i p) d -> p i d", p=P)
                             ).then_inc(x_loaded[n], 16)
            for out, what in ((q_w[:], wq), (kv_w[:, 0, :], wk), (kv_w[:, 1, :], wv), (o_w[:], wo)):
                sp.dma_start(out, what).then_inc(loaded, 16)

        @block.vector
        def _(dve):
            def link_copy(b, n):
                where = (gv[:, b, :], energy_T[:, b, :], eo[:, b, :], mix[:, b, :])[n]
                rows, width = where.shape
                dve.wait_ge(link, 4 * b + n + 1)
                if n == 2:
                    dve.tensor_scalar(where, psum[0:rows, 6, 0:width], SCALE, None,
                                      ALU.mult).then_inc(linked, 1)
                else:
                    dve.tensor_copy(where, psum[0:rows, 6, 0:width]).then_inc(linked, 1)

            def take_gram(b):
                dve.wait_ge(gram_summed, b + 1)
                dve.tensor_copy(gram[:, b, :], psum[:, 4 + b, 0:DM]).then_inc(linked, 1)

            def add(g):
                dve.wait_ge(out_ready, g + 1)
                rows = X[:, 4 * g:4 * g + 4, :].rearrange("p i d -> p (i d)")
                dve.tensor_tensor(rows, rows, psum[:, g % 4, :], ALU.add).then_inc(added, 1)

            at = 0
            for h in range(2):
                part = slice(h * TB, (h + 1) * TB)
                for n in range(2 * h, 2 * h + 2):
                    dve.wait_ge(x_loaded[n], 16)
                at = layer_norm_constants(dve, chain, at, stats[:, part, :], moments[:, part, :],
                                          lambda i: X[:, h * TB + i, :], TB)
                dve.tensor_scalar(rstd[:, part], moments[:, part, 1], LN_EPS, None,
                                  ALU.add).then_inc(variance, 1)
                dve.wait_ge(std_done, h + 1)
                dve.reciprocal(rstd[:, part], rstd[:, part]).then_inc(ln_ready, 1)
                dve.wait_ge(ln_ready, 2 * h + 1)
                dve.scalar_tensor_tensor(out=shift[:, part], in0=moments[:, part, 0], scalar=-1.0,
                                         in1=rstd[:, part], op0=ALU.mult,
                                         op1=ALU.mult).then_inc(ln_ready, 1)
            dve.wait_ge(ln_ready, 4)
            for i in range(TB, TILES):
                dve.tensor_scalar(f[:, i, :], X[:, i, :], rstd[:, i:i + 1], shift[:, i:i + 1],
                                  ALU.mult, ALU.add).then_inc(f_second, 1)
            dve.wait_ge(small_turned, 3)
            dve.tensor_copy(kv_T[:], psum[:, 7, 0:2 * HD].rearrange("p (a h) -> p a h", a=2)
                            ).then_inc(small_ready, 1)
            dve.tensor_copy(o_T[:], psum[0:HD, 7, 2 * HD:2 * HD + DM]).then_inc(small_ready, 1)
            take_gram(0)
            link_copy(0, 0)
            link_copy(0, 1)
            link_copy(0, 2)
            link_copy(0, 3)
            take_gram(1)
            for n in range(4):
                link_copy(1, n)
                add(n)
            for g in range(4, NB):
                add(g)

        @block.scalar
        def _(act):
            def root(h):
                part = slice(h * TB, (h + 1) * TB)
                act.wait_ge(variance, h + 1)
                act.activation(rstd[:, part], rstd[:, part], ACT.Sqrt).then_inc(std_done, 1)

            def normalise(first, end):
                for i in range(first, end):
                    act.activation(f[:, i, :], X[:, i, :], ACT.Identity, bias=shift[:, i:i + 1],
                                   scale=rstd[:, i:i + 1]).then_inc(f_first, 1)

            def take_turned(g):
                act.wait_ge(turned, g + 1)
                act.copy(f_T[:, g * BANK:(g + 1) * BANK], psum[:, g % 4, :]).then_inc(fT_ready, 1)

            root(0)
            act.wait_ge(ln_ready, 2)
            normalise(0, TB // 2)
            root(1)
            take_turned(0)
            normalise(TB // 2, 3 * TB // 4)
            take_turned(1)
            normalise(3 * TB // 4, TB)
            for g in range(2, NB):
                take_turned(g)

        @block.tensor
        def _(pe):
            pe.wait_ge(loaded, 16 * 4)
            for n in range(2):
                pe.transpose(psum[:, 7, n * HD:(n + 1) * HD], kv_w[:, n, :],
                             ident[0:HD, 0:HD]).then_inc(small_turned, 1)
            pe.transpose(psum[0:HD, 7, 2 * HD:2 * HD + DM], o_w[:], ident[:]).then_inc(small_turned, 1)
            def chain_link(b, n):
                out, left, right = (
                    (psum[:, 6, 0:HD], gram[:, b, :], kv_T[:, 1, :]),
                    (psum[0:HD, 6, 0:HD], gv[:, b, :], kv_T[:, 0, :]),
                    (psum[0:HD, 6, 0:DM], energy_T[:, b, :], o_T[:]),
                    (psum[:, 6, 0:DM], q_w[:], eo[:, b, :]),
                )[n]
                pe.wait_ge(linked, 5 * b + n + 1)
                pe.matmul(out, left, right, start=True, stop=True).then_inc(link, 1)

            def output(g):
                pe.wait_ge(fT_ready, g + 1)
                if g >= 4:
                    pe.wait_ge(added, g - 3)
                else:
                    pe.wait_ge(fT_ready, NB // 2 + g + 1)
                for i in range(4):
                    tile = 4 * g + i
                    last = pe.matmul(psum[:, g % 4, i * P:(i + 1) * P], f_T[:, tile * P:(tile + 1) * P],
                                     mix[:, tile // TB, :], start=True, stop=True)
                last.then_inc(out_ready, 1)

            for g in range(NB):
                if g >= 4:
                    pe.wait_ge(fT_ready, g - 3)
                for i in range(4):
                    tile = 4 * g + i
                    pe.wait_ge(f_first if tile < TB else f_second, tile % TB + 1)
                    last = pe.transpose(psum[:, g % 4, i * P:(i + 1) * P], f[:, tile, :], ident[:])
                    b, first = divmod(tile, TB)
                    gram_last = pe.matmul(psum[:, 4 + b, 0:DM], f[:, tile, :], f[:, tile, :],
                                          start=(first == 0), stop=(first == TB - 1))
                    if first == TB - 1:
                        gram_last.then_inc(gram_summed, 1)
                last.then_inc(turned, 1)
                if g == 4:
                    pe.wait_ge(small_ready, 2)
                if g >= 5:
                    chain_link(0, g - 5)
            chain_link(0, 3)
            pe.wait_ge(linked, 5)
            for n in range(4):
                chain_link(1, n)
                output(n)
            pe.wait_ge(linked, 10)
            for g in range(4, NB):
                output(g)


def build(nc, inputs, out):
    mixer = {k[len("L0_attn_a_"):]: v for k, v in inputs.items() if k.startswith("L0_attn_a_")}
    linear = {k[len("L0_attn_b_"):]: v for k, v in inputs.items() if k.startswith("L0_attn_b_")}
    experts = {k[len("L0_ffn_"):]: v for k, v in inputs.items() if k.startswith("L0_ffn_")}
    BATCH, L, DM = mixer["x"].shape
    T = BATCH * L
    between = nc.dram_tensor("between", [T, DM], F32, kind="Internal").ap()
    with ExitStack() as ctx:
        X = ctx.enter_context(nc.sbuf_tensor("X", [P, T // P, DM], F32))
        ident = ctx.enter_context(nc.sbuf_tensor("ident", [P, P], F32))
        identity(nc, ident)
        mamba(nc, X, ident, **mixer)
        E, FF, _ = experts["fc1s"].shape
        shared = {name: ctx.enter_context(nc.sbuf_tensor(f"shared_{name}", shape, F32))
                  for name, shape in (("gamma", [P, 2]), ("b1_T", [P, E * FF // P]),
                                      ("b2_all", [P, E, DM]), ("gate_T", [P, E]),
                                      ("w1_T", [P, E, FF]), ("w2_T", [P, E, FF // P, DM]))}
        moe(nc, X, ident, shared, "f1", between, True, **experts)
        attention(nc, X, ident, between, **linear)
        moe(nc, X, ident, shared, "f2", out.rearrange("b l d -> (b l) d"), False, **experts)


_INS = ["L0_attn_a_x", "L0_attn_a_W_in", "L0_attn_a_conv_w", "L0_attn_a_conv_b", "L0_attn_a_A_log",
        "L0_attn_a_D", "L0_attn_a_W_x", "L0_attn_a_W_dt", "L0_attn_a_b_dt", "L0_attn_a_W_out",
        "L0_attn_b_wq", "L0_attn_b_wk", "L0_attn_b_wv", "L0_attn_b_wo",
        "L0_ffn_gate_w", "L0_ffn_ln_gamma", "L0_ffn_ln_beta", "L0_ffn_fc1s", "L0_ffn_b1s",
        "L0_ffn_fc2s", "L0_ffn_b2s"]


def kernel(**inputs):
    import numpy as _np
    import concourse.bacc as _bacc
    from concourse.bass_utils import run_bass_kernel_spmd as _run

    nc = _bacc.Bacc("TRN2", target_bir_lowering=False, num_devices=1)
    arrays, args = {}, {}
    for name in _INS:
        a = _np.ascontiguousarray(inputs[name])
        arrays[f"in_{name}"] = a
        args[name] = nc.dram_tensor(f"in_{name}", a.shape, mybir.dt.from_np(a.dtype),
                                    kind="ExternalInput").ap()
    out = nc.dram_tensor("out_0", arrays["in_L0_attn_a_x"].shape, F32, kind="ExternalOutput").ap()
    build(nc, args, out)
    r = _run(nc, [arrays], core_ids=[0])
    return r.results[0]["out_0"]
```
